# Optimizing a Trainium2 kernel written in Bass

```python
import numpy as np
import jax
import jax.numpy as jnp

def _softmax(x, axis=-1):
    return jax.nn.softmax(x, axis=axis)

def _gelu(x):
    return jax.nn.gelu(x, approximate=True)

def _silu(x):
    return jax.nn.silu(x)

def _sigmoid(x):
    return jax.nn.sigmoid(x)

def _layernorm(x, axis=-1, eps=1e-05):
    m = jnp.mean(x, axis=axis, keepdims=True)
    v = jnp.var(x, axis=axis, keepdims=True)
    return (x - m) / jnp.sqrt(v + eps)

def _scatter_add(tgt, idx, src, axis=0):
    return tgt.at[idx].add(src)

def _segment_sum(src, seg, n):
    return jax.ops.segment_sum(src, seg, n)
kernel_name = 'mk_recurrent_d2_jaxref_r8_aad53b'

def setup_inputs(seed: int=0):
    np.random.seed(seed)
    _w = jnp.asarray

    def _L0_attn_setup():
        import jax, jax.numpy as jnp
        import numpy as np
        N_HEADS, N_KV, HEAD_DIM = (16, 4, 64)
        DIM = 512
        LATENT = N_HEADS * HEAD_DIM
        KV_DIM = N_KV * HEAD_DIM
        KSZ = 3

        def _causal_conv1d(x, w, b, groups):
            y = jax.lax.conv_general_dilated(x.transpose(0, 2, 1), w, window_strides=(1,), padding=[(w.shape[-1] - 1, 0)], feature_group_count=groups, dimension_numbers=('NCH', 'OIH', 'NCH'))
            return (y + b[None, :, None]).transpose(0, 2, 1)

        def _rope(x, cos, sin):
            x1, x2 = (x[..., ::2], x[..., 1::2])
            out = jnp.stack([x1 * cos - x2 * sin, x1 * sin + x2 * cos], axis=-1)
            return out.reshape(x.shape)

        def _l2norm(x):
            n = jnp.sqrt(jnp.sum(x * x, axis=-1, keepdims=True))
            return x / jnp.maximum(n, 1e-12)

        def _forward(x, w_qkv, w_o, qc1_w, qc1_b, qc2_w, qc2_b, kc1_w, kc1_b, kc2_w, kc2_b, key_temp):
            B, S, _ = x.shape
            qkv = x @ w_qkv.T
            q = qkv[..., :LATENT]
            k = qkv[..., LATENT:LATENT + KV_DIM]
            half = KV_DIM // 2
            v_curr = qkv[..., LATENT + KV_DIM:LATENT + KV_DIM + half]
            v_prev = qkv[..., LATENT + KV_DIM + half:]
            v = jnp.concatenate([v_curr, jnp.pad(v_prev[:, :-1, :], ((0, 0), (1, 0), (0, 0)))], axis=-1)
            q_pre, k_pre = (q, k)
            q = _causal_conv1d(_causal_conv1d(q, qc1_w, qc1_b, N_HEADS), qc2_w, qc2_b, 1)
            k = _causal_conv1d(_causal_conv1d(k, kc1_w, kc1_b, N_KV), kc2_w, kc2_b, 1)
            q_mean = q_pre.reshape(B, S, N_HEADS, HEAD_DIM).mean(axis=2)
            k_mean = k_pre.reshape(B, S, N_KV, HEAD_DIM).mean(axis=2)
            q = q.reshape(B, S, N_HEADS, HEAD_DIM) + 0.5 * k_mean[:, :, None, :]
            k = k.reshape(B, S, N_KV, HEAD_DIM) + 0.5 * q_mean[:, :, None, :]
            q = q.transpose(0, 2, 1, 3)
            k = k.transpose(0, 2, 1, 3)
            v = v.reshape(B, S, N_KV, HEAD_DIM).transpose(0, 2, 1, 3)
            q = _l2norm(q)
            k = _l2norm(k) * key_temp
            inv = 1.0 / 10000.0 ** (jnp.arange(0, HEAD_DIM, 2, dtype=jnp.float32) / HEAD_DIM)
            ang = jnp.arange(S, dtype=jnp.float32)[:, None] * inv[None, :]
            cos, sin = (jnp.cos(ang)[None, None], jnp.sin(ang)[None, None])
            q = _rope(q, cos, sin)
            k = _rope(k, cos, sin)
            kg = jnp.repeat(k, N_HEADS // N_KV, axis=1)
            vg = jnp.repeat(v, N_HEADS // N_KV, axis=1)
            scale = HEAD_DIM ** (-0.5)
            scores = jnp.einsum('bhqd,bhkd->bhqk', q, kg) * scale
            causal = jnp.tril(jnp.ones((S, S), dtype=bool))
            scores = jnp.where(causal[None, None], scores, jnp.finfo(scores.dtype).min)
            attn = jax.nn.softmax(scores, axis=-1)
            out = jnp.einsum('bhqk,bhkd->bhqd', attn, vg)
            out = out.transpose(0, 2, 1, 3).reshape(B, S, LATENT)
            return out @ w_o.T
        key = jax.random.key(seed)
        ks = jax.random.split(key, 12)
        sc = 0.02
        x = jax.random.normal(ks[0], (2, 256, DIM), jnp.float32)
        w_qkv = jax.random.normal(ks[1], (LATENT + 2 * KV_DIM, DIM), jnp.float32) * sc
        w_o = jax.random.normal(ks[2], (DIM, LATENT), jnp.float32) * sc
        qc1_w = jax.random.normal(ks[3], (LATENT, LATENT // N_HEADS, KSZ), jnp.float32) * sc
        qc1_b = jnp.zeros((LATENT,), jnp.float32)
        qc2_w = jax.random.normal(ks[4], (LATENT, LATENT, KSZ), jnp.float32) * sc
        qc2_b = jnp.zeros((LATENT,), jnp.float32)
        kc1_w = jax.random.normal(ks[5], (KV_DIM, KV_DIM // N_KV, KSZ), jnp.float32) * sc
        kc1_b = jnp.zeros((KV_DIM,), jnp.float32)
        kc2_w = jax.random.normal(ks[6], (KV_DIM, KV_DIM, KSZ), jnp.float32) * sc
        kc2_b = jnp.zeros((KV_DIM,), jnp.float32)
        key_temp = jnp.full((1,), float(HEAD_DIM) ** 0.5, jnp.float32)
        return dict(x=x, w_qkv=w_qkv, w_o=w_o, qc1_w=qc1_w, qc1_b=qc1_b, qc2_w=qc2_w, qc2_b=qc2_b, kc1_w=kc1_w, kc1_b=kc1_b, kc2_w=kc2_w, kc2_b=kc2_b, key_temp=key_temp)
    _L0_attn_in = _L0_attn_setup()

    def _L0_ffn_setup():
        import jax, jax.numpy as jnp
        import numpy as np
        HID, INT, LAT, NE, K = (512, 1024, 256, 8, 2)
        LN_EPS = 1e-05

        def _layernorm(x, gamma, beta):
            mu = jnp.mean(x, axis=-1, keepdims=True)
            var = jnp.var(x, axis=-1, keepdims=True)
            return (x - mu) * jax.lax.rsqrt(var + LN_EPS) * gamma + beta
        key = jax.random.key(seed)
        ks = jax.random.split(key, 8)
        s = lambda d: 1.0 / np.sqrt(d)
        return {'hidden_states': jax.random.normal(ks[0], (4, 256, HID), jnp.float32), 'gate_w': jax.random.normal(ks[1], (HID, NE), jnp.float32) * s(HID), 'up_w': jax.random.normal(ks[2], (HID, INT), jnp.float32) * s(HID), 'down_w': jax.random.normal(ks[3], (INT, HID), jnp.float32) * s(INT), 'fc1_w': jax.random.normal(ks[4], (HID, LAT), jnp.float32) * s(HID), 'fc2_w': jax.random.normal(ks[5], (LAT, HID), jnp.float32) * s(LAT), 'expert_w': jax.random.normal(ks[6], (LAT, LAT), jnp.float32), 'ln_gamma': jnp.ones((HID,), jnp.float32), 'ln_beta': jnp.zeros((HID,), jnp.float32)}
    _L0_ffn_in = _L0_ffn_setup()

    def _L1_attn_setup():
        import jax, jax.numpy as jnp
        import numpy as np
        import math
        HIDDEN = 512
        N_HEADS = 32
        N_KV_HEADS = 8
        HEAD_DIM = HIDDEN // N_HEADS
        GROUPS = N_HEADS // N_KV_HEADS
        ROPE_THETA = 10000.0
        TOKEN_BUDGET = 128
        INIT_BUDGET = 128
        RECENT_BUDGET = 128
        CHUNK = 16
        B, S = (1, 256)

        def _rotate_half(x):
            x1, x2 = jnp.split(x, 2, axis=-1)
            return jnp.concatenate([-x2, x1], axis=-1)

        def _rope(seq_len, dtype):
            inv_freq = 1.0 / ROPE_THETA ** (jnp.arange(0, HEAD_DIM, 2, dtype=jnp.float32) / HEAD_DIM)
            freqs = jnp.arange(seq_len, dtype=jnp.float32)[:, None] * inv_freq[None, :]
            emb = jnp.concatenate([freqs, freqs], axis=-1)
            return (jnp.cos(emb).astype(dtype), jnp.sin(emb).astype(dtype))
        key = jax.random.key(seed)
        ks = jax.random.split(key, 5)
        sc = 0.02
        return {'hidden_states': jax.random.normal(ks[0], (B, S, HIDDEN), dtype=jnp.float32), 'wq': jax.random.normal(ks[1], (N_HEADS * HEAD_DIM, HIDDEN), dtype=jnp.float32) * sc, 'wk': jax.random.normal(ks[2], (N_KV_HEADS * HEAD_DIM, HIDDEN), dtype=jnp.float32) * sc, 'wv': jax.random.normal(ks[3], (N_KV_HEADS * HEAD_DIM, HIDDEN), dtype=jnp.float32) * sc, 'wo': jax.random.normal(ks[4], (HIDDEN, N_HEADS * HEAD_DIM), dtype=jnp.float32) * sc}
    _L1_attn_in = _L1_attn_setup()

    def _L1_ffn_setup():
        import jax, jax.numpy as jnp
        import numpy as np
        ALPHA = 32
        R = 16
        SCALING = ALPHA / R
        key = jax.random.key(seed)
        k1, k2, k3, k4 = jax.random.split(key, 4)
        B_, S, D = (4, 256, 512)
        H, r, O = (8, R, 512)
        x = jax.random.normal(k1, (B_, S, D), dtype=jnp.float32)
        A = jax.random.normal(k2, (H, r, D), dtype=jnp.float32) * 0.02
        Bm = jax.random.normal(k3, (H, O, r), dtype=jnp.float32) * 0.02
        Wr = jax.random.normal(k4, (H, D), dtype=jnp.float32) * 0.02
        br = jnp.zeros((H,), dtype=jnp.float32)
        return {'x': x, 'A': A, 'B': Bm, 'Wr': Wr, 'br': br}
    _L1_ffn_in = _L1_ffn_setup()
    _d = {'L0_attn_x': _L0_attn_in['x'], 'L0_attn_w_qkv': _L0_attn_in['w_qkv'], 'L0_attn_w_o': _L0_attn_in['w_o'], 'L0_attn_qc1_w': _L0_attn_in['qc1_w'], 'L0_attn_qc1_b': _L0_attn_in['qc1_b'], 'L0_attn_qc2_w': _L0_attn_in['qc2_w'], 'L0_attn_qc2_b': _L0_attn_in['qc2_b'], 'L0_attn_kc1_w': _L0_attn_in['kc1_w'], 'L0_attn_kc1_b': _L0_attn_in['kc1_b'], 'L0_attn_kc2_w': _L0_attn_in['kc2_w'], 'L0_attn_kc2_b': _L0_attn_in['kc2_b'], 'L0_attn_key_temp': _L0_attn_in['key_temp'], 'L0_ffn_gate_w': _L0_ffn_in['gate_w'], 'L0_ffn_up_w': _L0_ffn_in['up_w'], 'L0_ffn_down_w': _L0_ffn_in['down_w'], 'L0_ffn_fc1_w': _L0_ffn_in['fc1_w'], 'L0_ffn_fc2_w': _L0_ffn_in['fc2_w'], 'L0_ffn_expert_w': _L0_ffn_in['expert_w'], 'L0_ffn_ln_gamma': _L0_ffn_in['ln_gamma'], 'L0_ffn_ln_beta': _L0_ffn_in['ln_beta'], 'L1_attn_wq': _L1_attn_in['wq'], 'L1_attn_wk': _L1_attn_in['wk'], 'L1_attn_wv': _L1_attn_in['wv'], 'L1_attn_wo': _L1_attn_in['wo'], 'L1_ffn_A': _L1_ffn_in['A'], 'L1_ffn_B': _L1_ffn_in['B'], 'L1_ffn_Wr': _L1_ffn_in['Wr'], 'L1_ffn_br': _L1_ffn_in['br']}
    _x0 = _d['L0_attn_x']
    _d['L0_attn_x'] = jax.random.normal(jax.random.fold_in(jax.random.key(seed), 1), (2, 1024, 512), dtype=_x0.dtype)
    del _x0
    return _d

def reference(L0_attn_x, L0_attn_w_qkv, L0_attn_w_o, L0_attn_qc1_w, L0_attn_qc1_b, L0_attn_qc2_w, L0_attn_qc2_b, L0_attn_kc1_w, L0_attn_kc1_b, L0_attn_kc2_w, L0_attn_kc2_b, L0_attn_key_temp, L0_ffn_gate_w, L0_ffn_up_w, L0_ffn_down_w, L0_ffn_fc1_w, L0_ffn_fc2_w, L0_ffn_expert_w, L0_ffn_ln_gamma, L0_ffn_ln_beta, L1_attn_wq, L1_attn_wk, L1_attn_wv, L1_attn_wo, L1_ffn_A, L1_ffn_B, L1_ffn_Wr, L1_ffn_br):

    def _L0_attn_ref(x, w_qkv, w_o, qc1_w, qc1_b, qc2_w, qc2_b, kc1_w, kc1_b, kc2_w, kc2_b, key_temp):
        import jax, jax.numpy as jnp
        import numpy as np
        N_HEADS, N_KV, HEAD_DIM = (16, 4, 64)
        DIM = 512
        LATENT = N_HEADS * HEAD_DIM
        KV_DIM = N_KV * HEAD_DIM
        KSZ = 3

        def _causal_conv1d(x, w, b, groups):
            y = jax.lax.conv_general_dilated(x.transpose(0, 2, 1), w, window_strides=(1,), padding=[(w.shape[-1] - 1, 0)], feature_group_count=groups, dimension_numbers=('NCH', 'OIH', 'NCH'))
            return (y + b[None, :, None]).transpose(0, 2, 1)

        def _rope(x, cos, sin):
            x1, x2 = (x[..., ::2], x[..., 1::2])
            out = jnp.stack([x1 * cos - x2 * sin, x1 * sin + x2 * cos], axis=-1)
            return out.reshape(x.shape)

        def _l2norm(x):
            n = jnp.sqrt(jnp.sum(x * x, axis=-1, keepdims=True))
            return x / jnp.maximum(n, 1e-12)

        def _forward(x, w_qkv, w_o, qc1_w, qc1_b, qc2_w, qc2_b, kc1_w, kc1_b, kc2_w, kc2_b, key_temp):
            B, S, _ = x.shape
            qkv = x @ w_qkv.T
            q = qkv[..., :LATENT]
            k = qkv[..., LATENT:LATENT + KV_DIM]
            half = KV_DIM // 2
            v_curr = qkv[..., LATENT + KV_DIM:LATENT + KV_DIM + half]
            v_prev = qkv[..., LATENT + KV_DIM + half:]
            v = jnp.concatenate([v_curr, jnp.pad(v_prev[:, :-1, :], ((0, 0), (1, 0), (0, 0)))], axis=-1)
            q_pre, k_pre = (q, k)
            q = _causal_conv1d(_causal_conv1d(q, qc1_w, qc1_b, N_HEADS), qc2_w, qc2_b, 1)
            k = _causal_conv1d(_causal_conv1d(k, kc1_w, kc1_b, N_KV), kc2_w, kc2_b, 1)
            q_mean = q_pre.reshape(B, S, N_HEADS, HEAD_DIM).mean(axis=2)
            k_mean = k_pre.reshape(B, S, N_KV, HEAD_DIM).mean(axis=2)
            q = q.reshape(B, S, N_HEADS, HEAD_DIM) + 0.5 * k_mean[:, :, None, :]
            k = k.reshape(B, S, N_KV, HEAD_DIM) + 0.5 * q_mean[:, :, None, :]
            q = q.transpose(0, 2, 1, 3)
            k = k.transpose(0, 2, 1, 3)
            v = v.reshape(B, S, N_KV, HEAD_DIM).transpose(0, 2, 1, 3)
            q = _l2norm(q)
            k = _l2norm(k) * key_temp
            inv = 1.0 / 10000.0 ** (jnp.arange(0, HEAD_DIM, 2, dtype=jnp.float32) / HEAD_DIM)
            ang = jnp.arange(S, dtype=jnp.float32)[:, None] * inv[None, :]
            cos, sin = (jnp.cos(ang)[None, None], jnp.sin(ang)[None, None])
            q = _rope(q, cos, sin)
            k = _rope(k, cos, sin)
            kg = jnp.repeat(k, N_HEADS // N_KV, axis=1)
            vg = jnp.repeat(v, N_HEADS // N_KV, axis=1)
            scale = HEAD_DIM ** (-0.5)
            scores = jnp.einsum('bhqd,bhkd->bhqk', q, kg) * scale
            causal = jnp.tril(jnp.ones((S, S), dtype=bool))
            scores = jnp.where(causal[None, None], scores, jnp.finfo(scores.dtype).min)
            attn = jax.nn.softmax(scores, axis=-1)
            out = jnp.einsum('bhqk,bhkd->bhqd', attn, vg)
            out = out.transpose(0, 2, 1, 3).reshape(B, S, LATENT)
            return out @ w_o.T
        return _forward(x, w_qkv, w_o, qc1_w, qc1_b, qc2_w, qc2_b, kc1_w, kc1_b, kc2_w, kc2_b, key_temp)

    def _L0_ffn_ref(hidden_states, gate_w, up_w, down_w, fc1_w, fc2_w, expert_w, ln_gamma, ln_beta):
        import jax, jax.numpy as jnp
        import numpy as np
        HID, INT, LAT, NE, K = (512, 1024, 256, 8, 2)
        LN_EPS = 1e-05

        def _layernorm(x, gamma, beta):
            mu = jnp.mean(x, axis=-1, keepdims=True)
            var = jnp.var(x, axis=-1, keepdims=True)
            return (x - mu) * jax.lax.rsqrt(var + LN_EPS) * gamma + beta
        logits = jnp.einsum('bsh,he->bse', hidden_states, gate_w)
        routing_weights, selected_experts = jax.lax.top_k(logits, K)
        h = jax.nn.relu(jnp.einsum('bsh,hi->bsi', hidden_states, up_w)) ** 2
        shared_out = jnp.einsum('bsi,ih->bsh', h, down_w)
        x_latent = jnp.einsum('bsh,hl->bsl', hidden_states, fc1_w)
        expert_out = jnp.einsum('bsl,lm->bsm', x_latent, expert_w)
        moe_out = expert_out * jnp.sum(routing_weights, axis=-1, keepdims=True)
        routed_out = jnp.einsum('bsl,lh->bsh', moe_out, fc2_w)
        return _layernorm(shared_out + routed_out, ln_gamma, ln_beta)

    def _L1_attn_ref(hidden_states, wq, wk, wv, wo):
        import jax, jax.numpy as jnp
        import numpy as np
        import math
        HIDDEN = 512
        N_HEADS = 32
        N_KV_HEADS = 8
        HEAD_DIM = HIDDEN // N_HEADS
        GROUPS = N_HEADS // N_KV_HEADS
        ROPE_THETA = 10000.0
        TOKEN_BUDGET = 128
        INIT_BUDGET = 128
        RECENT_BUDGET = 128
        CHUNK = 16
        B, S = (1, 256)

        def _rotate_half(x):
            x1, x2 = jnp.split(x, 2, axis=-1)
            return jnp.concatenate([-x2, x1], axis=-1)

        def _rope(seq_len, dtype):
            inv_freq = 1.0 / ROPE_THETA ** (jnp.arange(0, HEAD_DIM, 2, dtype=jnp.float32) / HEAD_DIM)
            freqs = jnp.arange(seq_len, dtype=jnp.float32)[:, None] * inv_freq[None, :]
            emb = jnp.concatenate([freqs, freqs], axis=-1)
            return (jnp.cos(emb).astype(dtype), jnp.sin(emb).astype(dtype))
        b, s, _ = hidden_states.shape
        dtype = hidden_states.dtype
        NEG = jnp.finfo(dtype).min
        q = (hidden_states @ wq.T).reshape(b, s, N_HEADS, HEAD_DIM).transpose(0, 2, 1, 3)
        k = (hidden_states @ wk.T).reshape(b, s, N_KV_HEADS, HEAD_DIM).transpose(0, 2, 1, 3)
        v = (hidden_states @ wv.T).reshape(b, s, N_KV_HEADS, HEAD_DIM).transpose(0, 2, 1, 3)
        cos, sin = _rope(s, dtype)
        q = q * cos[None, None] + _rotate_half(q) * sin[None, None]
        k = k * cos[None, None] + _rotate_half(k) * sin[None, None]
        k = jnp.repeat(k, GROUPS, axis=1)
        v = jnp.repeat(v, GROUPS, axis=1)
        scores = jnp.einsum('bhqd,bhkd->bhqk', q, k) / math.sqrt(HEAD_DIM)
        q_pos = jnp.arange(s)[:, None]
        k_pos = jnp.arange(s)[None, :]
        causal = k_pos <= q_pos
        masked = jnp.where(causal[None, None], scores, NEG)
        pad = -s % CHUNK
        padded = jnp.pad(masked, ((0, 0), (0, 0), (0, 0), (0, pad)), constant_values=NEG)
        n_chunks = (s + pad) // CHUNK
        chunk_max = padded.reshape(b, N_HEADS, s, n_chunks, CHUNK).max(axis=-1)
        k_top = min(max(3, TOKEN_BUDGET // CHUNK), n_chunks)
        _, topk_idx = jax.lax.top_k(chunk_max, k_top)
        chunk_mask = jnp.any(topk_idx[..., None] == jnp.arange(n_chunks), axis=-2)
        tok_mask = jnp.repeat(chunk_mask, CHUNK, axis=-1)[..., :s]
        init_mask = k_pos < INIT_BUDGET
        recent_mask = k_pos > q_pos - RECENT_BUDGET
        allowed = causal[None, None] & (tok_mask | init_mask[None, None] | recent_mask[None, None])
        final = jnp.where(allowed, scores, NEG)
        attn = jax.nn.softmax(final, axis=-1)
        out = jnp.einsum('bhqk,bhkd->bhqd', attn, v)
        out = out.transpose(0, 2, 1, 3).reshape(b, s, N_HEADS * HEAD_DIM)
        return out @ wo.T

    def _L1_ffn_ref(x, A, B, Wr, br):
        import jax, jax.numpy as jnp
        import numpy as np
        ALPHA = 32
        R = 16
        SCALING = ALPHA / R
        H = A.shape[0]
        router_logits = jnp.einsum('bsd,hd->bsh', x, Wr) + br
        scores = H * jax.nn.softmax(router_logits, axis=-1)
        low = jnp.einsum('bsd,hrd->bshr', x, A)
        out = jnp.einsum('bshr,hor,bsh->bso', low, B, scores)
        return SCALING * out
    x = L0_attn_x
    xn = _layernorm(x, axis=-1)
    s = _L0_attn_ref(xn, L0_attn_w_qkv, L0_attn_w_o, L0_attn_qc1_w, L0_attn_qc1_b, L0_attn_qc2_w, L0_attn_qc2_b, L0_attn_kc1_w, L0_attn_kc1_b, L0_attn_kc2_w, L0_attn_kc2_b, L0_attn_key_temp)
    g = _silu(_L0_ffn_ref(xn, L0_ffn_gate_w, L0_ffn_up_w, L0_ffn_down_w, L0_ffn_fc1_w, L0_ffn_fc2_w, L0_ffn_expert_w, L0_ffn_ln_gamma, L0_ffn_ln_beta))
    x = x + s * g
    xn = _layernorm(x, axis=-1)
    s = _L1_attn_ref(xn, L1_attn_wq, L1_attn_wk, L1_attn_wv, L1_attn_wo)
    g = _silu(_L1_ffn_ref(xn, L1_ffn_A, L1_ffn_B, L1_ffn_Wr, L1_ffn_br))
    x = x + s * g
    return x

_drawn_inputs = setup_inputs


def setup_inputs(seed=0):
    import zlib

    import numpy as np

    out = dict(_drawn_inputs(seed))
    spreads = {'L0_attn_qc1_b': (0.0, 0.8),
     'L0_attn_qc2_b': (0.0, 2.0),
     'L0_attn_kc1_b': (0.0, 2.0),
     'L0_attn_kc2_b': (0.0, 2.0),
     'L0_ffn_ln_gamma': (1.0, 0.6),
     'L0_ffn_ln_beta': (0.0, 0.8),
     'L1_ffn_br': (0.0, 0.8)}
    factors = {'L0_attn_w_qkv': 3.927,
     'L0_attn_w_o': 3.839,
     'L0_attn_qc1_w': 8.0,
     'L0_attn_qc2_w': 8.0,
     'L0_attn_kc1_w': 8.0,
     'L0_attn_kc2_w': 8.0,
     'L0_ffn_gate_w': 8.0,
     'L0_ffn_up_w': 8.0,
     'L0_ffn_down_w': 8.0,
     'L0_ffn_fc1_w': 4.123,
     'L0_ffn_fc2_w': 4.107,
     'L0_ffn_expert_w': 4.055,
     'L1_attn_wq': 8.0,
     'L1_attn_wk': 8.0,
     'L1_attn_wv': 8.0,
     'L1_attn_wo': 8.0,
     'L1_ffn_A': 8.0,
     'L1_ffn_B': 8.0,
     'L1_ffn_Wr': 8.0}
    for name, (base, spread) in spreads.items():
        noise = np.random.default_rng([zlib.crc32(name.encode()), seed]).standard_normal(out[name].shape)
        drawn = base * np.exp(spread * noise) if base else spread * noise
        out[name] = jnp.asarray(drawn.astype(out[name].dtype))
    for name, factor in factors.items():
        out[name] = (out[name] * factor).astype(out[name].dtype)
    return out
```

```python
from contextlib import ExitStack

import concourse.bass as bass
from concourse import mybir

F32 = mybir.dt.float32
F32R = mybir.dt.float32r
BF16 = mybir.dt.bfloat16
FP16 = mybir.dt.float16
ALU = mybir.AluOpType
ACT = mybir.ActivationFunctionType
AX = mybir.AxisListType

P = 128
B, S, D = 2, 1024, 512
T = B * S
CH = 512
NCH = T // CH
TT = CH // P
KD = D // P
EPS = 1e-5
BIG = 1e30

H0, KV0, HD0 = 16, 4, 64
LAT = H0 * HD0
KVD = KV0 * HD0
MQ, MK = LAT // P, KVD // P
TAPS = 3
PAD = TAPS - 1
INT, LATF, NE = 1024, 256, 8
MI, ML = INT // P, LATF // P
H1, KV1, HD1 = 32, 8, 16
GRP = H1 // KV1
CHUNK = 16
NC = S // CHUNK
QT = S // P
CPT = P // CHUNK
MISS = (S - 1 - P) // CHUNK - CPT
HL, RL, OL = 8, 16, 512
GAIN = 32.0 / RL * HL


def ds(start, size):
    return bass.ds(start, size)


def primed(engine, sem, value):
    engine.sem_inc(sem, value)


def wait_apart(engine, sem, value, ticks):
    engine.wait_ge(sem, value)
    engine.sem_inc(ticks, 1)


def gate_phase(nc, sem, dram, ident):
    with ExitStack() as ctx:
        def sb(name, shape, dt=F32):
            return ctx.enter_context(nc.sbuf_tensor(f"a_{name}", shape, dt))

        def bank(name):
            return ctx.enter_context(nc.psum_tensor(f"a_{name}", [P, CH], F32))

        up = sb("up", [P, KD, INT])
        down = sb("down", [P, MI, D])
        fc1 = sb("fc1", [P, KD, LATF])
        fc2 = sb("fc2", [P, ML, D])
        expert = sb("expert", [P, ML, LATF])
        gate = sb("gate", [P, KD, NE])
        gamma = sb("gamma", [P, D])
        beta = sb("beta", [P, D])
        half = sb("half", [P, TT])
        x_in = sb("x_in", [P, TT, D])
        xn = sb("xn", [P, TT, D])
        xnT = sb("xnT", [P, KD, CH])
        relu = sb("relu", [P, 2, CH])
        hidden = sb("hidden", [P, MI, CH])
        latent = sb("latent", [P, ML, CH])
        mixed = sb("mixed", [P, ML, CH])
        logits = sb("logits", [P, TT, NE])
        top = sb("top", [P, TT, NE])
        route = sb("route", [P, TT])
        y = sb("y", [P, TT, D])
        g_out = sb("g_out", [P, TT, D])
        stats = sb("stats", [P, TT, 6])
        mv = sb("mv", [P, TT, 2])
        var = sb("var", [P, TT])
        rstd = sb("rstd", [P, TT])
        stats2 = sb("stats2", [P, TT, 6])
        mv2 = sb("mv2", [P, TT, 2])
        var2 = sb("var2", [P, TT])
        rstd2 = sb("rstd2", [P, TT])
        ps_t = [bank(f"ps_t{i}") for i in range(2)]
        ps_m = [bank(f"ps_m{i}") for i in range(2)]
        ps_d = [bank(f"ps_d{i}") for i in range(2)]
        ps_r = [bank(f"ps_r{i}") for i in range(2)]

        x_loaded = sem("a_x_loaded")
        w_loaded = sem("a_w_loaded")
        w2_loaded = sem("a_w2_loaded")
        half_set = sem("a_half_set")
        stats_done = sem("a_stats_done")
        aggr_done = sem("a_aggr_done")
        var_ready = sem("a_var_ready")
        rstd_ready = sem("a_rstd_ready")
        xn_ready = sem("a_xn_ready")
        t_done = sem("a_t_done")
        xnT_ready = sem("a_xnT_ready")
        xnT_stored = sem("a_xnT_stored")
        m_done = sem("a_m_done")
        m_free = sem("a_m_free")
        h_ready = sem("a_h_ready")
        top_done = sem("a_top_done")
        route_ready = sem("a_route_ready")
        out_done = sem("a_out_done")
        y_routed = sem("a_y_routed")
        y_ready = sem("a_y_ready")
        stats2_done = sem("a_stats2_done")
        aggr2_done = sem("a_aggr2_done")
        var2_ready = sem("a_var2_ready")
        rstd2_ready = sem("a_rstd2_ready")
        yn_ready = sem("a_yn_ready")
        scaled = sem("a_scaled")
        shifted = sem("a_shifted")
        g_ready = sem("a_g_ready")
        g_stored = sem("a_g_stored")
        ticks = sem("a_ticks")

        UNITS = MI + ML + 1 + ML
        x_rows = dram["x"].rearrange("(c t p) d -> c p t d", t=TT, p=P)
        g_rows = dram["g"].rearrange("(c t p) d -> c p t d", t=TT, p=P)
        block = ctx.enter_context(nc.Block())

        @block.sync
        def _(sp):
            sp.dma_start(x_in[:], x_rows[0]).then_inc(x_loaded, 16)
            sp.dma_start(ident[:], dram["ident"]).then_inc(w_loaded, 16)
            sp.dma_start(up[:], dram["up_w"].rearrange("(k p) n -> p k n", p=P)).then_inc(w_loaded, 16)
            sp.dma_start(fc1[:], dram["fc1_w"].rearrange("(k p) n -> p k n", p=P)).then_inc(w_loaded, 16)
            sp.dma_start(gate[:], dram["gate_w"].rearrange("(k p) n -> p k n", p=P)).then_inc(w_loaded, 16)
            sp.dma_start(expert[:], dram["expert_w"].rearrange("(k p) n -> p k n", p=P)).then_inc(w2_loaded, 16)
            sp.dma_start(down[:], dram["down_w"].rearrange("(k p) n -> p k n", p=P)).then_inc(w2_loaded, 16)
            sp.dma_start(fc2[:], dram["fc2_w"].rearrange("(k p) n -> p k n", p=P)).then_inc(w2_loaded, 16)
            sp.dma_start(gamma[:], dram["ln_gamma"].rearrange("(a n) -> a n", a=1).to_broadcast((P, D))).then_inc(w2_loaded, 16)
            sp.dma_start(beta[:], dram["ln_beta"].rearrange("(a n) -> a n", a=1).to_broadcast((P, D))).then_inc(w2_loaded, 16)

            def store(c):
                sp.wait_ge(xnT_ready, (c + 1) * KD)
                sp.dma_start(dram["xnT"][:, :, ds(c * CH, CH)].rearrange("k p n -> p k n"), xnT[:]).then_inc(xnT_stored, 16)

            with sp.Fori(0, NCH - 1) as c:
                sp.wait_ge(xn_ready, c + 1)
                sp.dma_start(x_in[:], x_rows[ds(c + 1, 1)].rearrange("a p t d -> p (a t) d")).then_inc(x_loaded, 16)
                store(c)
            store(NCH - 1)
            sp.wait_ge(xnT_stored, 16 * (NCH + 1))
            sp.wait_ge(g_stored, 16 * (NCH + 1))

        @block.tensor
        def _(pe):
            pe.wait_ge(w_loaded, 64)
            with pe.Fori(0, NCH) as c:
                pe.wait_ge(xn_ready, c + 1)
                for k in range(KD):
                    if k >= 2:
                        pe.wait_ge(xnT_ready, c * KD + k - 1)
                    for t in range(TT):
                        last = pe.transpose(ps_t[k % 2][:, t * P:(t + 1) * P], xn[:, t, k * P:(k + 1) * P], ident[:])
                    last.then_inc(t_done, 1)
                pe.wait_ge(xnT_ready, (c + 1) * KD)
                for u in range(UNITS):
                    out = ps_m[u % 2]
                    if u == MI + ML + 1:
                        pe.wait_ge(w2_loaded, 80)
                    pe.wait_ge(m_free, c * UNITS + u + 1)
                    if u >= MI + ML + 1:
                        pe.wait_ge(m_free, c * UNITS + MI + ML + 2)
                    if u < MI + ML:
                        w = up[:, :, u * P:(u + 1) * P] if u < MI else fc1[:, :, (u - MI) * P:(u - MI + 1) * P]
                        for k in range(KD):
                            last = pe.matmul(out[:], w[:, k, :], xnT[:, k, :], start=(k == 0), stop=(k == KD - 1))
                    elif u == MI + ML:
                        for t in range(TT):
                            for k in range(KD):
                                last = pe.matmul(out[:, t * NE:(t + 1) * NE], xnT[:, k, t * P:(t + 1) * P], gate[:, k, :],
                                                 start=(k == 0), stop=(k == KD - 1))
                    else:
                        m = u - MI - ML - 1
                        for k in range(ML):
                            last = pe.matmul(out[:], expert[:, k, m * P:(m + 1) * P], latent[:, k, :],
                                             start=(k == 0), stop=(k == ML - 1))
                    last.then_inc(m_done, 1)
                pe.wait_ge(h_ready, (c + 1) * MI + 2)
                for t in range(TT):
                    pe.wait_ge(y_ready, c * TT + t + 1)
                    for k in range(MI):
                        last = pe.matmul(ps_d[t % 2][:], hidden[:, k, t * P:(t + 1) * P], down[:, k, :],
                                         start=(k == 0), stop=(k == MI - 1))
                    if t == 0:
                        pe.wait_ge(m_free, (c + 1) * UNITS + 2)
                    for k in range(ML):
                        last = pe.matmul(ps_r[t % 2][:], mixed[:, k, t * P:(t + 1) * P], fc2[:, k, :],
                                         start=(k == 0), stop=(k == ML - 1))
                    last.then_inc(out_done, 1)

        @block.scalar
        def _(act):
            primed(act, m_free, 2)
            primed(act, g_ready, TT)

            def products(c):
                for u in range(UNITS):
                    act.wait_ge(m_done, c * UNITS + u + 1)
                    src = ps_m[u % 2]
                    if u < MI:
                        act.wait_ge(h_ready, c * MI + u + 1)
                        last = act.activation(relu[:, u % 2, :], src[:], ACT.Relu)
                    elif u < MI + ML:
                        last = act.activation(latent[:, u - MI, :], src[:], ACT.Copy)
                    elif u == MI + ML:
                        last = act.activation(logits[:].rearrange("p t e -> p (t e)"), src[:, 0:TT * NE], ACT.Copy)
                    else:
                        last = act.activation(mixed[:, u - MI - ML - 1, :], src[:], ACT.Copy)
                    last.then_inc(m_free, 1)

            def silu(c):
                act.wait_ge(g_stored, 16 * (c + 1))
                for t in range(TT):
                    act.wait_ge(shifted, c * TT + t + 1)
                    act.activation(g_out[:, t, :], y[:, t, :], ACT.Silu).then_inc(g_ready, 1)
                act.wait_ge(g_ready, (c + 2) * TT)
                act.dma_start(g_rows[ds(c, 1)].rearrange("a p t d -> p (a t) d"), g_out[:]).then_inc(g_stored, 16)

            products(0)
            with act.Fori(0, NCH - 1) as c:
                products(c + 1)
                silu(c)
            silu(NCH - 1)

        @block.gpsimd
        def _(pool):
            primed(pool, g_stored, 16)
            primed(pool, xnT_stored, 16)
            pool.memset(half[:], -0.5).then_inc(half_set, 1)
            pool.wait_ge(half_set, 1)

            def norm_x(c):
                pool.wait_ge(var_ready, c + 1)
                pool.tensor_tensor(rstd[:], var[:], half[:], ALU.pow).then_inc(rstd_ready, 1)

            def norm_y(c):
                pool.wait_ge(var2_ready, c + 1)
                pool.tensor_tensor(rstd2[:], var2[:], half[:], ALU.pow).then_inc(rstd2_ready, 1)
                for t in range(TT):
                    pool.wait_ge(yn_ready, c * TT + t + 1)
                    pool.tensor_tensor(y[:, t, :], y[:, t, :], gamma[:], ALU.mult).then_inc(scaled, 1)
                    pool.wait_ge(scaled, c * TT + t + 1)
                    pool.tensor_tensor(y[:, t, :], y[:, t, :], beta[:], ALU.add).then_inc(shifted, 1)

            norm_x(0)
            pool.wait_ge(w2_loaded, 80)
            with pool.Fori(0, NCH - 1) as c:
                norm_x(c + 1)
                norm_y(c)
            norm_y(NCH - 1)

        @block.vector
        def _(dve):
            primed(dve, h_ready, 2)
            primed(dve, y_ready, 2)

            def norm_x(c):
                dve.wait_ge(x_loaded, 16 * (c + 1))
                for t in range(TT):
                    dve.bn_stats(stats[:, t, :], x_in[:, t, :]).then_inc(stats_done, 1)
                for t in range(TT):
                    wait_apart(dve, stats_done, c * TT + t + 1, ticks)
                    dve.bn_aggr(mv[:, t, :], stats[:, t, :]).then_inc(aggr_done, 1)
                dve.wait_ge(aggr_done, (c + 1) * TT)
                dve.tensor_scalar(var[:], mv[:, :, 1], EPS, None, ALU.add).then_inc(var_ready, 1)
                dve.wait_ge(rstd_ready, c + 1)
                for t in range(TT):
                    last = dve.tensor_scalar(xn[:, t, :], x_in[:, t, :], mv[:, t, 0:1], rstd[:, t:t + 1],
                                             ALU.subtract, ALU.mult)
                last.then_inc(xn_ready, 1)

            def transposed(c):
                dve.wait_ge(xnT_stored, 16 * (c + 1))
                for k in range(KD):
                    dve.wait_ge(t_done, c * KD + k + 1)
                    dve.tensor_copy(xnT[:, k, :], ps_t[k % 2][:]).then_inc(xnT_ready, 1)

            def finish(c):
                for u in range(MI):
                    dve.wait_ge(m_free, c * UNITS + u + 3)
                    dve.tensor_tensor(hidden[:, u, :], relu[:, u % 2, :], relu[:, u % 2, :], ALU.mult)\
                       .then_inc(h_ready, 1)
                wait_apart(dve, m_free, c * UNITS + MI + ML + 3, ticks)
                for t in range(TT):
                    dve.max(top[:, t, :], logits[:, t, :]).then_inc(top_done, 1)
                dve.wait_ge(top_done, (c + 1) * TT)
                dve.tensor_tensor(route[:], top[:, :, 0], top[:, :, 1], ALU.add).then_inc(route_ready, 1)
                dve.wait_ge(route_ready, c + 1)
                for t in range(TT):
                    dve.wait_ge(g_ready, c * TT + t + 1)
                    dve.wait_ge(out_done, c * TT + t + 1)
                    dve.tensor_scalar(y[:, t, :], ps_r[t % 2][:], route[:, t:t + 1], None, ALU.mult).then_inc(y_routed, 1)
                    dve.wait_ge(y_routed, c * TT + t + 1)
                    dve.tensor_tensor(y[:, t, :], y[:, t, :], ps_d[t % 2][:], ALU.add).then_inc(y_ready, 1)
                for t in range(TT):
                    dve.wait_ge(y_ready, c * TT + t + 3)
                    dve.bn_stats(stats2[:, t, :], y[:, t, :]).then_inc(stats2_done, 1)
                for t in range(TT):
                    wait_apart(dve, stats2_done, c * TT + t + 1, ticks)
                    dve.bn_aggr(mv2[:, t, :], stats2[:, t, :]).then_inc(aggr2_done, 1)
                dve.wait_ge(aggr2_done, (c + 1) * TT)
                dve.tensor_scalar(var2[:], mv2[:, :, 1], EPS, None, ALU.add).then_inc(var2_ready, 1)
                dve.wait_ge(rstd2_ready, c + 1)
                for t in range(TT):
                    dve.tensor_scalar(y[:, t, :], y[:, t, :], mv2[:, t, 0:1], rstd2[:, t:t + 1],
                                      ALU.subtract, ALU.mult).then_inc(yn_ready, 1)

            norm_x(0)
            with dve.Fori(0, NCH - 1) as c:
                transposed(c)
                norm_x(c + 1)
                finish(c)
            transposed(NCH - 1)
            finish(NCH - 1)


def project_phase(nc, sem, dram, ident, conv_in):
    with ExitStack() as ctx:
        def sb(name, shape, dt=F32):
            return ctx.enter_context(nc.sbuf_tensor(f"b_{name}", shape, dt))

        wT = sb("wT", [P, KD, LAT + 2 * KVD])
        meanT = sb("meanT", [P, 2, KD, P])
        mean = sb("mean", [P, 2, KD, HD0])
        c1T = sb("c1T", [P, MQ * TAPS, P])
        kc1T = sb("kc1T", [P, MK * TAPS, P])
        kc2T = sb("kc2T", [P, MK * TAPS, KVD])
        bias = sb("bias", [P, MQ + 2 * MK])

        w_loaded = sem("b_w_loaded")
        zeroed = sem("b_zeroed")
        conv_loaded = sem("b_conv_loaded")
        turned = sem("b_turned")
        out_act = sem("b_out_act")
        out_dve = sem("b_out_dve")
        mean_summed = sem("b_mean_summed")

        NO = (LAT + 2 * KVD) // P
        with ExitStack() as prep:
            rows = prep.enter_context(nc.sbuf_tensor("b_rows", [P, NO, D], F32))
            pairs = prep.enter_context(nc.sbuf_tensor("b_pairs", [P, MQ + MK, P, TAPS], F32))
            dense = prep.enter_context(nc.sbuf_tensor("b_dense", [P, MK, KVD, TAPS], F32))
            ps = [prep.enter_context(nc.psum_tensor(f"b_psw{i}", [P, CH], F32)) for i in range(4)]
            groups = []
            for o in range(NO):
                groups.append(([rows[:, o, k * P:(k + 1) * P] for k in range(KD)], wT[:, :, o * P:(o + 1) * P]))
            for m in range(MQ + MK):
                to = c1T[:, m * TAPS:(m + 1) * TAPS, :] if m < MQ else kc1T[:, (m - MQ) * TAPS:(m - MQ + 1) * TAPS, :]
                groups.append(([pairs[:, m, :, a] for a in range(TAPS)], to))
            for o in range(MK):
                for i in range(MK):
                    groups.append(([dense[:, o, i * P:(i + 1) * P, a] for a in range(TAPS)],
                                   kc2T[:, i * TAPS:(i + 1) * TAPS, o * P:(o + 1) * P]))
            with nc.Block() as block:
                @block.sync
                def _(sp):
                    w_rows = dram["w_qkv"].rearrange("(o p) d -> p o d", p=P)
                    sp.dma_start(rows[:], w_rows).then_inc(w_loaded, 16)
                    sp.dma_start(dense[:].rearrange("p o i a -> p o (i a)"),
                                 dram["kc2_w"].rearrange("(o p) i a -> p o (i a)", p=P)).then_inc(conv_loaded, 16)
                    sp.dma_start(bias[:, 0:MQ], dram["qc1_b"].rearrange("(m p) -> p m", p=P), allow_slow_non_contiguous=True).then_inc(conv_loaded, 16)
                    sp.dma_start(bias[:, MQ:MQ + MK], dram["kc1_b"].rearrange("(m p) -> p m", p=P), allow_slow_non_contiguous=True).then_inc(conv_loaded, 16)
                    sp.dma_start(bias[:, MQ + MK:], dram["kc2_b"].rearrange("(m p) -> p m", p=P), allow_slow_non_contiguous=True).then_inc(conv_loaded, 16)
                    sp.wait_ge(zeroed, 1)
                    for g in range(2):
                        lo = g * HD0
                        for src, at, n in ((dram["qc1_w"], 0, MQ), (dram["kc1_w"], MQ, MK)):
                            sp.dma_start(pairs[lo:lo + HD0, at:at + n, lo:lo + HD0, :].rearrange("p m i a -> p m (i a)"),
                                         src.rearrange("(m g p) i a -> g p m (i a)", g=2, p=HD0)[g]).then_inc(conv_loaded, 16)

                @block.gpsimd
                def _(pool):
                    pool.memset(pairs[:], 0.0).then_inc(zeroed, 1)
                    pool.memset(conv_in[:, :, :, 0:PAD], 0.0).then_inc(zeroed, 1)

                @block.tensor
                def _(pe):
                    for n, (blocks, _) in enumerate(groups):
                        if n == 0:
                            pe.wait_ge(w_loaded, 16)
                        if n == NO:
                            pe.wait_ge(conv_loaded, 16 * 8)
                        if n >= 4:
                            pe.wait_ge(out_dve if n % 2 else out_act, (n - 4) // 2 + 1)
                        for j, src in enumerate(blocks):
                            last = pe.transpose(ps[n % 4][:, j * P:(j + 1) * P], src, ident[:])
                        last.then_inc(turned, 1)

                @block.scalar
                def _(act):
                    for n, (blocks, to) in enumerate(groups):
                        if n % 2 == 0:
                            act.wait_ge(turned, n + 1)
                            act.activation(to, ps[n % 4][:, 0:len(blocks) * P].rearrange("p (j n) -> p j n", n=P),
                                           ACT.Copy).then_inc(out_act, 1)

                @block.vector
                def _(dve):
                    for n, (blocks, to) in enumerate(groups):
                        if n % 2 == 1:
                            dve.wait_ge(turned, n + 1)
                            dve.tensor_copy(to, ps[n % 4][:, 0:len(blocks) * P].rearrange("p (j n) -> p j n", n=P))\
                               .then_inc(out_dve, 1)
                    dve.wait_ge(out_act, (len(groups) + 1) // 2)
                    dve.wait_ge(out_dve, len(groups) // 2)
                    for n, (at, heads) in enumerate(((LAT, KV0), (0, H0))):
                        for k in range(KD):
                            dve.tensor_reduce(mean[:, n, k, :], wT[:, k, at:at + heads * HD0].rearrange("p (h c) -> p c h", c=HD0),
                                              AX.X, ALU.add).then_inc(mean_summed, 1)
                    dve.wait_ge(mean_summed, 2 * KD)
                    for n, heads in enumerate((KV0, H0)):
                        for copy in range(2):
                            dve.tensor_scalar(meanT[:, n, :, copy * HD0:(copy + 1) * HD0], mean[:, n, :, :], 0.5 / heads,
                                              None, ALU.mult)

        xb = [sb(f"xb{i}", [P, KD, CH + 1]) for i in range(2)]
        q_pre = sb("q_pre", [P, MQ, PAD + S])
        k_pre = sb("k_pre", [P, MK, PAD + S])
        k_conv = sb("k_conv", [P, MK, PAD + S])
        stage = [sb(f"stage{i}", [P, CH]) for i in range(5)]
        UNITS, RING = MQ + MK + MQ + MK + 2 + 1 + MK, 5
        assert UNITS % RING == 0
        ps = [ctx.enter_context(nc.psum_tensor(f"b_ps{i}", [P, CH], F32)) for i in range(RING)]
        Q0, K0, C0, KC0, V0, M0, K20 = 0, MQ, MQ + MK, 2 * MQ + MK, 2 * MQ + 2 * MK, 2 * MQ + 2 * MK + 2, 2 * MQ + 2 * MK + 3

        padded = sem("b_padded")
        x_loaded = [sem(f"b_x_loaded{i}") for i in range(2)]
        made = sem("b_made")
        took_act = sem("b_took_act")
        took_dve = sem("b_took_dve")
        stored = sem("b_stored")
        N_ACT, N_DVE = (UNITS + 1) // 2, UNITS // 2

        def taken(n, u):
            if u % 2 == 0:
                return took_act, (n + 1) * N_ACT + u // 2 + 1
            return took_dve, (n + 1) * N_DVE + u // 2 + 1

        block = ctx.enter_context(nc.Block())

        @block.sync
        def _(sp):
            primed(sp, stored, 16 * 5)
            sp.wait_ge(padded, 1)
            src = dram["xnT"].rearrange("k p t -> p k t")
            with sp.Fori(0, B) as b:
                for h in range(2):
                    rows = ds(b * S, CH) if h == 0 else ds(b * S + CH - 1, CH + 1)
                    sp.wait_ge(took_act, (2 * b + h) * N_ACT + (1 - h))
                    sp.dma_start(xb[h][:, :, 1 - h:], src[:, :, rows]).then_inc(x_loaded[h], 16)
                for h in range(2):
                    n = 2 * b + h
                    for i, u in enumerate((V0, V0 + 1)):
                        sp.wait_ge(*taken(n, u))
                        sp.dma_start(dram["v"].rearrange("(n t p) c -> n p t c", t=2, p=P)[ds(2 * n + i, 1)].rearrange("a p t c -> p (a t) c"),
                                     stage[i][:].rearrange("p (t c) -> p t c", t=2)).then_inc(stored, 16)
                    sp.wait_ge(*taken(n, M0))
                    sp.dma_start(dram["k_mean"][:, ds(n * CH, CH)], stage[2][:]).then_inc(stored, 16)
                    for i in range(MK):
                        sp.wait_ge(*taken(n, K20 + i))
                        sp.dma_start(dram["k_raw"][i, :, ds(n * CH, CH)], stage[3 + i][:]).then_inc(stored, 16)
            sp.wait_ge(stored, 16 * 5 * (NCH + 1))

        @block.gpsimd
        def _(pool):
            pool.memset(q_pre[:, :, 0:PAD], 0.0)
            pool.memset(k_pre[:, :, 0:PAD], 0.0)
            pool.memset(k_conv[:, :, 0:PAD], 0.0)
            pool.memset(xb[0][:, :, 0:1], 0.0).then_inc(padded, 1)

        @block.tensor
        def _(pe):
            pe.wait_ge(padded, 1)

            def unit(b, h, u):
                n, out = 2 * b + h, ps[u % RING]
                pe.wait_ge(*(taken(n, u - RING) if u >= RING else taken(n - 1, u + UNITS - RING)))
                x, lo = xb[h], h * CH
                if u < C0:
                    for k in range(KD):
                        last = pe.matmul(out[:], wT[:, k, u * P:(u + 1) * P], x[:, k, 1:], start=(k == 0), stop=(k == KD - 1))
                elif u < V0:
                    m, wgt, src, of = (u - C0, c1T, q_pre, Q0) if u < KC0 else (u - KC0, kc1T, k_pre, K0)
                    pe.wait_ge(*taken(n, of + m))
                    for a in range(TAPS):
                        last = pe.matmul(out[:], wgt[:, m * TAPS + a, :], src[:, m, lo + a:lo + a + CH],
                                         start=(a == 0), stop=(a == TAPS - 1))
                elif u < M0:
                    for t in range(2):
                        col = (2 * (u - V0) + t) * P
                        for late in range(2):
                            for k in range(KD):
                                last = pe.matmul(out[:, t * KVD + late * P:t * KVD + (late + 1) * P],
                                                 x[:, k, col + 1 - late:col + 1 - late + P],
                                                 wT[:, k, LAT + KVD + late * P:LAT + KVD + (late + 1) * P],
                                                 start=(k == 0), stop=(k == KD - 1))
                elif u == M0:
                    for k in range(KD):
                        last = pe.matmul(out[:], meanT[:, 0, k, :], x[:, k, 1:], start=(k == 0), stop=(k == KD - 1))
                else:
                    o = u - K20
                    for k in range(KD):
                        pe.matmul(out[:], meanT[:, 1, k, :], x[:, k, 1:], start=(k == 0), stop=False)
                    for i in range(MK):
                        pe.wait_ge(*taken(n, KC0 + i))
                        for a in range(TAPS):
                            last = pe.matmul(out[:], kc2T[:, i * TAPS + a, o * P:(o + 1) * P], k_conv[:, i, lo + a:lo + a + CH],
                                             start=False, stop=(i == MK - 1 and a == TAPS - 1))
                last.then_inc(made, 1)

            with pe.Fori(0, B) as b:
                for h in range(2):
                    pe.wait_ge(x_loaded[h], 16 * (b + 1))
                    for u in range(UNITS):
                        unit(b, h, u)

        def take(engine, b, h, u):
            n, src, lo = 2 * b + h, ps[u % RING], PAD + h * CH
            engine.wait_ge(made, n * UNITS + u + 1)
            if u >= V0 and u != K20 + 1:
                engine.wait_ge(stored, 16 * 5 * (n + 1))
            if u < K0:
                to, add = q_pre[:, u, lo:lo + CH], None
            elif u < C0:
                to, add = k_pre[:, u - K0, lo:lo + CH], None
            elif u < KC0:
                to, add = conv_in[:, u - C0, ds(b, 1), lo:lo + CH].rearrange("p b n -> p (b n)"), u - C0
            elif u < V0:
                to, add = k_conv[:, u - KC0, lo:lo + CH], MQ + u - KC0
            else:
                to, add = stage[u - V0][:], (MQ + MK + u - K20 if u >= K20 else None)
            if engine.engine == mybir.EngineType.Activation:
                if add is None:
                    return engine.activation(to, src[:], ACT.Copy)
                return engine.activation(to, src[:], ACT.Identity, bias=bias[:, add:add + 1])
            if add is None:
                return engine.tensor_copy(to, src[:])
            return engine.tensor_scalar(to, src[:], bias[:, add:add + 1], None, ALU.add)

        @block.scalar
        def _(act):
            primed(act, took_act, N_ACT)
            with act.Fori(0, B) as b:
                for h in range(2):
                    for u in range(0, UNITS, 2):
                        take(act, b, h, u).then_inc(took_act, 1)

        @block.vector
        def _(dve):
            primed(dve, took_dve, N_DVE)
            with dve.Fori(0, B) as b:
                for h in range(2):
                    for u in range(1, UNITS, 2):
                        take(dve, b, h, u).then_inc(took_dve, 1)


def query_phase(nc, sem, dram, ident, conv_in):
    with ExitStack() as ctx:
        def sb(name, shape, dt=F32):
            return ctx.enter_context(nc.sbuf_tensor(f"c_{name}", shape, dt))

        def bank(name):
            return ctx.enter_context(nc.psum_tensor(f"c_{name}", [P, CH], F32))

        rows = [sb(f"rows{i}", [P, LAT, TAPS]) for i in range(2)]
        wT = [sb(f"wT{i}", [P, MQ * TAPS, P]) for i in range(2)]
        k_mean = sb("k_mean", [P, T])
        k_in = sb("k_in", [P, MK, T])
        raw = [sb(f"raw{i}", [P, T]) for i in range(2)]
        square = sb("square", [P, T])
        swapped = sb("swapped", [P, B, S])
        turned = sb("turned", [P, B, S])
        high = sb("high", [P, T], FP16)
        low = sb("low", [P, T], FP16)
        cos = sb("cos", [P, S])
        sin = sb("sin", [P, S])
        head2 = sb("head2", [P, 2])
        temp = sb("temp", [P, 1])
        bias = sb("bias", [P, MQ])
        norm = sb("norm", [P, 2 * T // P])
        rnorm = sb("rnorm", [P, 2 * T // P])
        half = sb("half", [P, 2 * T // P])
        ps_c = [bank(f"ps_c{i}") for i in range(2)]
        ps_t = [bank(f"ps_t{i}") for i in range(2)]
        ps_b = [bank(f"ps_b{i}") for i in range(2)]
        ps_s = bank("ps_s")

        tables = sem("c_tables")
        k_loaded = sem("c_k_loaded")
        rows_loaded = [sem(f"c_rows_loaded{i}") for i in range(2)]
        half_set = sem("c_half_set")
        w_turned = sem("c_w_turned")
        w_ready = sem("c_w_ready")
        conv_done = sem("c_conv_done")
        raw_ready = sem("c_raw_ready")
        square_ready = sem("c_square_ready")
        sums_done = sem("c_sums_done")
        norm_ready = sem("c_norm_ready")
        powed = sem("c_powed")
        rnorm_ready = sem("c_rnorm_ready")
        swap_ready = sem("c_swap_ready")
        rot_step = sem("c_rot_step")
        spread_done = sem("c_spread_done")
        unit_ready = sem("c_unit_ready")
        high_ready = sem("c_high_ready")
        low_ready = sem("c_low_ready")
        stored = sem("c_stored")
        ticks = sem("c_ticks")

        BLOCKS = MQ * TAPS
        WG = BLOCKS // 4
        PAIRS = [p ^ 1 for p in range(32)]

        def stored_by(j):
            return 128 * j if isinstance(j, int) and j <= MK else 128 * MK + (j - MK) * 64

        def after(m, n):
            if isinstance(m, int) and m == 0:
                return ((("sums", 0),), (("turn", 0), ("spread", 0)), (("sums", 1), ("turn", 1)), (("spread", 1),))[n]
            turn = () if isinstance(m, int) and m == MQ - 1 else (("turn", n - 1),)
            return ((("sums", m + 1),), turn, (("spread", m + 1),) + turn, ())[n]

        block = ctx.enter_context(nc.Block())

        @block.sync
        def _(sp):
            w_rows = dram["qc2_w"].rearrange("(m p) i a -> m p (i a)", p=P)

            def load_rows(m, u):
                sp.dma_start(rows[u][:].rearrange("p i a -> p (i a)"), w_rows[ds(m, 1)].rearrange("m p n -> p (m n)"))\
                  .then_inc(rows_loaded[u], 16)

            load_rows(0, 0)
            sp.dma_start(k_in[:], dram["k_raw"].rearrange("m p t -> p m t")).then_inc(k_loaded, 16)
            sp.dma_start(k_mean[:], dram["k_mean"]).then_inc(tables, 16)
            sp.dma_start(bias[:], dram["qc2_b"].rearrange("(m p) -> p m", p=P), allow_slow_non_contiguous=True).then_inc(tables, 16)
            sp.dma_start(head2[:], dram["head2"]).then_inc(tables, 16)
            sp.dma_start(cos[:], dram["cos0"]).then_inc(tables, 16)
            sp.dma_start(sin[:], dram["sin0"]).then_inc(tables, 16)
            sp.dma_start(temp[:], dram["key_temp"].rearrange("(a n) -> a n", a=1).to_broadcast((P, 1))).then_inc(tables, 16)
            load_rows(1, 1)

            def store_keys(j):
                sp.wait_ge(low_ready, j + 1)
                for g in range(2):
                    for part, to in ((high, "k_high"), (low, "k_low")):
                        for copy in range(2):
                            sp.dma_start(dram[to][2 * j + g, copy * HD0:(copy + 1) * HD0, :], part[g * HD0:(g + 1) * HD0, :])\
                              .then_inc(stored, 16)

            def store_queries(m):
                sp.wait_ge(low_ready, m + MK + 1)
                for g in range(2):
                    for n, part in enumerate((high, low)):
                        sp.dma_start(dram["q_parts"][ds(2 * m + g, 1), n * HD0:(n + 1) * HD0, :].rearrange("a p t -> p (a t)"),
                                     part[g * HD0:(g + 1) * HD0, :]).then_inc(stored, 16)

            store_keys(0)
            store_keys(1)
            with sp.Fori(0, MQ // 2 - 1) as i:
                for u in range(2):
                    sp.wait_ge(w_turned, WG * (2 * i + u + 1))
                    load_rows(2 * i + 2 + u, u)
                for u in range(2):
                    store_queries(2 * i + u)
            store_queries(MQ - 2)
            store_queries(MQ - 1)
            sp.wait_ge(stored, stored_by(MQ + MK))

        @block.tensor
        def _(pe):
            def turn(k, u, loaded, groups):
                for g in groups:
                    if g == 0:
                        pe.wait_ge(rows_loaded[u], 16 * loaded)
                    if g >= 2 or not isinstance(k, int) or k > 0:
                        pe.wait_ge(w_ready, WG * k + g - 1 if g >= 2 else WG * k)
                    for j in range(4):
                        i, a = divmod(4 * g + j, TAPS)
                        last = pe.transpose(ps_t[g % 2][:, j * P:(j + 1) * P], rows[u][:, i * P:(i + 1) * P, a], ident[:])
                    last.then_inc(w_turned, 1)

            def sums(j):
                pe.wait_ge(square_ready, j + 1)
                if not isinstance(j, int) or j > 0:
                    pe.wait_ge(norm_ready, j)
                for t in range(T // P):
                    last = pe.matmul(ps_s[:, 2 * t:2 * t + 2], square[:, t * P:(t + 1) * P], head2[:], start=True, stop=True)
                last.then_inc(sums_done, 1)

            def spread(j):
                pe.wait_ge(rnorm_ready, j + 1)
                for n in range(NCH):
                    if n >= 2:
                        pe.wait_ge(unit_ready, NCH * j + n - 1)
                    for t in range(TT):
                        c = 2 * (n * TT + t)
                        last = pe.matmul(ps_b[n % 2][:, t * P:(t + 1) * P],
                                         square[:, c * HD0:(c + 2) * HD0],
                                         ident[:], start=True, stop=True)
                    last.then_inc(spread_done, 1)

            def tile(m, u, loaded):
                pe.wait_ge(w_ready, WG * (m + 1))
                for n in range(NCH):
                    if n >= 2 or not isinstance(m, int) or m > 0:
                        pe.wait_ge(raw_ready, NCH * m + n - 1)
                    b, h = divmod(n, NCH // B)
                    for i in range(MQ):
                        for a in range(TAPS):
                            last = pe.matmul(ps_c[n % 2][:], wT[u][:, i * TAPS + a, :], conv_in[:, i, b, h * CH + a:h * CH + a + CH],
                                             start=(i == 0 and a == 0), stop=(i == MQ - 1 and a == TAPS - 1))
                    last.then_inc(conv_done, 1)
                    for what, j in after(m, n):
                        if what == "sums":
                            sums(j)
                        elif what == "spread":
                            spread(j)
                        else:
                            turn(m + 1, 1 - u, loaded, range(j * WG // 2, (j + 1) * WG // 2))

            pe.wait_ge(tables, 16 * 6)
            turn(0, 0, 1, range(WG))
            tile(0, 0, 1)
            with pe.Fori(0, MQ // 2 - 1) as i:
                tile(2 * i + 1, 1, i + 2)
                tile(2 * i + 2, 0, i + 2)
            tile(MQ - 1, 1, None)
            sums(MQ + 1)
            spread(MQ + 1)

        @block.scalar
        def _(act):
            def weights(k, u, groups):
                for g in groups:
                    act.wait_ge(w_turned, WG * k + g + 1)
                    act.activation(wT[u][:, 4 * g:4 * g + 4, :].rearrange("p j n -> p (j n)"), ps_t[g % 2][:], ACT.Copy)\
                       .then_inc(w_ready, 1)

            def squares(j, src):
                if isinstance(j, int) and j < MK:
                    act.wait_ge(k_loaded, 16)
                else:
                    act.wait_ge(raw_ready, NCH * (j - MK + 1))
                if not isinstance(j, int) or j > 0:
                    act.wait_ge(spread_done, NCH * j)
                act.activation(square[:], src, ACT.Square).then_inc(square_ready, 1)

            def highs(j):
                act.wait_ge(unit_ready, NCH * (j + 1))
                if not isinstance(j, int) or j > 0:
                    act.wait_ge(stored, stored_by(j))
                act.activation(high[:], turned[:].rearrange("p b s -> p (b s)"), ACT.Copy).then_inc(high_ready, 1)

            def tile(m, u):
                squares(m + 1, raw[1 - u][:])
                weights(m + 1, 1 - u, range(WG))
                highs(m + 1)

            weights(0, 0, range(WG))
            squares(0, k_in[:, 0, :])
            weights(1, 1, range(WG // 2))
            highs(0)
            squares(1, k_in[:, 1, :])
            weights(1, 1, range(WG // 2, WG))
            highs(1)
            with act.Fori(0, MQ // 2 - 1) as i:
                tile(2 * i + 1, 1)
                tile(2 * i + 2, 0)
            squares(MQ, raw[0][:])
            highs(MQ)
            squares(MQ + 1, raw[1][:])
            highs(MQ + 1)

        @block.gpsimd
        def _(pool):
            pool.memset(half[:], -0.5).then_inc(half_set, 1)
            pool.wait_ge(half_set, 1)
            pool.wait_ge(tables, 16 * 6)

            def rotate(j, src):
                src = src.rearrange("p (b s) -> p b s", b=B)
                if not isinstance(j, int) or j > 0:
                    pool.wait_ge(spread_done, NCH * j)
                pool.wait_ge(norm_ready, j + 1)
                pool.tensor_tensor(rnorm[:], norm[:], half[:], ALU.pow).then_inc(powed, 1)
                wait_apart(pool, powed, j + 1, ticks)
                pool.tensor_scalar(square[:].rearrange("p (n c) -> p n c", c=HD0),
                                   rnorm[:].rearrange("p (n o) -> p n o", o=1).to_broadcast((P, 2 * T // P, HD0)),
                                   temp[:, 0:1] if isinstance(j, int) and j < MK else 1.0, None, ALU.mult)\
                    .then_inc(rnorm_ready, 1)
                if not isinstance(j, int) or j > 0:
                    pool.wait_ge(low_ready, j)
                pool.wait_ge(swap_ready, j + 1)
                for b in range(B):
                    pool.tensor_tensor(turned[:, b, :], src[:, b, :], cos[:], ALU.mult)
                    pool.tensor_tensor(swapped[:, b, :], swapped[:, b, :], sin[:], ALU.mult).then_inc(rot_step, 1)
                for b in range(B):
                    pool.wait_ge(rot_step, 2 * B * j + B)
                    pool.tensor_tensor(turned[:, b, :], turned[:, b, :], swapped[:, b, :], ALU.add).then_inc(rot_step, 1)

            rotate(0, k_in[:, 0, :])
            rotate(1, k_in[:, 1, :])
            with pool.Fori(0, MQ // 2 - 1) as i:
                rotate(2 * i + 2, raw[0][:])
                rotate(2 * i + 3, raw[1][:])
            rotate(MQ, raw[0][:])
            rotate(MQ + 1, raw[1][:])

        @block.vector
        def _(dve):
            dve.wait_ge(tables, 16 * 6)

            def take(m, u, n):
                dve.wait_ge(conv_done, NCH * m + n + 1)
                dve.scalar_tensor_tensor(raw[u][:, n * CH:(n + 1) * CH], ps_c[n % 2][:], bias[:, ds(m, 1)],
                                         k_mean[:, n * CH:(n + 1) * CH], ALU.add, ALU.add).then_inc(raw_ready, 1)

            def norms(j, src):
                dve.wait_ge(sums_done, j + 1)
                dve.tensor_scalar(norm[:], ps_s[:, 0:2 * T // P], 1e-24, None, ALU.max).then_inc(norm_ready, 1)
                if isinstance(j, int) and j < MK:
                    dve.wait_ge(k_loaded, 16)
                else:
                    wait_apart(dve, raw_ready, NCH * (j - MK + 1), ticks)
                dve.stream_shuffle(swapped[:].rearrange("p b s -> p (b s)"), src, PAIRS).then_inc(swap_ready, 1)

            def split(j):
                dve.wait_ge(rot_step, 2 * B * (j + 1))
                flat = turned[:].rearrange("p b s -> p (b s)")
                for n in range(NCH):
                    dve.wait_ge(spread_done, NCH * j + n + 1)
                    dve.tensor_tensor(flat[:, n * CH:(n + 1) * CH], flat[:, n * CH:(n + 1) * CH], ps_b[n % 2][:], ALU.mult)\
                       .then_inc(unit_ready, 1)
                dve.wait_ge(high_ready, j + 1)
                dve.tensor_tensor(low[:], flat, high[:], ALU.subtract).then_inc(low_ready, 1)

            def tile(m, u):
                take(m, u, 0)
                norms(m + 1, raw[1 - u][:])
                take(m, u, 1)
                take(m, u, 2)
                split(m + 1)
                take(m, u, 3)

            take(0, 0, 0)
            norms(0, k_in[:, 0, :])
            take(0, 0, 1)
            split(0)
            take(0, 0, 2)
            norms(1, k_in[:, 1, :])
            take(0, 0, 3)
            split(1)
            with dve.Fori(0, MQ // 2 - 1) as i:
                tile(2 * i + 1, 1)
                tile(2 * i + 2, 0)
            tile(MQ - 1, 1)
            norms(MQ + 1, raw[1][:])
            split(MQ + 1)


def attend_phase(nc, sem, dram, ident_bf, mask_kq):
    with ExitStack() as ctx:
        def sb(name, shape, dt=F32):
            return ctx.enter_context(nc.sbuf_tensor(f"d_{name}", shape, dt))

        G0 = H0 // KV0
        RING = 4
        q = [sb(f"q{b}", [P, G0, S], FP16) for b in range(B)]
        k_high = [sb(f"k_high{b}", [P, S], FP16) for b in range(B)]
        k_low = [sb(f"k_low{b}", [P, S], FP16) for b in range(B)]
        v = [sb(f"v{b}", [P, QT, 3 * HD0]) for b in range(B)]
        probs = [sb(f"probs{i}", [P, S]) for i in range(RING)]
        inverse = [sb(f"inverse{i}", [P, S]) for i in range(2)]
        stage = [sb(f"stage{i}", [P, S]) for i in range(2)]
        temp = sb("temp", [P, 1])
        minus = sb("minus", [P, 1])
        bound = sb("bound", [P, 1])
        shift = sb("shift", [P, 1])
        ps_s = [ctx.enter_context(nc.psum_tensor(f"d_ps_s{i}", [P, S], F32)) for i in range(2)]
        ps_o = [ctx.enter_context(nc.psum_tensor(f"d_ps_o{i}", [P, S], F32)) for i in range(2)]

        masks_loaded = sem("d_masks_loaded")
        temp_loaded = sem("d_temp_loaded")
        ones_set = sem("d_ones_set")
        bound_step = sem("d_bound_step")
        loaded = [sem(f"d_loaded{b}") for b in range(B)]
        s_done = sem("d_s_done")
        p_ready = sem("d_p_ready")
        pv_done = sem("d_pv_done")
        inverse_ready = sem("d_inverse_ready")
        o_used = sem("d_o_used")
        stored = [sem(f"d_stored{i}") for i in range(2)]

        STEPS = QT
        BODY = B * G0 * STEPS
        HEADS = B * G0
        PAIRS = HEADS // 2
        block = ctx.enter_context(nc.Block())

        @block.sync
        def _(sp):
            sp.dma_start(ident_bf[:], dram["ident_bf"]).then_inc(masks_loaded, 16)
            sp.dma_start(mask_kq[:], dram["mask_kq"]).then_inc(masks_loaded, 16)
            sp.dma_start(temp[:], dram["key_temp"].rearrange("(a n) -> a n", a=1).to_broadcast((P, 1))).then_inc(temp_loaded, 16)
            sp.wait_ge(ones_set, 2 * B)

            def load(g, b):
                sp.dma_start(q[b][:], dram["q_parts"].rearrange("(g h) p t -> g p h t", h=G0)[ds(g, 1), :, :, b * S:(b + 1) * S]
                             .rearrange("a p h t -> p (a h) t")).then_inc(loaded[b], 16)
                for to, name in ((k_high, "k_high"), (k_low, "k_low")):
                    sp.dma_start(to[b][:], dram[name][ds(g, 1), :, b * S:(b + 1) * S].rearrange("a p t -> p (a t)")).then_inc(loaded[b], 16)
                sp.dma_start(v[b][:, :, HD0:2 * HD0],
                             dram["v"][b * S:(b + 1) * S, ds(g * HD0, HD0)].rearrange("(n p) c -> p n c", p=P)).then_inc(loaded[b], 16)

            def store(g, b):
                for n in range(b * (G0 // 2), (b + 1) * (G0 // 2)):
                    sp.wait_ge(o_used, g * HEADS + 2 * n + 4)
                    sp.dma_start(dram["o0T"][ds(g * (G0 // 2) + n % (G0 // 2), 1), :, b * S:(b + 1) * S].rearrange("a p t -> p (a t)"),
                                 stage[n % 2][:]).then_inc(stored[n % 2], 16)

            for b in range(B):
                load(0, b)
            with sp.Fori(0, KV0 - 1) as g:
                for b in range(B):
                    store(g, b)
                    sp.wait_ge(pv_done, g * BODY + (b + 1) * G0 * STEPS + RING)
                    load(g + 1, b)
            for b in range(B):
                store(KV0 - 1, b)
            for i in range(2):
                sp.wait_ge(stored[i], 16 * (KV0 * PAIRS // 2 + 1))

        def halves(kt):
            return [(max(lo, kt * P), lo + CH) for lo in range(0, S, CH) if lo + CH > kt * P]

        @block.tensor
        def _(pe):
            def scores(g, n):
                hb, kt = divmod(n, STEPS)
                b, h = divmod(hb, G0)
                if n % (G0 * STEPS) == 0:
                    pe.wait_ge(loaded[b], 64 * (g + 1))
                pe.wait_ge(p_ready, g * BODY + n + 1)
                out = ps_s[n % 2]
                for lo, hi in halves(kt):
                    pe.matmul(out[:, lo:hi], k_high[b][:, kt * P:(kt + 1) * P], q[b][:, h, lo:hi], start=True, stop=False)
                pe.matmul(out[:, kt * P:(kt + 1) * P], ident_bf[:], mask_kq[:], start=False, stop=False)
                for lo, hi in halves(kt):
                    last = pe.matmul(out[:, lo:hi], k_low[b][:, kt * P:(kt + 1) * P], q[b][:, h, lo:hi], start=False, stop=True)
                last.then_inc(s_done, 1)

            def values(g, n):
                hb, kt = divmod(n, STEPS)
                b, h = divmod(hb, G0)
                if kt == 0:
                    pe.wait_ge(o_used, g * HEADS + hb + 1)
                pe.wait_ge(p_ready, g * BODY + n + 3)
                at = HD0 if h % 2 == 0 else 0
                for lo, hi in halves(kt):
                    last = pe.matmul(ps_o[hb % 2][:, lo:hi], v[b][:, kt, at:at + P], probs[n % RING][:, lo:hi],
                                     start=(kt == 0), stop=((kt + 1) * P == hi))
                last.then_inc(pv_done, 1)

            pe.wait_ge(masks_loaded, 32)
            with pe.Fori(0, KV0) as g:
                scores(g, 0)
                for n in range(BODY):
                    if n + 1 < BODY:
                        scores(g, n + 1)
                    values(g, n)

        @block.scalar
        def _(act):
            primed(act, p_ready, 2)
            act.wait_ge(bound_step, 4)
            with act.Fori(0, KV0) as g:
                for n in range(BODY):
                    kt = n % STEPS
                    act.wait_ge(pv_done, g * BODY + n + 1)
                    act.wait_ge(s_done, g * BODY + n + 1)
                    act.activation(probs[n % RING][:, kt * P:], ps_s[n % 2][:, kt * P:], ACT.Exp, bias=shift[:, 0:1],
                                   scale=HD0 ** -0.5).then_inc(p_ready, 1)

        @block.gpsimd
        def _(pool):
            primed(pool, pv_done, RING)
            for b in range(B):
                pool.memset(v[b][:, :, 0:HD0], 1.0).then_inc(ones_set, 1)
                pool.memset(v[b][:, :, 2 * HD0:], 1.0).then_inc(ones_set, 1)

        @block.vector
        def _(dve):
            primed(dve, o_used, 2)
            for i in range(2):
                primed(dve, stored[i], 16)
            dve.wait_ge(temp_loaded, 16)
            dve.tensor_scalar(minus[:], temp[:], -1.0, None, ALU.mult).then_inc(bound_step, 1)
            dve.wait_ge(bound_step, 1)
            dve.tensor_tensor(bound[:], temp[:], minus[:], ALU.max).then_inc(bound_step, 1)
            dve.wait_ge(bound_step, 2)
            dve.tensor_scalar(minus[:], bound[:], -HD0 ** -0.5, 60.0, ALU.mult, ALU.add).then_inc(bound_step, 1)
            dve.wait_ge(bound_step, 3)
            dve.tensor_scalar(shift[:], minus[:], 0.0, None, ALU.min).then_inc(bound_step, 1)
            with dve.Fori(0, KV0) as g:
                for hb in range(HEADS):
                    rows, sums = (slice(0, HD0), slice(HD0, P)) if hb % 2 == 0 else (slice(HD0, P), slice(0, HD0))
                    n = hb // 2
                    dve.wait_ge(pv_done, g * BODY + (hb + 1) * STEPS + RING)
                    dve.reciprocal(inverse[hb % 2][rows, :], ps_o[hb % 2][sums, :]).then_inc(inverse_ready, 1)
                    if hb % 2 == 0:
                        dve.wait_ge(stored[n % 2], 16 * (g * PAIRS // 2 + n // 2 + 1))
                    dve.wait_ge(inverse_ready, g * HEADS + hb + 1)
                    dve.tensor_tensor(stage[n % 2][rows, :], ps_o[hb % 2][rows, :], inverse[hb % 2][rows, :], ALU.mult)\
                       .then_inc(o_used, 1)


def middle_phase(nc, sem, dram, ident):
    with ExitStack() as ctx:
        def sb(name, shape, dt=F32):
            return ctx.enter_context(nc.sbuf_tensor(f"e_{name}", shape, dt))

        KV1D = KV1 * HD1
        TOK = KV1D + HL * RL + HL
        LOW, LOG = KV1D, KV1D + HL * RL
        NQK = D // P + KV1D // P
        oT = sb("oT", [P, MQ, D])
        qkT = sb("qkT", [P, NQK, KD, P])
        tokT = sb("tokT", [P, KD, TOK])
        bT = sb("bT", [P, OL])
        br = sb("br", [P, HL])
        cos = sb("cos", [P, B, S])
        sin = sb("sin", [P, B, S])
        half = sb("half", [P, TT])

        w_loaded = sem("e_w_loaded")
        turned = sem("e_turned")
        out_act = sem("e_out_act")
        out_dve = sem("e_out_dve")
        tables = sem("e_tables")

        with ExitStack() as prep:
            def raw_w(name, shape):
                return prep.enter_context(nc.sbuf_tensor(f"e_w_{name}", shape, F32))

            o_rows = raw_w("o", [P, KD, LAT])
            q_rows = raw_w("q", [P, NQK, D])
            v_rows = raw_w("v", [P, 2, D])
            r_rows = raw_w("r", [HL, D])
            b_rows = raw_w("b", [P, OL // P, HL, RL])
            ps = [prep.enter_context(nc.psum_tensor(f"e_psw{i}", [P, CH], F32)) for i in range(4)]
            groups = []
            for m in range(MQ):
                groups.append(([o_rows[:, o, m * P:(m + 1) * P] for o in range(KD)], P, oT[:, m, :].rearrange("p (o n) -> p o n", n=P)))
            for i in range(NQK):
                groups.append(([q_rows[:, i, k * P:(k + 1) * P] for k in range(KD)], P, qkT[:, i, :, :]))
            for i in range(2):
                groups.append(([v_rows[:, i, k * P:(k + 1) * P] for k in range(KD)], P, tokT[:, :, i * P:(i + 1) * P]))
            groups.append(([r_rows[:, k * P:(k + 1) * P] for k in range(KD)], HL, tokT[:, :, LOG:]))
            groups.append(([b_rows[:, o, :, :].rearrange("p h r -> p (h r)") for o in range(OL // P)], P,
                           bT[:].rearrange("p (o n) -> p o n", n=P)))
            with nc.Block() as block:
                @block.sync
                def _(sp):
                    sp.dma_start(o_rows[:], dram["w_o"].rearrange("(o p) c -> p o c", p=P)).then_inc(w_loaded, 16)
                    sp.dma_start(q_rows[:, 0:D // P, :], dram["wq"].rearrange("(o p) c -> p o c", p=P)).then_inc(w_loaded, 16)
                    sp.dma_start(q_rows[:, D // P:, :], dram["wk"].rearrange("(o p) c -> p o c", p=P)).then_inc(w_loaded, 16)
                    sp.dma_start(v_rows[:, 0, :], dram["wv"]).then_inc(w_loaded, 16)
                    sp.dma_start(v_rows[:, 1, :], dram["lora_a"].rearrange("h r d -> (h r) d")).then_inc(w_loaded, 16)
                    sp.dma_start(r_rows[:], dram["lora_r"]).then_inc(w_loaded, 16)
                    for o in range(OL // P):
                        sp.dma_start(b_rows[:, o, :, :], dram["lora_b"][:, o * P:(o + 1) * P, :].rearrange("h p r -> p h r")).then_inc(w_loaded, 16)
                    for b in range(B):
                        sp.dma_start(cos[:, b, :], dram["cos1"]).then_inc(tables, 16)
                        sp.dma_start(sin[:, b, :], dram["sin1"]).then_inc(tables, 16)
                    sp.dma_start(br[:], dram["lora_br"].rearrange("(a n) -> a n", a=1).to_broadcast((P, HL))).then_inc(tables, 16)

                @block.tensor
                def _(pe):
                    pe.wait_ge(w_loaded, 16 * (6 + OL // P))
                    for n, (blocks, cols, _) in enumerate(groups):
                        if n >= 4:
                            pe.wait_ge(out_dve if n % 2 else out_act, (n - 4) // 2 + 1)
                        for j, src in enumerate(blocks):
                            last = pe.transpose(ps[n % 4][:, j * cols:(j + 1) * cols], src, ident[0:cols, 0:cols])
                        last.then_inc(turned, 1)

                @block.scalar
                def _(act):
                    for n, (blocks, cols, to) in enumerate(groups):
                        if n % 2 == 0:
                            act.wait_ge(turned, n + 1)
                            act.activation(to, ps[n % 4][:, 0:len(blocks) * cols].rearrange("p (j n) -> p j n", n=cols),
                                           ACT.Copy).then_inc(out_act, 1)

                @block.vector
                def _(dve):
                    for n, (blocks, cols, to) in enumerate(groups):
                        if n % 2 == 1:
                            dve.wait_ge(turned, n + 1)
                            dve.tensor_copy(to, ps[n % 4][:, 0:len(blocks) * cols].rearrange("p (j n) -> p j n", n=cols))\
                               .then_inc(out_dve, 1)

        x_in = sb("x_in", [P, TT, D])
        g_in = sb("g_in", [P, TT, D])
        o_in = sb("o_in", [P, MQ, CH])
        x1 = sb("x1", [P, TT, D])
        stats = sb("stats", [P, TT, 6])
        mv = sb("mv", [P, TT, 2])
        var = sb("var", [P, TT])
        rstd = sb("rstd", [P, TT])
        xn = sb("xn", [P, TT, D])
        xnT = sb("xnT", [P, KD, CH])
        raw = sb("raw", [P, NQK, CH])
        swapped = sb("swapped", [P, NQK, CH])
        turn = sb("turn", [P, NQK, CH])
        high = sb("high", [P, NQK, CH], F32R)
        low = sb("low", [P, NQK, CH], F32R)
        tok = sb("tok", [P, TT, TOK])
        logits = sb("logits", [P, TT, HL])
        top = sb("top", [P, TT])
        expo = sb("expo", [P, TT, HL])
        total = sb("total", [P, TT])
        inverse = sb("inverse", [P, TT])
        share = sb("share", [P, TT, HL])
        weighted = sb("weighted", [P, TT, HL * RL])
        weightedT = sb("weightedT", [P, CH])
        gate = sb("gate", [P, TT, OL])

        def bank(name):
            return ctx.enter_context(nc.psum_tensor(f"e_{name}", [P, CH], F32))
        ps_s = [bank(f"ps_s{i}") for i in range(2)]
        ps_t = [bank(f"ps_t{i}") for i in range(2)]
        ps_q = [bank(f"ps_q{i}") for i in range(2)]
        ps_y = [bank(f"ps_y{i}") for i in range(2)]

        loaded = sem("e_loaded")
        half_set = sem("e_half_set")
        s_done = sem("e_s_done")
        s_used = sem("e_s_used")
        x1_ready = sem("e_x1_ready")
        x1_stored = sem("e_x1_stored")
        stats_done = sem("e_stats_done")
        aggr_done = sem("e_aggr_done")
        var_ready = sem("e_var_ready")
        rstd_ready = sem("e_rstd_ready")
        xn_ready = sem("e_xn_ready")
        t_done = sem("e_t_done")
        xnT_ready = sem("e_xnT_ready")
        tok_done = sem("e_tok_done")
        tok_ready = sem("e_tok_ready")
        tok_stored = sem("e_tok_stored")
        qk_done = sem("e_qk_done")
        raw_ready = sem("e_raw_ready")
        swap_ready = sem("e_swap_ready")
        rot_step = sem("e_rot_step")
        turn_ready = sem("e_turn_ready")
        high_ready = sem("e_high_ready")
        low_ready = sem("e_low_ready")
        parts_stored = sem("e_parts_stored")
        soft_step = sem("e_soft_step")
        expo_ready = sem("e_expo_ready")
        wT_done = sem("e_wT_done")
        wT_ready = sem("e_wT_ready")
        y_done = sem("e_y_done")
        gate_ready = sem("e_gate_ready")
        gate_stored = sem("e_gate_stored")
        ticks = sem("e_ticks")
        SOFT = 7

        def tokens(name, width):
            return dram[name].rearrange("(c t p) d -> c p t d", t=TT, p=P)

        block = ctx.enter_context(nc.Block())

        @block.sync
        def _(sp):
            def load(c):
                sp.dma_start(o_in[:], dram["o0T"][:, :, ds(c * CH, CH)].rearrange("m p t -> p m t")).then_inc(loaded, 16)
                sp.dma_start(g_in[:], tokens("g", D)[ds(c, 1)].rearrange("a p t d -> p (a t) d")).then_inc(loaded, 16)
                sp.dma_start(x_in[:], tokens("x", D)[ds(c, 1)].rearrange("a p t d -> p (a t) d")).then_inc(loaded, 16)

            def store_x1(c):
                sp.wait_ge(x1_ready, TT * (c + 1))
                sp.dma_start(tokens("x1", D)[ds(c, 1)].rearrange("a p t d -> p (a t) d"), x1[:]).then_inc(x1_stored, 16)

            def store_rest(c):
                sp.wait_ge(tok_ready, TT * (c + 1))
                sp.dma_start(tokens("v1", KV1D)[ds(c, 1)].rearrange("a p t d -> p (a t) d"), tok[:, :, 0:KV1D]).then_inc(tok_stored, 16)
                sp.wait_ge(low_ready, NQK * (c + 2))
                for n, part in enumerate((high, low)):
                    sp.dma_start(dram["qk1"][n, :, :, ds(c * CH, CH)].rearrange("n p t -> p n t"), part[:].bitcast(F32)).then_inc(parts_stored, 16)
                sp.wait_ge(gate_ready, TT * (c + 2))
                sp.dma_start(tokens("g1", OL)[ds(c, 1)].rearrange("a p t d -> p (a t) d"), gate[:]).then_inc(gate_stored, 16)

            load(0)
            store_x1(0)
            load(1)
            with sp.Fori(0, NCH - 2) as c:
                store_x1(c + 1)
                load(c + 2)
                store_rest(c)
            store_x1(NCH - 1)
            store_rest(NCH - 2)
            store_rest(NCH - 1)
            sp.wait_ge(x1_stored, 16 * (NCH + 1))
            sp.wait_ge(tok_stored, 16 * (NCH + 1))
            sp.wait_ge(parts_stored, 32 * (NCH + 1))
            sp.wait_ge(gate_stored, 16 * (NCH + 1))

        @block.tensor
        def _(pe):
            def project(c):
                pe.wait_ge(loaded, 48 * (c + 1))
                for t in range(TT):
                    pe.wait_ge(s_used, TT * c + t + 1)
                    for m in range(MQ):
                        last = pe.matmul(ps_s[t % 2][:], o_in[:, m, t * P:(t + 1) * P], oT[:, m, :], start=(m == 0), stop=(m == MQ - 1))
                    last.then_inc(s_done, 1)

            def rest(c):
                pe.wait_ge(xn_ready, c + 1)
                for k in range(KD):
                    if k == 0:
                        pe.wait_ge(wT_ready, c + 1)
                    pe.wait_ge(xnT_ready, KD * c + max(k - 1, 0) + 2)
                    for t in range(TT):
                        last = pe.transpose(ps_t[k % 2][:, t * P:(t + 1) * P], xn[:, t, k * P:(k + 1) * P], ident[:])
                    last.then_inc(t_done, 1)
                pe.wait_ge(xnT_ready, KD * (c + 1) + 2)
                pe.wait_ge(gate_ready, TT * (c + 1))
                for t in range(TT):
                    if t >= 2:
                        pe.wait_ge(tok_ready, TT * c + t - 1)
                    for k in range(KD):
                        last = pe.matmul(ps_y[t % 2][:, 0:TOK], xnT[:, k, t * P:(t + 1) * P], tokT[:, k, :],
                                         start=(k == 0), stop=(k == KD - 1))
                    last.then_inc(tok_done, 1)
                for i in range(NQK):
                    pe.wait_ge(raw_ready, NQK * c + max(i - 1, 0) + 2)
                    for k in range(KD):
                        last = pe.matmul(ps_q[i % 2][:], qkT[:, i, k, :], xnT[:, k, :], start=(k == 0), stop=(k == KD - 1))
                    last.then_inc(qk_done, 1)
                pe.wait_ge(soft_step, SOFT * (c + 1))
                for t in range(TT):
                    last = pe.transpose(ps_t[0][:, t * P:(t + 1) * P], weighted[:, t, :], ident[:])
                last.then_inc(wT_done, 1)
                pe.wait_ge(wT_ready, c + 2)
                pe.wait_ge(tok_ready, TT * (c + 1))
                for t in range(TT):
                    if t >= 2:
                        pe.wait_ge(gate_ready, TT * (c + 1) + t - 1)
                    pe.matmul(ps_y[t % 2][:], weightedT[:, t * P:(t + 1) * P], bT[:], start=True, stop=True).then_inc(y_done, 1)

            project(0)
            with pe.Fori(0, NCH - 1) as c:
                project(c + 1)
                rest(c)
            rest(NCH - 1)

        @block.scalar
        def _(act):
            primed(act, xnT_ready, 2)
            primed(act, wT_ready, 1)
            primed(act, raw_ready, 2)
            primed(act, gate_ready, TT)

            def rest(c):
                for k in range(KD):
                    act.wait_ge(t_done, KD * c + k + 1)
                    act.activation(xnT[:, k, :], ps_t[k % 2][:], ACT.Copy).then_inc(xnT_ready, 1)
                act.wait_ge(tok_stored, 16 * (c + 1))
                for t in range(TT):
                    act.wait_ge(tok_done, TT * c + t + 1)
                    act.activation(tok[:, t, :], ps_y[t % 2][:, 0:TOK], ACT.Copy).then_inc(tok_ready, 1)

                def highs(i):
                    act.wait_ge(turn_ready, NQK * c + i + 1)
                    act.activation(high[:, i, :], turn[:, i, :], ACT.Copy).then_inc(high_ready, 1)

                for i in range(NQK):
                    act.wait_ge(qk_done, NQK * c + i + 1)
                    act.activation(raw[:, i, :], ps_q[i % 2][:], ACT.Copy).then_inc(raw_ready, 1)
                    if i == 0:
                        act.wait_ge(soft_step, SOFT * c + 3)
                        act.activation(expo[:], logits[:], ACT.Exp).then_inc(expo_ready, 1)
                    if i == 2:
                        act.wait_ge(parts_stored, 32 * (c + 1))
                    if i >= 2:
                        highs(i - 2)
                highs(NQK - 2)
                act.wait_ge(wT_done, c + 1)
                act.activation(weightedT[:], ps_t[0][:], ACT.Copy).then_inc(wT_ready, 1)
                highs(NQK - 1)
                act.wait_ge(gate_stored, 16 * (c + 1))
                for t in range(TT):
                    act.wait_ge(y_done, TT * c + t + 1)
                    act.activation(gate[:, t, :], ps_y[t % 2][:], ACT.Silu).then_inc(gate_ready, 1)

            with act.Fori(0, NCH) as c:
                rest(c)

        @block.gpsimd
        def _(pool):
            primed(pool, x1_stored, 16)
            primed(pool, tok_stored, 16)
            primed(pool, parts_stored, 32)
            primed(pool, gate_stored, 16)
            pool.memset(half[:], -0.5).then_inc(half_set, 1)
            pool.wait_ge(half_set, 1)
            pool.wait_ge(tables, 16 * (2 * B + 1))

            def power(c):
                pool.wait_ge(var_ready, c + 1)
                pool.tensor_tensor(rstd[:], var[:], half[:], ALU.pow).then_inc(rstd_ready, 1)

            def rotate(c):
                flat = [t[:].rearrange("p b s -> p (b s)") for t in (cos, sin)]
                for i in range(NQK):
                    wait_apart(pool, raw_ready, NQK * c + i + 3, ticks)
                    wait_apart(pool, high_ready, NQK * c + i + 1, ticks)
                    wait_apart(pool, low_ready, NQK * c + i + 1, ticks)
                    pool.tensor_tensor(turn[:, i, :], raw[:, i, :], flat[0][:, ds(c * CH, CH)], ALU.mult)
                    wait_apart(pool, swap_ready, NQK * c + i + 1, ticks)
                    pool.tensor_tensor(swapped[:, i, :], swapped[:, i, :], flat[1][:, ds(c * CH, CH)], ALU.mult)\
                        .then_inc(rot_step, 1)

            power(0)
            with pool.Fori(0, NCH - 1) as c:
                rotate(c)
                power(c + 1)
            rotate(NCH - 1)

        @block.vector
        def _(dve):
            primed(dve, s_used, 2)
            primed(dve, high_ready, NQK)
            primed(dve, low_ready, NQK)
            SWAP = [p ^ (HD1 // 2) for p in range(32)]
            dve.wait_ge(tables, 16 * (2 * B + 1))

            def add(c):
                dve.wait_ge(x1_stored, 16 * (c + 1))
                if not isinstance(c, int):
                    dve.wait_ge(xn_ready, c)
                for t in range(TT):
                    dve.wait_ge(s_done, TT * c + t + 1)
                    dve.tensor_tensor(x1[:, t, :], ps_s[t % 2][:], g_in[:, t, :], ALU.mult).then_inc(s_used, 1)
                    dve.wait_ge(s_used, TT * c + t + 3)
                    dve.tensor_tensor(x1[:, t, :], x1[:, t, :], x_in[:, t, :], ALU.add).then_inc(x1_ready, 1)

            def norm(c):
                for t in range(TT):
                    dve.wait_ge(x1_ready, TT * c + t + 1)
                    dve.bn_stats(stats[:, t, :], x1[:, t, :]).then_inc(stats_done, 1)
                for t in range(TT):
                    wait_apart(dve, stats_done, c * TT + t + 1, ticks)
                    dve.bn_aggr(mv[:, t, :], stats[:, t, :]).then_inc(aggr_done, 1)
                dve.wait_ge(aggr_done, (c + 1) * TT)
                dve.tensor_scalar(var[:], mv[:, :, 1], EPS, None, ALU.add).then_inc(var_ready, 1)
                dve.wait_ge(rstd_ready, c + 1)
                for t in range(TT):
                    last = dve.tensor_scalar(xn[:, t, :], x1[:, t, :], mv[:, t, 0:1], rstd[:, t:t + 1],
                                             ALU.subtract, ALU.mult)
                last.then_inc(xn_ready, 1)

            def route(c):
                dve.wait_ge(tok_ready, TT * (c + 1))
                for t in range(TT):
                    last = dve.tensor_tensor(logits[:, t, :], tok[:, t, LOG:], br[:], ALU.add)
                last.then_inc(soft_step, 1)
                dve.wait_ge(soft_step, SOFT * c + 1)
                dve.tensor_reduce(top[:], logits[:], AX.X, ALU.max).then_inc(soft_step, 1)
                dve.wait_ge(soft_step, SOFT * c + 2)
                dve.tensor_tensor(logits[:], logits[:], top[:].rearrange("p (t o) -> p t o", o=1).to_broadcast((P, TT, HL)),
                                  ALU.subtract).then_inc(soft_step, 1)
                dve.wait_ge(expo_ready, c + 1)
                dve.tensor_reduce(total[:], expo[:], AX.X, ALU.add).then_inc(soft_step, 1)
                dve.wait_ge(soft_step, SOFT * c + 4)
                dve.reciprocal(inverse[:], total[:]).then_inc(soft_step, 1)
                dve.wait_ge(soft_step, SOFT * c + 5)
                dve.tensor_tensor(share[:], expo[:], inverse[:].rearrange("p (t o) -> p t o", o=1).to_broadcast((P, TT, HL)),
                                  ALU.mult).then_inc(soft_step, 1)
                dve.wait_ge(soft_step, SOFT * c + 6)
                for t in range(TT):
                    last = dve.scalar_tensor_tensor(weighted[:, t, :].rearrange("p (h r) -> p h r", r=RL),
                                                    tok[:, t, LOW:LOG].rearrange("p (h r) -> p h r", r=RL), GAIN,
                                                    share[:, t, :].rearrange("p (h o) -> p h o", o=1).to_broadcast((P, HL, RL)),
                                                    ALU.mult, ALU.mult)
                last.then_inc(soft_step, 1)

            def rotate(c):
                def swap(i):
                    wait_apart(dve, raw_ready, NQK * c + i + 3, ticks)
                    dve.stream_shuffle(swapped[:, i, :], raw[:, i, :], SWAP).then_inc(swap_ready, 1)

                def combine(i):
                    dve.wait_ge(rot_step, NQK * c + i + 1)
                    dve.tensor_tensor(turn[:, i, :], turn[:, i, :], swapped[:, i, :], ALU.add).then_inc(turn_ready, 1)

                def split(i):
                    dve.wait_ge(high_ready, NQK * (c + 1) + i + 1)
                    dve.tensor_tensor(low[:, i, :], turn[:, i, :], high[:, i, :].bitcast(F32), ALU.subtract).then_inc(low_ready, 1)

                for i in range(NQK + 2):
                    if i < NQK:
                        swap(i)
                    if 1 <= i <= NQK:
                        combine(i - 1)
                    if i >= 2:
                        split(i - 2)

            add(0)
            norm(0)
            with dve.Fori(0, NCH - 1) as c:
                add(c + 1)
                route(c)
                rotate(c)
                norm(c + 1)
            route(NCH - 1)
            rotate(NCH - 1)


def select_phase(nc, sem, dram, ident, ident_bf, mask_kq):
    with ExitStack() as ctx:
        def sb(name, shape, dt=F32):
            return ctx.enter_context(nc.sbuf_tensor(f"f_{name}", shape, dt))

        PAIRS = GRP // 2
        LATE = QT - 2
        GROUPS = B * KV1
        PARTS = 3 * HD1
        EXTRA = P // 2
        SENT = 3e38
        qa = [sb(f"qa{u}", [P, GRP, S], F32R) for u in range(B)]
        ka = [sb(f"ka{u}", [P, S], F32R) for u in range(B)]
        qs = [sb(f"qs{u}", [P, GRP, S], F32R) for u in range(B)]
        ks = [sb(f"ks{u}", [P, S], F32R) for u in range(B)]
        v_all = sb("v_all", [P, QT, B, KV1 * HD1])
        v = [sb(f"v{u}", [P, QT, 2 * HD1]) for u in range(B)]
        chunk_max = sb("chunk_max", [P, LATE, 2, NC])
        rest = [sb(f"rest{p}", [P, LATE, 2, NC]) for p in range(PAIRS)]
        top = [sb(f"top{p}", [P, QT, 2, 8]) for p in range(PAIRS)]
        penalty = [sb(f"penalty{p}", [P, QT, 2, EXTRA]) for p in range(PAIRS)]
        part = [sb(f"part{p}", [P, 2, LATE, CPT]) for p in range(PAIRS)]
        missed = [sb(f"missed{p}", [P, 2 * LATE]) for p in range(PAIRS)]
        diag = [[sb(f"diag{u}{p}", [P, 2 * LATE, P], BF16) for p in range(PAIRS)] for u in range(B)]
        probs = [sb(f"probs{i}", [P, GRP, CH]) for i in range(2)]
        o_rows = sb("o_rows", [P, CH])
        inverse = sb("inverse", [P, TT * GRP])
        o_out = [sb(f"o_out{i}", [P, TT, GRP * HD1]) for i in range(2)]
        may_miss = sb("may_miss", [P, 2 * LATE, MISS])
        part_chunk = sb("part_chunk", [P, CPT])
        mask_qk = sb("mask_qk", [P, P], BF16)
        mask_part = sb("mask_part", [P, P], BF16)
        ps_a = [ctx.enter_context(nc.psum_tensor(f"f_ps_a{i}", [P, S], F32)) for i in range(2)]
        ps_s = [ctx.enter_context(nc.psum_tensor(f"f_ps_s{i}", [P, CH], F32)) for i in range(2)]
        ps_o = ctx.enter_context(nc.psum_tensor("f_ps_o", [P, CH], F32))
        ps_t = ctx.enter_context(nc.psum_tensor("f_ps_t", [P, CH], F32))

        tables = sem("f_tables")
        zeroed = sem("f_zeroed")
        v_loaded = sem("f_v_loaded")
        a_loaded = [sem(f"f_a_loaded{u}") for u in range(B)]
        s_loaded = [sem(f"f_s_loaded{u}") for u in range(B)]
        a_done = sem("f_a_done")
        a_used = sem("f_a_used")
        top_done = sem("f_top_done")
        rest_done = sem("f_rest_done")
        pen_step = sem("f_pen_step")
        missed_ready = sem("f_missed_ready")
        diag_ready = sem("f_diag_ready")
        v_ready = sem("f_v_ready")
        tp_done = sem("f_tp_done")
        qs_ready = sem("f_qs_ready")
        s_done = sem("f_s_done")
        exp_ready = sem("f_exp_ready")
        pv_done = sem("f_pv_done")
        o_copied = sem("f_o_copied")
        to_done = sem("f_to_done")
        inverse_ready = sem("f_inverse_ready")
        o_ready = sem("f_o_ready")
        o_stored = [sem(f"f_o_stored{i}") for i in range(2)]
        ticks = sem("f_ticks")

        UNITS = GRP * QT
        PUNITS = 2 * QT
        KTILES = [(0, kt) for kt in range(QT // 2)] + [(1, kt) for kt in range(QT)]
        M = len(KTILES)
        N_S = M * GRP

        def unit(n):
            p, r = divmod(n, PUNITS)
            return p, r // 2, r % 2

        def columns(m):
            half, kt = KTILES[m]
            return max(half * CH, kt * P), (half + 1) * CH

        steps = []
        for m in range(M):
            steps += [("s", m, 0), ("s", m, 1)]
            if m > 0:
                steps.append(("pv", m - 1))
            steps += [("s", m, 2), ("s", m, 3)]
            if m == 6:
                steps.append(("turn", 0))
        steps.append(("pv", M - 1))
        FIRST, LAST = 3, 27

        def second(n):
            count = LAST - FIRST + 1
            at = [0] * FIRST + [len(steps) * k // count for k in range(count)] + [len(steps)] * (UNITS - LAST)
            return steps[at[n]:at[n + 1]] if n + 1 < len(at) else []

        block = ctx.enter_context(nc.Block())

        @block.sync
        def _(sp):
            sp.dma_start(mask_qk[:], dram["mask_qk"]).then_inc(tables, 16)
            sp.dma_start(mask_part[:], dram["mask_part"]).then_inc(tables, 16)
            sp.dma_start(part_chunk[:], dram["part_chunk"]).then_inc(tables, 16)
            sp.dma_start(may_miss[:], dram["may_miss"].rearrange("p q h k -> p (q h) k")).then_inc(tables, 16)
            for u in range(B):
                sp.dma_start(v_all[:, :, u, :], dram["v1"][u * S:(u + 1) * S, :].rearrange("(n p) c -> p n c", p=P)).then_inc(v_loaded, 16)

            def store(i, j, u, half):
                sp.wait_ge(o_ready, 2 * i + half + 3)
                sp.dma_start(dram["o1"][u * S + half * CH:u * S + (half + 1) * CH, ds(j * GRP * HD1, GRP * HD1)].rearrange("(t p) c -> p t c", p=P),
                             o_out[half][:]).then_inc(o_stored[half], 16)

            with sp.Fori(0, KV1) as j:
                for u in range(B):
                    for half in range(2):
                        store(2 * j + u, j, u, half)
            for half in range(2):
                sp.wait_ge(o_stored[half], 16 * (GROUPS + 1))

        @block.tensor
        def _(pe):
            primed(pe, s_done, 1)
            primed(pe, to_done, 1)

            def choose(g, j, u, n):
                p, qt, h = unit(n)
                if n == 0:
                    pe.wait_ge(a_loaded[u], 96 * (j + 1))
                pe.wait_ge(a_used, UNITS * g + n + 1)
                out, end = ps_a[n % 2], (qt + 1) * P
                for lo in range(0, end, CH):
                    hi = min(end, lo + CH)
                    pe.matmul(out[:, lo:hi], qa[u][:, 2 * p + h, qt * P:end], ka[u][:, lo:hi], start=True, stop=(hi < end))
                pe.matmul(out[:, qt * P:end], ident_bf[:], mask_qk[:], start=False, stop=True).then_inc(a_done, 1)

            def penalties(g, p, half):
                pe.wait_ge(pen_step, 4 * (2 * g + p) + 2)
                pe.wait_ge(qs_ready, 4 * g + 2 * p + half + 1)
                pe.wait_ge(o_ready, 2 * g + 1 + p)
                for t in range(TT):
                    last = pe.transpose(ps_t[:, t * P:(t + 1) * P], penalty[p][:, half * TT + t, :, :].rearrange("p h k -> p (h k)"), ident[:])
                last.then_inc(tp_done, 1)

            def scores(i, j, u, m, h):
                n, (half, kt) = m * GRP + h, KTILES[m]
                lo, hi = columns(m)
                if n == 0:
                    pe.wait_ge(s_loaded[u], 96 * (j + 1) + 16)
                    pe.wait_ge(qs_ready, 4 * i + 5)
                if n == GRP:
                    pe.wait_ge(diag_ready, 2 * (i + 1))
                pe.wait_ge(exp_ready, N_S * i + n + 1)
                out, q0 = ps_s[n % 2], half * CH
                masked, parted = kt * P >= q0, kt >= 1 and q0 <= (kt + 1) * P < hi
                last = pe.matmul(out[:, lo - q0:], ks[u][:, kt * P:(kt + 1) * P], qs[u][:, h, lo:hi],
                                 start=True, stop=not (masked or parted))
                if masked:
                    last = pe.matmul(out[:, lo - q0:lo - q0 + P], ident_bf[:], mask_kq[:], start=False, stop=not parted)
                if parted:
                    at = (kt + 1) * P - q0
                    last = pe.matmul(out[:, at:at + P], mask_part[:], diag[u][h // 2][:, (h % 2) * LATE + kt - 1, :], start=False, stop=True)
                last.then_inc(s_done, 1)

            def values(i, u, m):
                half, kt = KTILES[m]
                lo, hi = columns(m)
                if m == 0:
                    pe.wait_ge(v_ready, i + 1)
                if kt == 0:
                    pe.wait_ge(o_copied, 2 * i + half + 1)
                pe.wait_ge(exp_ready, N_S * i + (m + 1) * GRP + 2)
                for h in range(GRP):
                    last = pe.matmul(ps_o[2 * HD1 * h:2 * HD1 * (h + 1), lo - half * CH:], v[u][:, kt, :],
                                     probs[m % 2][:, h, lo - half * CH:], start=(kt == 0), stop=((kt + 1) * P == hi))
                last.then_inc(pv_done, 1)

            def outputs(i, half, last_group):
                pe.wait_ge(o_copied, 2 * i + half + 2)
                pe.wait_ge(qs_ready, 4 * i + 5 if half == 0 or last_group else 4 * i + 7)
                pe.wait_ge(o_ready, 2 * i + half + 2)
                for t in range(TT):
                    last = pe.transpose(ps_t[:, t * P:(t + 1) * P], o_rows[:, t * P:(t + 1) * P], ident[:])
                last.then_inc(to_done, 1)

            def attend(i, j, u, todo, last_group):
                for what, *at in todo:
                    if what == "s":
                        scores(i, j, u, *at)
                    elif what == "pv":
                        values(i, u, *at)
                    else:
                        outputs(i, *at, last_group)

            def iteration(i, j, u, ja):
                for n in range(UNITS):
                    choose(i + 1, ja, 1 - u, n)
                    if n in (1, 2):
                        penalties(i, 1, n - 1)
                    if n in (22, 23):
                        penalties(i + 1, 0, n - 22)
                    attend(i, j, u, second(n), False)
                outputs(i, 1, False)

            pe.wait_ge(tables, 16 * 4)
            for n in range(UNITS):
                choose(0, 0, 0, n)
                if n in (22, 23):
                    penalties(0, 0, n - 22)
            with pe.Fori(0, KV1 - 1) as j:
                iteration(2 * j, j, 0, j)
                iteration(2 * j + 1, j, 1, j + 1)
            iteration(GROUPS - 2, KV1 - 1, 0, KV1 - 1)
            for half in range(2):
                penalties(GROUPS - 1, 1, half)
            attend(GROUPS - 1, KV1 - 1, 1, steps, True)
            outputs(GROUPS - 1, 1, True)

        @block.scalar
        def _(act):
            primed(act, qs_ready, 1)
            primed(act, exp_ready, 2)
            primed(act, o_copied, 1)

            def penalties(g, u, p, half):
                act.wait_ge(tp_done, 4 * g + 2 * p + half + 1)
                for h in range(2):
                    last = act.activation(qs[u][EXTRA:, 2 * p + h, half * CH:(half + 1) * CH], ps_t[h * EXTRA:(h + 1) * EXTRA, :], ACT.Copy)
                last.then_inc(qs_ready, 1)

            def exponentials(i, m, h):
                n, (half, kt) = m * GRP + h, KTILES[m]
                at = columns(m)[0] - half * CH
                if h == 0:
                    act.wait_ge(pv_done, M * i + m + 1)
                act.wait_ge(s_done, N_S * i + n + 2)
                act.activation(probs[m % 2][:, h, at:], ps_s[n % 2][:, at:], ACT.Exp, scale=HD1 ** -0.5).then_inc(exp_ready, 1)

            def outputs(i, half):
                act.wait_ge(to_done, 2 * i + half + 1)
                act.wait_ge(pv_done, M * i + (QT // 2 if half == 0 else M) + 2)
                act.activation(o_rows[:], ps_o[:], ACT.Copy).then_inc(o_copied, 1)

            def attend(i, todo):
                for what, *at in todo:
                    if what == "s":
                        exponentials(i, *at)
                        if at == [QT // 2, GRP - 1]:
                            outputs(i, 0)

            def iteration(i, u):
                for n in range(UNITS):
                    if n in (1, 2):
                        penalties(i, u, 1, n - 1)
                    if n in (22, 23):
                        penalties(i + 1, 1 - u, 0, n - 22)
                    attend(i, second(n))
                outputs(i, 1)

            for half in range(2):
                penalties(0, 0, 0, half)
            with act.Fori(0, KV1 - 1) as j:
                for u in range(B):
                    iteration(2 * j + u, u)
            iteration(GROUPS - 2, 0)
            for half in range(2):
                penalties(GROUPS - 1, 1, 1, half)
            attend(GROUPS - 1, steps)
            outputs(GROUPS - 1, 1)

        @block.gpsimd
        def _(pool):
            primed(pool, pv_done, 2)
            for u in range(B):
                pool.memset(qa[u][:].bitcast(F32), 0.0)
                pool.memset(ka[u][:].bitcast(F32), 0.0)
                pool.memset(v[u][:, :, HD1:], 1.0)
            for p in range(PAIRS):
                pool.memset(rest[p][:], 0.0)
                pool.memset(penalty[p][:], 0.0)
            pool.memset(o_rows[:], 0.0).then_inc(zeroed, 1)
            pool.wait_ge(zeroed, 3)
            rows = dram["qk1"].rearrange("a n p t -> a (n p) t")
            k0 = H1 * HD1

            def load(j, u, q, k, loaded):
                for n, (qp, kp) in enumerate(((0, 0), (0, 1), (1, 0))):
                    to = slice(n * HD1, (n + 1) * HD1)
                    pool.dma_start(q[u][to, :, :],
                                   rows[qp, ds(j * GRP * HD1, GRP * HD1), u * S:(u + 1) * S].rearrange("(h c) t -> c h t", c=HD1)).then_inc(loaded[u], 16)
                    pool.dma_start(k[u][to, :], rows[kp, ds(k0 + j * HD1, HD1), u * S:(u + 1) * S]).then_inc(loaded[u], 16)

            def reload_choose(j, u):
                wait_apart(pool, a_done, UNITS * (2 * j + u + 1), ticks)
                load(j + 1, u, qa, ka, a_loaded)

            def reload_attend(j, u):
                wait_apart(pool, s_done, N_S * (2 * j + u + 1) + 1, ticks)
                load(j + 1, u, qs, ks, s_loaded)

            for u in range(B):
                load(0, u, qa, ka, a_loaded)
                load(0, u, qs, ks, s_loaded)
                pool.dma_start(ks[u][EXTRA:, :], dram["chunk_of"]).then_inc(s_loaded[u], 16)
            pool.wait_ge(v_loaded, 16 * B)

            def prepare(g, j, u, first):
                if not first:
                    wait_apart(pool, pv_done, M * (g - 1) + 2, ticks)
                pool.tensor_copy(v[u][:, :, 0:HD1], v_all[:, :, u, ds(j * HD1, HD1)]).then_inc(v_ready, 1)
                if not first:
                    wait_apart(pool, s_done, N_S * (g - 1) + 1, ticks)
                for p in range(PAIRS):
                    pool.wait_ge(missed_ready, 2 * g + p + 1)
                    pool.tensor_tensor(diag[u][p][:], ident[:].rearrange("p (o n) -> p o n", o=1).to_broadcast((P, 2 * LATE, P)),
                                       missed[p][:].rearrange("p (n o) -> p n o", o=1).to_broadcast((P, 2 * LATE, P)), ALU.mult)\
                        .then_inc(diag_ready, 1)

            prepare(0, 0, 0, True)
            with pool.Fori(0, KV1 - 1) as j:
                reload_choose(j, 0)
                prepare(2 * j + 1, j, 1, False)
                reload_attend(j, 0)
                reload_choose(j, 1)
                prepare(2 * j + 2, j + 1, 0, False)
                reload_attend(j, 1)
            prepare(GROUPS - 1, KV1 - 1, 1, False)

        @block.vector
        def _(dve):
            primed(dve, a_used, 2)
            primed(dve, o_ready, 2)
            for half in range(2):
                primed(dve, o_stored[half], 16)
            dve.memset(qs[0][32:64, :, :].bitcast(F32), 0.0)
            dve.memset(ks[0][32:64, :].bitcast(F32), 0.0).then_inc(zeroed, 1)
            dve.memset(qs[1][32:64, :, :].bitcast(F32), 0.0)
            dve.memset(ks[1][32:64, :].bitcast(F32), 0.0).then_inc(zeroed, 1)
            dve.wait_ge(tables, 16 * 4)
            dve.wait_ge(zeroed, 3)

            def reduce(g, n):
                p, qt, h = unit(n)
                dve.wait_ge(a_done, UNITS * g + n + 1)
                src = ps_a[n % 2][:, 0:(qt + 1) * P]
                if qt < 2:
                    dve.tensor_reduce(top[p][:, qt, h, 0:1], src, AX.X, ALU.max).then_inc(a_used, 1)
                else:
                    dve.tensor_reduce(chunk_max[:, qt - 2, h, 0:(qt + 1) * CPT], src.rearrange("p (c k) -> p c k", k=CHUNK),
                                      AX.X, ALU.max).then_inc(a_used, 1)

            def choose(g, q):
                tiles = [unit(n) for n in range(4 * q, 4 * q + 4)]
                for n in range(4 * q, 4 * q + 4):
                    reduce(g, n)
                if tiles[0][1] < 2:
                    return
                late = 12 * (q // 4) + 4 * (q % 4 - 1)
                wait_apart(dve, a_used, UNITS * g + 4 * q + 6, ticks)
                for p, qt, h in tiles:
                    dve.max(top[p][:, qt, h, :], chunk_max[:, qt - 2, h, 0:(qt + 1) * CPT]).then_inc(top_done, 1)
                wait_apart(dve, top_done, 2 * 2 * LATE * g + late + 4, ticks)
                for p, qt, h in tiles:
                    n = (qt + 1) * CPT
                    dve.match_replace(rest[p][:, qt - 2, h, 0:n], top[p][:, qt, h, :], chunk_max[:, qt - 2, h, 0:n], SENT).then_inc(rest_done, 1)

            def penalise(g, p, first):
                if not first:
                    dve.wait_ge(tp_done, 4 * (g - 1) + 2 * p + 2)
                dve.wait_ge(rest_done, 2 * 2 * LATE * g + 2 * LATE * (p + 1))
                dve.tensor_scalar(penalty[p][:, :, :, MISS:MISS + 1].rearrange("p q h o -> p (q h) o"),
                                  top[p][:, :, :, 0:1].rearrange("p q h o -> p (q h) o"), -1.0, None, ALU.mult).then_inc(pen_step, 1)
                dve.scalar_tensor_tensor(penalty[p][:, 2:, :, 0:MISS].rearrange("p q h k -> p (q h) k"),
                                         rest[p][:, :, :, CPT:CPT + MISS].rearrange("p q h k -> p (q h) k"), SENT, may_miss[:],
                                         ALU.not_equal, ALU.mult).then_inc(pen_step, 1)
                for h in range(2):
                    flat = rest[p][:].rearrange("p q h k -> p (q h k)")
                    dve.scalar_tensor_tensor(part[p][:, h, :, :], diagonal(flat, h), SENT,
                                             part_chunk[:].rearrange("p (o k) -> p o k", o=1).to_broadcast((P, LATE, CPT)),
                                             ALU.not_equal, ALU.mult).then_inc(pen_step, 1)
                if not first:
                    dve.wait_ge(diag_ready, 2 * (g - 1) + p + 1)
                dve.wait_ge(pen_step, 4 * (2 * g + p + 1))
                dve.tensor_reduce(missed[p][:], part[p][:].rearrange("p h q k -> p (h q) k"), AX.X, ALU.add).then_inc(missed_ready, 1)

            def diagonal(flat, h):
                start, pitch = h * NC + CPT, 2 * NC + CPT
                return bass.AP(tensor=flat.tensor, offset=flat.offset + start, ap=[list(flat.ap[0]), [pitch, LATE], [1, CPT]])

            def outputs(i, half):
                src = ps_t[:].rearrange("p (n c) -> p n c", c=2 * HD1)
                dve.wait_ge(to_done, 2 * i + half + 2)
                dve.reciprocal(inverse[:].rearrange("p (n o) -> p n o", o=1), src[:, :, HD1:HD1 + 1]).then_inc(inverse_ready, 1)
                dve.wait_ge(o_stored[half], 16 * (i + 1))
                dve.wait_ge(inverse_ready, 2 * i + half + 1)
                dve.tensor_tensor(o_out[half][:].rearrange("p t (h c) -> p (t h) c", c=HD1), src[:, :, 0:HD1],
                                  inverse[:].rearrange("p (n o) -> p n o", o=1).to_broadcast((P, TT * GRP, HD1)), ALU.mult).then_inc(o_ready, 1)

            def stage(g, i, first):
                for q in range(UNITS // 4):
                    choose(g, q)
                    if q % 4 == 3:
                        penalise(g, q // 4, first)
                    if q == 4 and not first:
                        outputs(i, 0)
                if not first:
                    outputs(i, 1)

            stage(0, None, True)
            with dve.Fori(0, KV1 - 1) as j:
                for u in range(B):
                    stage(2 * j + u + 1, 2 * j + u, False)
            stage(GROUPS - 1, GROUPS - 2, False)
            for half in range(2):
                outputs(GROUPS - 1, half)


def finish_phase(nc, sem, dram, ident, out):
    with ExitStack() as ctx:
        def sb(name, shape, dt=F32):
            return ctx.enter_context(nc.sbuf_tensor(f"h_{name}", shape, dt))

        KO = H1 * HD1 // P
        w_rows = sb("w_rows", [P, D // P, KO * P])
        wT = sb("wT", [P, KO, D])
        o_in = [sb(f"o_in{i}", [P, TT, KO * P]) for i in range(2)]
        g_in = [sb(f"g_in{i}", [P, TT, D]) for i in range(2)]
        x_in = [sb(f"x_in{i}", [P, TT, D]) for i in range(2)]
        oT = [sb(f"oT{i}", [P, KO, CH]) for i in range(2)]
        y = [sb(f"y{i}", [P, TT, D]) for i in range(2)]
        ps_t = [ctx.enter_context(nc.psum_tensor(f"h_ps_t{i}", [P, CH], F32)) for i in range(4)]
        ps_y = [ctx.enter_context(nc.psum_tensor(f"h_ps_y{i}", [P, CH], F32)) for i in range(2)]

        w_loaded = sem("h_w_loaded")
        w_turned = sem("h_w_turned")
        w_ready = sem("h_w_ready")
        loaded = [sem(f"h_loaded{i}") for i in range(2)]
        t_done = sem("h_t_done")
        t_ready = sem("h_t_ready")
        y_done = sem("h_y_done")
        gated = sem("h_gated")
        y_ready = sem("h_y_ready")
        stored = [sem(f"h_stored{i}") for i in range(2)]
        block = ctx.enter_context(nc.Block())

        def tokens(ap):
            return ap.rearrange("(c t p) d -> c p t d", t=TT, p=P)

        @block.sync
        def _(sp):
            sp.dma_start(w_rows[:], dram["wo"].rearrange("(o p) c -> p o c", p=P)).then_inc(w_loaded, 16)

            def load(c, u):
                for to, name in ((o_in, "o1"), (g_in, "g1"), (x_in, "x1")):
                    sp.dma_start(to[u][:], tokens(dram[name])[ds(c, 1)].rearrange("a p t d -> p (a t) d")).then_inc(loaded[u], 16)

            def store(c, u):
                sp.wait_ge(y_ready, TT * (c + 1))
                sp.dma_start(tokens(out)[ds(c, 1)].rearrange("a p t d -> p (a t) d"), y[u][:]).then_inc(stored[u], 16)

            for u in range(2):
                load(u, u)
            with sp.Fori(0, NCH // 2 - 1) as i:
                for u in range(2):
                    store(2 * i + u, u)
                    load(2 * i + 2 + u, u)
            for u in range(2):
                store(NCH - 2 + u, u)
            for u in range(2):
                sp.wait_ge(stored[u], 16 * (NCH // 2 + 1))

        @block.tensor
        def _(pe):
            primed(pe, y_done, 2 * TT)
            pe.wait_ge(w_loaded, 16)
            for k in range(KO):
                for o in range(D // P):
                    last = pe.transpose(ps_t[k % 4][:, o * P:(o + 1) * P], w_rows[:, o, k * P:(k + 1) * P], ident[:])
                last.then_inc(w_turned, 1)

            def turn(i, u):
                pe.wait_ge(loaded[u], 48 * (i + 1))
                for k in range(KO):
                    if k == 0:
                        pe.wait_ge(w_ready, KO)
                    pe.wait_ge(t_ready, KO * (2 * i + u) + k + 1)
                    for t in range(TT):
                        last = pe.transpose(ps_t[k][:, t * P:(t + 1) * P], o_in[u][:, t, k * P:(k + 1) * P], ident[:])
                    last.then_inc(t_done, 1)

            def project(i, u):
                c = 2 * i + u
                pe.wait_ge(t_ready, KO * (c + 2))
                for t in range(TT):
                    pe.wait_ge(gated, TT * c + t + 1)
                    for k in range(KO):
                        last = pe.matmul(ps_y[t % 2][:], oT[u][:, k, t * P:(t + 1) * P], wT[:, k, :], start=(k == 0), stop=(k == KO - 1))
                    last.then_inc(y_done, 1)

            turn(0, 0)
            with pe.Fori(0, NCH // 2 - 1) as i:
                turn(i, 1)
                project(i, 0)
                turn(i + 1, 0)
                project(i, 1)
            turn(NCH // 2 - 1, 1)
            project(NCH // 2 - 1, 0)
            project(NCH // 2 - 1, 1)

        @block.scalar
        def _(act):
            primed(act, t_ready, KO)
            for k in range(KO):
                act.wait_ge(w_turned, k + 1)
                act.activation(wT[:, k, :], ps_t[k % 4][:], ACT.Copy).then_inc(w_ready, 1)
            with act.Fori(0, NCH // 2) as i:
                for u in range(2):
                    c = 2 * i + u
                    act.wait_ge(y_done, TT * (c + 1))
                    for k in range(KO):
                        act.wait_ge(t_done, KO * c + k + 1)
                        act.activation(oT[u][:, k, :], ps_t[k][:], ACT.Copy).then_inc(t_ready, 1)

        @block.gpsimd
        def _(pool):
            primed(pool, gated, 2)

        @block.vector
        def _(dve):
            for u in range(2):
                primed(dve, stored[u], 16)
            with dve.Fori(0, NCH // 2) as i:
                for u in range(2):
                    c = 2 * i + u
                    dve.wait_ge(loaded[u], 48 * (i + 1))
                    dve.wait_ge(stored[u], 16 * (i + 1))
                    for t in range(TT):
                        dve.wait_ge(y_done, TT * (c + 2) + t + 1)
                        dve.tensor_tensor(y[u][:, t, :], ps_y[t % 2][:], g_in[u][:, t, :], ALU.mult).then_inc(gated, 1)
                        dve.wait_ge(gated, TT * c + t + 3)
                        dve.tensor_tensor(y[u][:, t, :], y[u][:, t, :], x_in[u][:, t, :], ALU.add).then_inc(y_ready, 1)


def program(nc, dram, out):
    def scratch(name, shape, dt=F32):
        dram[name] = nc.dram_tensor(name, shape, dt, kind="Internal").ap()

    scratch("xnT", (KD, P, T))
    scratch("g", (T, D))
    scratch("v", (T, KVD))
    scratch("k_mean", (P, T))
    scratch("k_raw", (MK, P, T))
    scratch("k_high", (KV0, P, T), FP16)
    scratch("k_low", (KV0, P, T), FP16)
    scratch("q_parts", (H0, P, T), FP16)
    scratch("o0T", (MQ, P, T))
    scratch("x1", (T, D))
    scratch("v1", (T, KV1 * HD1))
    scratch("qk1", (2, (H1 + KV1) * HD1 // P, P, T))
    scratch("g1", (T, OL))
    scratch("o1", (T, H1 * HD1))
    with ExitStack() as ctx:
        def sem(name):
            return ctx.enter_context(nc.semaphore(name))

        def kept(name, shape, dt=F32):
            return ctx.enter_context(nc.sbuf_tensor(name, shape, dt))

        ident = kept("ident", [P, P])
        ident_bf = kept("ident_bf", [P, P], BF16)
        mask_kq = kept("mask_kq", [P, P], BF16)
        gate_phase(nc, sem, dram, ident)
        with ExitStack() as inner:
            conv_in = inner.enter_context(nc.sbuf_tensor("conv_in", [P, MQ, B, PAD + S], F32))
            project_phase(nc, sem, dram, ident, conv_in)
            query_phase(nc, sem, dram, ident, conv_in)
        attend_phase(nc, sem, dram, ident_bf, mask_kq)
        middle_phase(nc, sem, dram, ident)
        select_phase(nc, sem, dram, ident, ident_bf, mask_kq)
        finish_phase(nc, sem, dram, ident, out)


NAMES = {"x": "L0_attn_x", "w_qkv": "L0_attn_w_qkv", "w_o": "L0_attn_w_o", "qc1_w": "L0_attn_qc1_w",
         "qc1_b": "L0_attn_qc1_b", "qc2_w": "L0_attn_qc2_w", "qc2_b": "L0_attn_qc2_b", "kc1_w": "L0_attn_kc1_w",
         "kc1_b": "L0_attn_kc1_b", "kc2_w": "L0_attn_kc2_w", "kc2_b": "L0_attn_kc2_b", "key_temp": "L0_attn_key_temp",
         "gate_w": "L0_ffn_gate_w", "up_w": "L0_ffn_up_w", "down_w": "L0_ffn_down_w", "fc1_w": "L0_ffn_fc1_w",
         "fc2_w": "L0_ffn_fc2_w", "expert_w": "L0_ffn_expert_w", "ln_gamma": "L0_ffn_ln_gamma",
         "ln_beta": "L0_ffn_ln_beta", "wq": "L1_attn_wq", "wk": "L1_attn_wk", "wv": "L1_attn_wv", "wo": "L1_attn_wo",
         "lora_a": "L1_ffn_A", "lora_b": "L1_ffn_B", "lora_r": "L1_ffn_Wr", "lora_br": "L1_ffn_br"}


def constants():
    import numpy as np

    bf = mybir.dt.np(BF16)
    part, row = np.arange(P)[:, None], np.arange(P)[None, :]
    c = {"ident": np.eye(P, dtype=np.float32)}

    def angles(dim):
        inv = (1.0 / np.float32(10000.0) ** (np.arange(0, dim, 2, dtype=np.float32) / np.float32(dim))).astype(np.float32)
        return (np.arange(S, dtype=np.float32)[:, None] * inv[None, :]).astype(np.float32)

    a = angles(HD0)[:, (np.arange(P) % HD0) // 2].T
    c["cos0"] = np.cos(a).astype(np.float32)
    c["sin0"] = (np.sin(a) * np.where(np.arange(P) % 2 == 0, -1, 1)[:, None]).astype(np.float32)
    a = angles(HD1)[:, np.arange(P) % (HD1 // 2)].T
    c["cos1"] = np.cos(a).astype(np.float32)
    c["sin1"] = (np.sin(a) * np.where(np.arange(P) % HD1 < HD1 // 2, -1, 1)[:, None]).astype(np.float32)
    c["head2"] = (part // HD0 == np.arange(2)[None, :]).astype(np.float32)
    c["ident_bf"] = np.eye(P).astype(bf)
    c["mask_kq"] = np.where(part <= row, 0, -BIG).astype(bf)
    c["mask_qk"] = np.where(row <= part, 0, -BIG).astype(bf)
    c["mask_part"] = np.where((part // CHUNK == row // CHUNK) & (row <= part), -BIG, 0).astype(bf)
    chunk = np.arange(CPT, CPT + MISS)[:, None] == np.arange(S)[None, :] // CHUNK
    c["chunk_of"] = np.concatenate([chunk, np.ones((1, S)), np.zeros((P // 2 - MISS - 1, S))]).astype(np.float32)
    q = np.arange(P)[:, None, None, None] + P * np.arange(2, QT)[None, :, None, None]
    k = np.arange(CPT, CPT + MISS)[None, None, None, :]
    c["may_miss"] = np.where((k < (q - P) // CHUNK) & np.ones((1, 1, 2, 1), bool), -BIG, 0).astype(np.float32)
    c["part_chunk"] = (part // CHUNK == np.arange(CPT)[None, :]).astype(np.float32)
    return c


def kernel(**inputs):
    import concourse.bacc as bacc
    import numpy as np
    from concourse.bass_utils import run_bass_kernel_spmd as run

    nc = bacc.Bacc("TRN2", target_bir_lowering=False, num_devices=1)
    arrays = {short: np.ascontiguousarray(inputs[name]) for short, name in NAMES.items()}
    arrays["x"] = arrays["x"].reshape(T, D)
    arrays.update(constants())
    dram = {n: nc.dram_tensor(f"in_{n}", a.shape, mybir.dt.from_np(a.dtype), kind="ExternalInput").ap()
            for n, a in arrays.items()}
    out = nc.dram_tensor("out", (T, D), F32, kind="ExternalOutput").ap()
    program(nc, dram, out)
    results = run(nc, [{f"in_{n}": a for n, a in arrays.items()}], core_ids=[0]).results[0]
    return results["out"].reshape(inputs["L0_attn_x"].shape)
```

```python
from contextlib import ExitStack

import concourse.bass as bass
from concourse import mybir

F32 = mybir.dt.float32
F32R = mybir.dt.float32r
BF16 = mybir.dt.bfloat16
FP16 = mybir.dt.float16
ALU = mybir.AluOpType
ACT = mybir.ActivationFunctionType
AX = mybir.AxisListType

P = 128
B, S, D = 2, 1024, 512
T = B * S
CH = 512
NCH = T // CH
TT = CH // P
KD = D // P
EPS = 1e-5
FULL = 30000.0
BIG = 1e30

H0, KV0, HD0 = 16, 4, 64
LAT = H0 * HD0
KVD = KV0 * HD0
MQ, MK = LAT // P, KVD // P
TAPS = 3
PAD = TAPS - 1
INT, LATF, NE = 1024, 256, 8
MI, ML = INT // P, LATF // P
H1, KV1, HD1 = 32, 8, 16
GRP = H1 // KV1
CHUNK = 16
NC = S // CHUNK
QT = S // P
CPT = P // CHUNK
MISS = (S - 1 - P) // CHUNK - CPT
HL, RL, OL = 8, 16, 512
GAIN = 32.0 / RL * HL


def ds(start, size):
    return bass.ds(start, size)


def primed(engine, sem, value):
    engine.sem_inc(sem, value)


def wait_apart(engine, sem, value, ticks):
    engine.wait_ge(sem, value)
    engine.sem_inc(ticks, 1)


def gate_phase(nc, sem, dram, ident, half, weights):
    with ExitStack() as ctx:
        def sb(name, shape, dt=F32):
            return ctx.enter_context(nc.sbuf_tensor(f"a_{name}", shape, dt))

        def bank(name):
            return ctx.enter_context(nc.psum_tensor(f"a_{name}", [P, CH], F32))

        up = sb("up", [P, KD, INT])
        down = sb("down", [P, MI, D])
        fc1 = sb("fc1", [P, KD, LATF])
        fc2 = sb("fc2", [P, ML, D])
        expert = sb("expert", [P, ML, LATF])
        gate = sb("gate", [P, KD, NE])
        gamma = sb("gamma", [P, D])
        beta = sb("beta", [P, D])
        x_in = sb("x_in", [P, TT, D])
        xn = sb("xn", [P, TT, D])
        xnT = sb("xnT", [P, KD, CH])
        relu = sb("relu", [P, 2, CH])
        hidden = sb("hidden", [P, MI, CH])
        latent = sb("latent", [P, ML, CH])
        mixed = sb("mixed", [P, ML, CH])
        logits = sb("logits", [P, TT, NE])
        top = sb("top", [P, TT, NE])
        route = sb("route", [P, TT])
        y = sb("y", [P, TT, D])
        g_out = sb("g_out", [P, TT, D])
        stats = sb("stats", [P, TT, 6])
        mv = sb("mv", [P, TT, 2])
        var = sb("var", [P, TT])
        rstd = sb("rstd", [P, TT])
        stats2 = sb("stats2", [P, TT, 6])
        mv2 = sb("mv2", [P, TT, 2])
        var2 = sb("var2", [P, TT])
        rstd2 = sb("rstd2", [P, TT])
        ps_t = [bank(f"ps_t{i}") for i in range(2)]
        ps_m = [bank(f"ps_m{i}") for i in range(2)]
        ps_d = [bank(f"ps_d{i}") for i in range(2)]
        ps_r = [bank(f"ps_r{i}") for i in range(2)]

        x_loaded = sem("a_x_loaded")
        w_loaded = sem("a_w_loaded")
        w2_loaded = sem("a_w2_loaded")
        half_set = sem("a_half_set")
        stats_done = sem("a_stats_done")
        var_ready = sem("a_var_ready")
        rstd_ready = sem("a_rstd_ready")
        xn_ready = sem("a_xn_ready")
        t_done = sem("a_t_done")
        xnT_ready = sem("a_xnT_ready")
        xnT_stored = sem("a_xnT_stored")
        m_done = sem("a_m_done")
        m_free = sem("a_m_free")
        h_ready = sem("a_h_ready")
        top_done = sem("a_top_done")
        route_ready = sem("a_route_ready")
        out_done = sem("a_out_done")
        y_routed = sem("a_y_routed")
        y_ready = sem("a_y_ready")
        stats2_done = sem("a_stats2_done")
        var2_ready = sem("a_var2_ready")
        rstd2_ready = sem("a_rstd2_ready")
        yn_ready = sem("a_yn_ready")
        scaled = sem("a_scaled")
        shifted = sem("a_shifted")
        g_ready = sem("a_g_ready")
        g_stored = sem("a_g_stored")
        ticks = sem("ticks")

        UNITS = MI + ML + 1 + ML
        x_rows = dram["x"].rearrange("(c t p) d -> c p t d", t=TT, p=P)
        g_rows = dram["g"].rearrange("(c t p) d -> c p t d", t=TT, p=P)
        block = ctx.enter_context(nc.Block())

        @block.sync
        def _(sp):
            sp.dma_start(x_in[:], x_rows[0]).then_inc(x_loaded, 16)
            sp.dma_start(ident[:], dram["ident"]).then_inc(w_loaded, 16)
            sp.dma_start(up[:], dram["up_w"].rearrange("(k p) n -> p k n", p=P)).then_inc(w_loaded, 16)
            sp.dma_start(fc1[:], dram["fc1_w"].rearrange("(k p) n -> p k n", p=P)).then_inc(w_loaded, 16)
            sp.dma_start(gate[:], dram["gate_w"].rearrange("(k p) n -> p k n", p=P)).then_inc(w_loaded, 16)
            sp.dma_start(expert[:], dram["expert_w"].rearrange("(k p) n -> p k n", p=P)).then_inc(w_loaded, 16)
            sp.dma_start(down[:], dram["down_w"].rearrange("(k p) n -> p k n", p=P)).then_inc(w2_loaded, 16)
            sp.dma_start(fc2[:], dram["fc2_w"].rearrange("(k p) n -> p k n", p=P)).then_inc(w2_loaded, 16)
            sp.dma_start(gamma[:], dram["ln_gamma"].rearrange("(a n) -> a n", a=1).to_broadcast((P, D))).then_inc(w2_loaded, 16)
            sp.dma_start(beta[:], dram["ln_beta"].rearrange("(a n) -> a n", a=1).to_broadcast((P, D))).then_inc(w2_loaded, 16)

            weights.load(sp)
            sp.wait_ge(weights.zeroed, 1)
            weights.load_pairs(sp)

            def store(c):
                sp.wait_ge(xnT_ready, (c + 1) * KD)
                sp.dma_start(dram["xnT"][:, :, ds(c * CH, CH)].rearrange("k p n -> p k n"), xnT[:]).then_inc(xnT_stored, 16)

            with sp.Fori(0, NCH - 1) as c:
                sp.wait_ge(xn_ready, c + 1)
                sp.dma_start(x_in[:], x_rows[ds(c + 1, 1)].rearrange("a p t d -> p (a t) d")).then_inc(x_loaded, 16)
                store(c)
            store(NCH - 1)
            sp.wait_ge(xnT_stored, 16 * (NCH + 1))
            sp.wait_ge(g_stored, 16 * (NCH + 1))

        @block.tensor
        def _(pe):
            pe.wait_ge(w_loaded, 80)
            with pe.Fori(0, NCH) as c:
                pe.wait_ge(xn_ready, c + 1)
                for k in range(KD):
                    if k >= 2:
                        pe.wait_ge(xnT_ready, c * KD + k - 1)
                    for t in range(TT):
                        last = pe.transpose(ps_t[k % 2][:, t * P:(t + 1) * P], xn[:, t, k * P:(k + 1) * P], ident[:])
                    last.then_inc(t_done, 1)
                pe.wait_ge(xnT_ready, (c + 1) * KD)
                for u in range(UNITS):
                    out = ps_m[u % 2]
                    pe.wait_ge(m_free, c * UNITS + u + 1)
                    if u >= MI + ML + 1:
                        pe.wait_ge(m_free, c * UNITS + ML + 2)
                    if u < MI + ML:
                        w = fc1[:, :, u * P:(u + 1) * P] if u < ML else up[:, :, (u - ML) * P:(u - ML + 1) * P]
                        for k in range(KD):
                            last = pe.matmul(out[:], w[:, k, :], xnT[:, k, :], start=(k == 0), stop=(k == KD - 1))
                    elif u == MI + ML:
                        for t in range(TT):
                            for k in range(KD):
                                last = pe.matmul(out[:, t * NE:(t + 1) * NE], xnT[:, k, t * P:(t + 1) * P], gate[:, k, :],
                                                 start=(k == 0), stop=(k == KD - 1))
                    else:
                        m = u - MI - ML - 1
                        for k in range(ML):
                            last = pe.matmul(out[:], expert[:, k, m * P:(m + 1) * P], latent[:, k, :],
                                             start=(k == 0), stop=(k == ML - 1))
                    last.then_inc(m_done, 1)
                pe.wait_ge(w2_loaded, 64)
                pe.wait_ge(h_ready, (c + 1) * MI + 2)
                for t in range(TT):
                    pe.wait_ge(y_ready, c * TT + t + 1)
                    for k in range(MI):
                        last = pe.matmul(ps_d[t % 2][:], hidden[:, k, t * P:(t + 1) * P], down[:, k, :],
                                         start=(k == 0), stop=(k == MI - 1))
                    if t == 0:
                        pe.wait_ge(m_free, (c + 1) * UNITS + 2)
                    for k in range(ML):
                        last = pe.matmul(ps_r[t % 2][:], mixed[:, k, t * P:(t + 1) * P], fc2[:, k, :],
                                         start=(k == 0), stop=(k == ML - 1))
                    last.then_inc(out_done, 1)

        @block.scalar
        def _(act):
            primed(act, m_free, 2)
            primed(act, g_ready, TT)

            def transposed(c):
                act.wait_ge(xnT_stored, 16 * (c + 1))
                for k in range(KD):
                    act.wait_ge(t_done, c * KD + k + 1)
                    act.activation(xnT[:, k, :], ps_t[k % 2][:], ACT.Copy).then_inc(xnT_ready, 1)

            def products(c):
                for u in range(UNITS):
                    act.wait_ge(m_done, c * UNITS + u + 1)
                    src = ps_m[u % 2]
                    if u < ML:
                        last = act.activation(latent[:, u, :], src[:], ACT.Copy)
                    elif u < MI + ML:
                        act.wait_ge(h_ready, c * MI + u - ML + 1)
                        last = act.activation(relu[:, (u - ML) % 2, :], src[:], ACT.Relu)
                    elif u == MI + ML:
                        last = act.activation(logits[:].rearrange("p t e -> p (t e)"), src[:, 0:TT * NE], ACT.Copy)
                    else:
                        last = act.activation(mixed[:, u - MI - ML - 1, :], src[:], ACT.Copy)
                    last.then_inc(m_free, 1)

            def silu(c):
                act.wait_ge(g_stored, 16 * (c + 1))
                for t in range(TT):
                    act.wait_ge(shifted, c * TT + t + 1)
                    act.activation(g_out[:, t, :], y[:, t, :], ACT.Silu).then_inc(g_ready, 1)
                act.wait_ge(g_ready, (c + 2) * TT)
                act.dma_start(g_rows[ds(c, 1)].rearrange("a p t d -> p (a t) d"), g_out[:]).then_inc(g_stored, 16)

            transposed(0)
            products(0)
            with act.Fori(0, NCH - 1) as c:
                transposed(c + 1)
                products(c + 1)
                silu(c)
            silu(NCH - 1)

        @block.gpsimd
        def _(pool):
            primed(pool, g_stored, 16)
            primed(pool, xnT_stored, 16)
            pool.memset(half[:], -0.5).then_inc(half_set, 1)
            pool.wait_ge(half_set, 1)

            def norm_x(c):
                pool.wait_ge(var_ready, c + 1)
                pool.tensor_tensor(rstd[:], var[:], half[:, 0:TT], ALU.pow).then_inc(rstd_ready, 1)

            def norm_y(c):
                pool.wait_ge(var2_ready, c + 1)
                pool.tensor_tensor(rstd2[:], var2[:], half[:, 0:TT], ALU.pow).then_inc(rstd2_ready, 1)
                for t in range(TT):
                    pool.wait_ge(yn_ready, c * TT + t + 1)
                    pool.tensor_tensor(y[:, t, :], y[:, t, :], gamma[:], ALU.mult).then_inc(scaled, 1)
                    pool.wait_ge(scaled, c * TT + t + 1)
                    pool.tensor_tensor(y[:, t, :], y[:, t, :], beta[:], ALU.add).then_inc(shifted, 1)

            norm_x(0)
            pool.memset(weights.pairs, 0.0).then_inc(weights.zeroed, 1)
            pool.wait_ge(w2_loaded, 64)
            with pool.Fori(0, NCH - 1) as c:
                norm_x(c + 1)
                norm_y(c)
            norm_y(NCH - 1)

        @block.vector
        def _(dve):
            primed(dve, h_ready, 2)
            primed(dve, y_ready, 2)

            def norm_x(c):
                dve.wait_ge(x_loaded, 16 * (c + 1))
                for t in range(TT):
                    dve.bn_stats(stats[:, t, :], x_in[:, t, :]).then_inc(stats_done, 1)
                for t in range(TT):
                    wait_apart(dve, stats_done, 2 * c * TT + t + 1, ticks)
                    dve.bn_aggr(mv[:, t, :], stats[:, t, :]).then_inc(stats_done, 1)
                dve.wait_ge(stats_done, 2 * (c + 1) * TT)
                dve.tensor_scalar(var[:], mv[:, :, 1], EPS, None, ALU.add).then_inc(var_ready, 1)
                dve.wait_ge(rstd_ready, c + 1)
                if not isinstance(c, int):
                    dve.wait_ge(t_done, c * KD)
                for t in range(TT):
                    last = dve.tensor_scalar(xn[:, t, :], x_in[:, t, :], mv[:, t, 0:1], rstd[:, t:t + 1],
                                             ALU.subtract, ALU.mult)
                last.then_inc(xn_ready, 1)

            def finish(c):
                for u in range(MI):
                    dve.wait_ge(m_free, c * UNITS + ML + u + 3)
                    dve.tensor_tensor(hidden[:, u, :], relu[:, u % 2, :], relu[:, u % 2, :], ALU.mult)\
                       .then_inc(h_ready, 1)
                wait_apart(dve, m_free, c * UNITS + MI + ML + 3, ticks)
                for t in range(TT):
                    dve.max(top[:, t, :], logits[:, t, :]).then_inc(top_done, 1)
                dve.wait_ge(top_done, (c + 1) * TT)
                dve.tensor_tensor(route[:], top[:, :, 0], top[:, :, 1], ALU.add).then_inc(route_ready, 1)
                dve.wait_ge(route_ready, c + 1)
                for t in range(TT):
                    dve.wait_ge(g_ready, c * TT + t + 1)
                    dve.wait_ge(out_done, c * TT + t + 1)
                    dve.tensor_scalar(y[:, t, :], ps_r[t % 2][:], route[:, t:t + 1], None, ALU.mult).then_inc(y_routed, 1)
                    dve.wait_ge(y_routed, c * TT + t + 1)
                    dve.tensor_tensor(y[:, t, :], y[:, t, :], ps_d[t % 2][:], ALU.add).then_inc(y_ready, 1)
                for t in range(TT):
                    dve.wait_ge(y_ready, c * TT + t + 3)
                    dve.bn_stats(stats2[:, t, :], y[:, t, :]).then_inc(stats2_done, 1)
                for t in range(TT):
                    wait_apart(dve, stats2_done, 2 * c * TT + t + 1, ticks)
                    dve.bn_aggr(mv2[:, t, :], stats2[:, t, :]).then_inc(stats2_done, 1)
                dve.wait_ge(stats2_done, 2 * (c + 1) * TT)
                dve.tensor_scalar(var2[:], mv2[:, :, 1], EPS, None, ALU.add).then_inc(var2_ready, 1)
                dve.wait_ge(rstd2_ready, c + 1)
                for t in range(TT):
                    dve.tensor_scalar(y[:, t, :], y[:, t, :], mv2[:, t, 0:1], rstd2[:, t:t + 1],
                                      ALU.subtract, ALU.mult).then_inc(yn_ready, 1)

            norm_x(0)
            with dve.Fori(0, NCH - 1) as c:
                norm_x(c + 1)
                finish(c)
            finish(NCH - 1)


class ProjectionWeights:

    def __init__(self, dram, sem, space):
        flat = space[:].rearrange("p a m b n -> p (a m b n)").bitcast(F32)
        NO = (LAT + 2 * KVD) // P
        ends = [NO * D, (MQ + MK) * P * TAPS, MK * KVD * TAPS]
        at = [sum(ends[:i]) for i in range(4)]
        self.dram = dram
        self.rows = flat[:, at[0]:at[1]].rearrange("p (o d) -> p o d", d=D)
        self.pairs = flat[:, at[1]:at[2]].rearrange("p (m i a) -> p m i a", i=P, a=TAPS)
        self.dense = flat[:, at[2]:at[3]].rearrange("p (o i a) -> p o i a", i=KVD, a=TAPS)
        self.loaded = sem("b_w_loaded")
        self.conv_loaded = sem("b_conv_loaded")
        self.zeroed = sem("b_zeroed")

    def load(self, sp):
        sp.dma_start(self.rows, self.dram["w_qkv"].rearrange("(o p) d -> p o d", p=P)).then_inc(self.loaded, 16)
        sp.dma_start(self.dense.rearrange("p o i a -> p o (i a)"),
                     self.dram["kc2_w"].rearrange("(o p) i a -> p o (i a)", p=P)).then_inc(self.conv_loaded, 16)

    def load_pairs(self, sp):
        for g in range(2):
            lo = g * HD0
            for src, at, n in ((self.dram["qc1_w"], 0, MQ), (self.dram["kc1_w"], MQ, MK)):
                sp.dma_start(self.pairs[lo:lo + HD0, at:at + n, lo:lo + HD0, :].rearrange("p m i a -> p m (i a)"),
                             src.rearrange("(m g p) i a -> g p m (i a)", g=2, p=HD0)[g]).then_inc(self.conv_loaded, 16)


def project_phase(nc, sem, dram, ident, conv_in, weights, unscale, rows0, rows0_loaded):
    with ExitStack() as ctx:
        def sb(name, shape, dt=F32):
            return ctx.enter_context(nc.sbuf_tensor(f"b_{name}", shape, dt))

        wT = sb("wT", [P, KD, LAT + 2 * KVD])
        meanT = sb("meanT", [P, 2, KD, P])
        mean = sb("mean", [P, 2, KD, HD0])
        c1T = sb("c1T", [P, MQ * TAPS, P])
        kc1T = sb("kc1T", [P, MK * TAPS, P])
        kc2T = sb("kc2T", [P, MK * TAPS, KVD])
        bias = sb("bias", [P, MQ + 2 * MK])
        scale = sb("scale", [P, 1])
        scaled_bias = sb("scaled_bias", [P, MQ])

        rows, pairs, dense = weights.rows, weights.pairs, weights.dense
        turned = sem("b_turned")
        out_act = sem("b_out_act")
        out_dve = sem("b_out_dve")
        mean_summed = sem("b_mean_summed")

        NO = (LAT + 2 * KVD) // P
        with ExitStack() as prep:
            magnitude = prep.enter_context(nc.sbuf_tensor("b_magnitude", [P, MQ, P * TAPS], F32))
            squares = prep.enter_context(nc.sbuf_tensor("b_squares", [P, MQ, D], F32))
            sums = prep.enter_context(nc.sbuf_tensor("b_sums", [P, 2, MQ], F32))
            most = prep.enter_context(nc.sbuf_tensor("b_most", [P, 3], F32))
            most_all = prep.enter_context(nc.sbuf_tensor("b_most_all", [P, 3], F32))
            peak = prep.enter_context(nc.sbuf_tensor("b_peak", [3, 1], F32))
            peaks = prep.enter_context(nc.sbuf_tensor("b_peaks", [3, 3], F32))
            ones = prep.enter_context(nc.sbuf_tensor("b_ones", [3, P], F32))
            root = prep.enter_context(nc.sbuf_tensor("b_root", [P, 2], F32))
            size = prep.enter_context(nc.sbuf_tensor("b_size", [P, MQ], F32))
            ps_w = prep.enter_context(nc.psum_tensor("b_ps_w", [P, P], F32))
            PIECES = tuple(range(4, 4 + 2 * MQ, 4))
            set_up, measured, bound_step = sem("b_set_up"), sem("b_measured"), sem("b_bound_step")
            peak_done, rooted = sem("b_peak_done"), sem("b_rooted")
            ps = [prep.enter_context(nc.psum_tensor(f"b_psw{i}", [P, CH], F32)) for i in range(4)]
            groups = []
            for o in range(NO):
                groups.append(([rows[:, o, k * P:(k + 1) * P] for k in range(KD)], wT[:, :, o * P:(o + 1) * P]))
            for m in range(MQ + MK):
                to = c1T[:, m * TAPS:(m + 1) * TAPS, :] if m < MQ else kc1T[:, (m - MQ) * TAPS:(m - MQ + 1) * TAPS, :]
                groups.append(([pairs[:, m, :, a] for a in range(TAPS)], to))
            for o in range(MK):
                for i in range(MK):
                    groups.append(([dense[:, o, i * P:(i + 1) * P, a] for a in range(TAPS)],
                                   kc2T[:, i * TAPS:(i + 1) * TAPS, o * P:(o + 1) * P]))
            with nc.Block() as block:
                @block.sync
                def _(sp):
                    for name, at, n in (("qc1_b", 0, MQ), ("kc1_b", MQ, MK), ("kc2_b", MQ + MK, MK)):
                        sp.dma_start(bias[:, at:at + n], dram[name].rearrange("(m p) -> p m", p=P), allow_slow_non_contiguous=True)\
                          .then_inc(weights.conv_loaded, 16)

                @block.tensor
                def _(pe):
                    for n, (blocks, _) in enumerate(groups):
                        if n == 0:
                            pe.wait_ge(weights.loaded, 16)
                        if n == NO:
                            pe.wait_ge(weights.conv_loaded, 16 * 8)
                        if n >= 4:
                            pe.wait_ge(out_dve if n % 2 else out_act, (n - 4) // 2 + 1)
                        for j, src in enumerate(blocks):
                            last = pe.transpose(ps[n % 4][:, j * P:(j + 1) * P], src, ident[:])
                        last.then_inc(turned, 1)
                    pe.wait_ge(bound_step, 2)
                    pe.matmul(ps_w[0:3, :], most[:], ident[:], start=True, stop=True).then_inc(peak_done, 1)
                    pe.wait_ge(bound_step, 4)
                    pe.wait_ge(set_up, 2)
                    pe.matmul(ps_w[:, 0:3], ones[:], peaks[:], start=True, stop=True).then_inc(peak_done, 1)

                @block.gpsimd
                def _(pool):
                    pool.memset(ones[:], 1.0).then_inc(set_up, 1)
                    pool.memset(root[:, 1:2], 0.5).then_inc(set_up, 1)
                    pool.wait_ge(set_up, 2)
                    pool.wait_ge(bound_step, 5)
                    pool.tensor_tensor(root[:, 0:1], most_all[:, 0:1], root[:, 1:2], ALU.pow).then_inc(rooted, 1)

                @block.scalar
                def _(act):
                    for n, (blocks, to) in enumerate(groups):
                        if n in PIECES:
                            tiles = slice(2 * PIECES.index(n), 2 * PIECES.index(n) + 2)
                            act.wait_ge(weights.loaded, 16)
                            act.wait_ge(weights.conv_loaded, 16 * 8)
                            act.activation(magnitude[:, tiles, :], pairs[:, tiles, :, :].rearrange("p m i a -> p m (i a)"), ACT.Abs)
                            act.activation(size[:, tiles], bias[:, tiles], ACT.Abs)
                            act.activation(squares[:, tiles, :], rows[:, tiles, :], ACT.Square).then_inc(measured, 1)
                        if n % 2 == 0:
                            act.wait_ge(turned, n + 1)
                            act.activation(to, ps[n % 4][:, 0:len(blocks) * P].rearrange("p (j n) -> p j n", n=P),
                                           ACT.Copy).then_inc(out_act, 1)

                @block.vector
                def _(dve):
                    for n, (blocks, to) in enumerate(groups):
                        if n - 3 in PIECES:
                            piece = PIECES.index(n - 3)
                            tiles = slice(2 * piece, 2 * piece + 2)
                            dve.wait_ge(measured, piece + 1)
                            dve.tensor_reduce(sums[:, 0, tiles], squares[:, tiles, :], AX.X, ALU.add)
                            last = dve.tensor_reduce(sums[:, 1, tiles], magnitude[:, tiles, :], AX.X, ALU.add)
                            if piece == len(PIECES) - 1:
                                last.then_inc(bound_step, 1)
                                dve.wait_ge(bound_step, 1)
                                dve.tensor_reduce(most[:, 0:2], sums[:], AX.X, ALU.max)
                                dve.tensor_reduce(most[:, 2:3], size[:], AX.X, ALU.max).then_inc(bound_step, 1)
                        if n % 2 == 1:
                            dve.wait_ge(turned, n + 1)
                            dve.tensor_copy(to, ps[n % 4][:, 0:len(blocks) * P].rearrange("p (j n) -> p j n", n=P))\
                               .then_inc(out_dve, 1)
                    dve.wait_ge(peak_done, 1)
                    dve.tensor_reduce(peak[:], ps_w[0:3, :], AX.X, ALU.max).then_inc(bound_step, 1)
                    dve.wait_ge(bound_step, 3)
                    dve.tensor_scalar(peaks[:], ident[0:3, 0:3], peak[:, 0:1], None, ALU.mult).then_inc(bound_step, 1)
                    dve.wait_ge(peak_done, 2)
                    dve.tensor_scalar(most_all[:], ps_w[:, 0:3], 1e-30, None, ALU.max).then_inc(bound_step, 1)
                    dve.wait_ge(rooted, 1)
                    dve.tensor_scalar(root[:, 0:1], root[:, 0:1], most_all[:, 1:2], D ** 0.5 / FULL, ALU.mult, ALU.mult).then_inc(bound_step, 1)
                    dve.wait_ge(bound_step, 6)
                    dve.scalar_tensor_tensor(unscale[:], most_all[:, 2:3], 1 / FULL, root[:, 0:1], ALU.mult, ALU.add).then_inc(bound_step, 1)
                    dve.wait_ge(bound_step, 7)
                    dve.reciprocal(scale[:], unscale[:]).then_inc(bound_step, 1)
                    dve.wait_ge(bound_step, 8)
                    dve.tensor_scalar(scaled_bias[:], bias[:, 0:MQ], scale[:, 0:1], None, ALU.mult)
                    dve.wait_ge(out_act, (len(groups) + 1) // 2)
                    dve.wait_ge(out_dve, len(groups) // 2)
                    for n, (at, heads) in enumerate(((LAT, KV0), (0, H0))):
                        for k in range(KD):
                            dve.tensor_reduce(mean[:, n, k, :], wT[:, k, at:at + heads * HD0].rearrange("p (h c) -> p c h", c=HD0),
                                              AX.X, ALU.add).then_inc(mean_summed, 1)
                    dve.wait_ge(mean_summed, 2 * KD)
                    for n, heads in enumerate((KV0, H0)):
                        for copy in range(2):
                            dve.tensor_scalar(meanT[:, n, :, copy * HD0:(copy + 1) * HD0], mean[:, n, :, :], 0.5 / heads,
                                              None, ALU.mult)

        xb = [sb(f"xb{i}", [P, KD, CH + 1]) for i in range(2)]
        q_pre = sb("q_pre", [P, MQ, PAD + S])
        k_pre = sb("k_pre", [P, MK, PAD + S])
        k_conv = sb("k_conv", [P, MK, PAD + S])
        stage = [sb(f"stage{i}", [P, CH]) for i in range(5)]
        convs = [sb(f"convs{i}", [P, CH]) for i in range(2)]
        UNITS, RING = MQ + MK + MQ + MK + 2 + 1 + MK, 5
        assert UNITS % RING == 0
        ps = [ctx.enter_context(nc.psum_tensor(f"b_ps{i}", [P, CH], F32)) for i in range(RING)]
        Q0, K0, C0, KC0, V0, M0, K20 = 0, MQ, MQ + MK, 2 * MQ + MK, 2 * MQ + 2 * MK, 2 * MQ + 2 * MK + 2, 2 * MQ + 2 * MK + 3

        padded = sem("b_padded")
        high_ready = sem("b_high_ready")
        low_ready = sem("b_low_ready")
        ticks = sem("ticks")
        x_loaded = [sem(f"b_x_loaded{i}") for i in range(2)]
        made = sem("b_made")
        took_act = sem("b_took_act")
        took_dve = sem("b_took_dve")
        stored = sem("b_stored")
        N_ACT, N_DVE = (UNITS + 1) // 2, UNITS // 2

        def taken(n, u):
            if u % 2 == 0:
                return took_act, (n + 1) * N_ACT + u // 2 + 1
            return took_dve, (n + 1) * N_DVE + u // 2 + 1

        block = ctx.enter_context(nc.Block())

        @block.sync
        def _(sp):
            primed(sp, stored, 16 * 5)
            sp.wait_ge(padded, 1)
            src = dram["xnT"].rearrange("k p t -> p k t")

            def load(b, h):
                if b > 0:
                    sp.wait_ge(took_act, (2 * b + h) * N_ACT)
                first = b * S + h * CH - h
                sp.dma_start(xb[h][:, :, 1 - h:], src[:, :, first:b * S + (h + 1) * CH]).then_inc(x_loaded[h], 16)

            def store(n):
                for i, u in enumerate((V0, V0 + 1)):
                    sp.wait_ge(*taken(n, u))
                    sp.dma_start(dram["v"].rearrange("(n t p) c -> n p t c", t=2, p=P)[2 * n + i],
                                 stage[i][:].rearrange("p (t c) -> p t c", t=2)).then_inc(stored, 16)
                sp.wait_ge(*taken(n, M0))
                sp.dma_start(dram["k_mean"][:, n * CH:(n + 1) * CH], stage[2][:]).then_inc(stored, 16)
                for i in range(MK):
                    sp.wait_ge(*taken(n, K20 + i))
                    sp.dma_start(dram["k_raw"][i, :, n * CH:(n + 1) * CH], stage[3 + i][:]).then_inc(stored, 16)

            for h in range(2):
                load(0, h)
            sp.dma_start(rows0[:].rearrange("p i a -> p (i a)"), dram["qc2_w"][0:P].rearrange("p i a -> p (i a)")).then_inc(rows0_loaded, 16)
            for b in range(B):
                for h in range(2):
                    store(2 * b + h)
                    if b + 1 < B:
                        load(b + 1, h)
            sp.wait_ge(stored, 16 * 5 * (NCH + 1))

        @block.gpsimd
        def _(pool):
            pool.memset(q_pre[:, :, 0:PAD], 0.0)
            pool.memset(k_pre[:, :, 0:PAD], 0.0)
            pool.memset(k_conv[:, :, 0:PAD], 0.0)
            pool.memset(conv_in[:, :, :, :, 0:PAD], 0.0)
            pool.memset(xb[0][:, :, 0:1], 0.0).then_inc(padded, 1)
            primed(pool, low_ready, 2)
            with pool.Fori(0, B) as b:
                for h in range(2):
                    n, lo = 2 * b + h, PAD + h * CH
                    for m in range(MQ):
                        def to(part):
                            return conv_in[:, part, m, ds(b, 1), lo:lo + CH].rearrange("p b n -> p (b n)")

                        src = convs[m % 2][:]
                        wait_apart(pool, taken(n, C0 + m)[0], taken(n, C0 + m)[1], ticks)
                        pool.tensor_copy(to(0), src).then_inc(high_ready, 1)
                        wait_apart(pool, high_ready, n * MQ + m + 1, ticks)
                        pool.tensor_tensor(to(1), src, to(0), ALU.subtract).then_inc(low_ready, 1)

        @block.tensor
        def _(pe):
            pe.wait_ge(padded, 1)

            def unit(b, h, u):
                n, out = 2 * b + h, ps[u % RING]
                pe.wait_ge(*(taken(n, u - RING) if u >= RING else taken(n - 1, u + UNITS - RING)))
                x, lo = xb[h], h * CH
                if u < C0:
                    for k in range(KD):
                        last = pe.matmul(out[:], wT[:, k, u * P:(u + 1) * P], x[:, k, 1:], start=(k == 0), stop=(k == KD - 1))
                elif u < V0:
                    m, wgt, src, of = (u - C0, c1T, q_pre, Q0) if u < KC0 else (u - KC0, kc1T, k_pre, K0)
                    pe.wait_ge(*taken(n, of + m))
                    for a in range(TAPS):
                        last = pe.matmul(out[:], wgt[:, m * TAPS + a, :], src[:, m, lo + a:lo + a + CH],
                                         start=(a == 0), stop=(a == TAPS - 1))
                elif u < M0:
                    for t in range(2):
                        col = (2 * (u - V0) + t) * P
                        for late in range(2):
                            for k in range(KD):
                                last = pe.matmul(out[:, t * KVD + late * P:t * KVD + (late + 1) * P],
                                                 x[:, k, col + 1 - late:col + 1 - late + P],
                                                 wT[:, k, LAT + KVD + late * P:LAT + KVD + (late + 1) * P],
                                                 start=(k == 0), stop=(k == KD - 1))
                elif u == M0:
                    for k in range(KD):
                        last = pe.matmul(out[:], meanT[:, 0, k, :], x[:, k, 1:], start=(k == 0), stop=(k == KD - 1))
                else:
                    o = u - K20
                    for k in range(KD):
                        pe.matmul(out[:], meanT[:, 1, k, :], x[:, k, 1:], start=(k == 0), stop=False)
                    for i in range(MK):
                        pe.wait_ge(*taken(n, KC0 + i))
                        for a in range(TAPS):
                            last = pe.matmul(out[:], kc2T[:, i * TAPS + a, o * P:(o + 1) * P], k_conv[:, i, lo + a:lo + a + CH],
                                             start=False, stop=(i == MK - 1 and a == TAPS - 1))
                last.then_inc(made, 1)

            with pe.Fori(0, B) as b:
                for h in range(2):
                    pe.wait_ge(x_loaded[h], 16 * (b + 1))
                    for u in range(UNITS):
                        unit(b, h, u)

        def take(engine, b, h, u):
            n, src, lo = 2 * b + h, ps[u % RING], PAD + h * CH
            engine.wait_ge(made, n * UNITS + u + 1)
            if u >= V0 and u != K20 + 1:
                engine.wait_ge(stored, 16 * 5 * (n + 1))
            if u < K0:
                to, add = q_pre[:, u, lo:lo + CH], None
            elif u < C0:
                to, add = k_pre[:, u - K0, lo:lo + CH], None
            elif u < KC0:
                engine.wait_ge(low_ready, n * MQ + u - C0 + 1)
                to, add = convs[(u - C0) % 2][:], u - C0
                if engine.engine == mybir.EngineType.Activation:
                    return engine.activation(to, src[:], ACT.Identity, bias=scaled_bias[:, add:add + 1], scale=scale[:, 0:1])
                return engine.tensor_scalar(to, src[:], scale[:, 0:1], scaled_bias[:, add:add + 1], ALU.mult, ALU.add)
            elif u < V0:
                to, add = k_conv[:, u - KC0, lo:lo + CH], MQ + u - KC0
            else:
                to, add = stage[u - V0][:], (MQ + MK + u - K20 if u >= K20 else None)
            if engine.engine == mybir.EngineType.Activation:
                if add is None:
                    return engine.activation(to, src[:], ACT.Copy)
                return engine.activation(to, src[:], ACT.Identity, bias=bias[:, add:add + 1])
            if add is None:
                return engine.tensor_copy(to, src[:])
            return engine.tensor_scalar(to, src[:], bias[:, add:add + 1], None, ALU.add)

        @block.scalar
        def _(act):
            primed(act, took_act, N_ACT)
            with act.Fori(0, B) as b:
                for h in range(2):
                    for u in range(0, UNITS, 2):
                        take(act, b, h, u).then_inc(took_act, 1)

        @block.vector
        def _(dve):
            primed(dve, took_dve, N_DVE)
            with dve.Fori(0, B) as b:
                for h in range(2):
                    for u in range(1, UNITS, 2):
                        take(dve, b, h, u).then_inc(took_dve, 1)


def query_phase(nc, sem, dram, ident, half, conv_in, unscale, rows0, rows0_loaded):
    with ExitStack() as ctx:
        def sb(name, shape, dt=F32):
            return ctx.enter_context(nc.sbuf_tensor(f"c_{name}", shape, dt))

        def bank(name):
            return ctx.enter_context(nc.psum_tensor(f"c_{name}", [P, CH], F32))

        rows = [rows0, sb("rows1", [P, LAT, TAPS])]
        wT = [sb(f"wT{i}", [P, 2, MQ * TAPS, P], FP16) for i in range(2)]
        k_mean = sb("k_mean", [P, T])
        k_in = sb("k_in", [P, T])
        raw = [sb(f"raw{i}", [P, T]) for i in range(2)]
        square = sb("square", [P, T])
        swapped = sb("swapped", [P, B, S])
        turned = sb("turned", [P, B, S])
        high = sb("high", [P, T], FP16)
        low = sb("low", [P, T], FP16)
        cos = sb("cos", [P, S])
        sin = sb("sin", [P, S])
        head2 = sb("head2", [P, 2])
        temp = sb("temp", [P, 1])
        bias = sb("bias", [P, MQ])
        ends = sb("ends", [P, 4])
        w_scale = [sb(f"w_scale{i}", [P, 1]) for i in range(2)]
        w_unscale = [sb(f"w_unscale{i}", [P, 1]) for i in range(2)]
        offset = [sb(f"offset{i}", [P, T]) for i in range(2)]
        norm = sb("norm", [P, 2 * T // P])
        rnorm = sb("rnorm", [P, 2 * T // P])
        ps_c = [bank(f"ps_c{i}") for i in range(2)]
        ps_t = [bank(f"ps_t{i}") for i in range(2)]
        ps_b = [bank(f"ps_b{i}") for i in range(2)]
        ps_s = bank("ps_s")

        tables = sem("c_tables")
        k_loaded = sem("c_k_loaded")
        rows_loaded = [rows0_loaded, sem("c_rows1_loaded")]
        w_turned = sem("c_w_turned")
        w_high = sem("c_w_high")
        w_ready = sem("c_w_ready")
        w_step = sem("c_w_step")
        w_scaled = sem("c_w_scaled")
        offset_ready = sem("c_offset_ready")
        conv_done = sem("c_conv_done")
        raw_ready = sem("c_raw_ready")
        square_ready = sem("c_square_ready")
        sums_done = sem("c_sums_done")
        norm_ready = sem("c_norm_ready")
        powed = sem("c_powed")
        rnorm_ready = sem("c_rnorm_ready")
        swap_ready = sem("c_swap_ready")
        rot_step = sem("c_rot_step")
        spread_done = sem("c_spread_done")
        unit_ready = sem("c_unit_ready")
        high_ready = sem("c_high_ready")
        low_ready = sem("c_low_ready")
        stored = sem("c_stored")
        ticks = sem("ticks")

        BLOCKS = MQ * TAPS
        WG = BLOCKS // 4
        PAIRS = [p ^ 1 for p in range(32)]

        def stored_by(j):
            return 128 * j if isinstance(j, int) and j <= MK else 128 * MK + (j - MK) * 64

        def after(m, n):
            if isinstance(m, int) and m == 0:
                return ((("spread", 0), ("turn", 0)), (("turn", 1), ("sums", 1)), (("turn", 2),), (("spread", 1),))[n]
            turn = () if isinstance(m, int) and m == MQ - 1 else (("turn", n),)
            return ((("sums", m + 1),) + turn, turn, (("spread", m + 1),) + turn, ())[n]

        block = ctx.enter_context(nc.Block())

        @block.sync
        def _(sp):
            w_rows = dram["qc2_w"].rearrange("(m p) i a -> m p (i a)", p=P)

            def load_rows(m, u):
                sp.dma_start(rows[u][:].rearrange("p i a -> p (i a)"), w_rows[ds(m, 1)].rearrange("m p n -> p (m n)"))\
                  .then_inc(rows_loaded[u], 16)

            for j, to in enumerate((k_in, raw[1])):
                sp.dma_start(to[:], dram["k_raw"][j]).then_inc(k_loaded, 16)
            sp.dma_start(k_mean[:], dram["k_mean"]).then_inc(tables, 16)
            sp.dma_start(bias[:], dram["qc2_b"].rearrange("(m p) -> p m", p=P), allow_slow_non_contiguous=True).then_inc(tables, 16)
            sp.dma_start(head2[:], dram["head2"]).then_inc(tables, 16)
            sp.dma_start(cos[:], dram["cos0"]).then_inc(tables, 16)
            sp.dma_start(sin[:], dram["sin0"]).then_inc(tables, 16)
            sp.dma_start(temp[:], dram["key_temp"].rearrange("(a n) -> a n", a=1).to_broadcast((P, 1))).then_inc(tables, 16)
            load_rows(1, 1)

            def store_keys(j):
                sp.wait_ge(low_ready, j + 1)
                for g in range(2):
                    for part, to in ((high, "k_high"), (low, "k_low")):
                        for copy in range(2):
                            sp.dma_start(dram[to][2 * j + g, copy * HD0:(copy + 1) * HD0, :], part[g * HD0:(g + 1) * HD0, :])\
                              .then_inc(stored, 16)

            def store_queries(m):
                sp.wait_ge(low_ready, m + MK + 1)
                for g in range(2):
                    for n, part in enumerate((high, low)):
                        sp.dma_start(dram["q_parts"][ds(2 * m + g, 1), n * HD0:(n + 1) * HD0, :].rearrange("a p t -> p (a t)"),
                                     part[g * HD0:(g + 1) * HD0, :]).then_inc(stored, 16)

            store_keys(0)
            store_keys(1)
            with sp.Fori(0, MQ // 2 - 1) as i:
                for u in range(2):
                    sp.wait_ge(w_turned, WG * (2 * i + u + 1))
                    load_rows(2 * i + 2 + u, u)
                for u in range(2):
                    store_queries(2 * i + u)
            store_queries(MQ - 2)
            store_queries(MQ - 1)
            sp.wait_ge(stored, stored_by(MQ + MK))

        @block.tensor
        def _(pe):
            def turn(k, u, groups):
                for g in groups:
                    if g == 0:
                        pe.wait_ge(w_scaled, k + 1)
                    if g >= 2 or not isinstance(k, int) or k > 0:
                        pe.wait_ge(w_ready, WG * k + g - 1 if g >= 2 else WG * k)
                    for j in range(4):
                        i, a = divmod(4 * g + j, TAPS)
                        last = pe.transpose(ps_t[g % 2][:, j * P:(j + 1) * P], rows[u][:, i * P:(i + 1) * P, a], ident[:])
                    last.then_inc(w_turned, 1)

            def sums(j):
                pe.wait_ge(square_ready, j + 1)
                if not isinstance(j, int) or j > 0:
                    pe.wait_ge(norm_ready, j)
                for t in range(T // P):
                    last = pe.matmul(ps_s[:, 2 * t:2 * t + 2], square[:, t * P:(t + 1) * P], head2[:], start=True, stop=True)
                last.then_inc(sums_done, 1)

            def spread(j):
                pe.wait_ge(rnorm_ready, j + 1)
                for n in range(NCH):
                    if n >= 2:
                        pe.wait_ge(unit_ready, NCH * j + n - 1)
                    for t in range(TT):
                        c = 2 * (n * TT + t)
                        last = pe.matmul(ps_b[n % 2][:, t * P:(t + 1) * P],
                                         square[:, c * HD0:(c + 2) * HD0],
                                         ident[:], start=True, stop=True)
                    last.then_inc(spread_done, 1)

            def tile(m, u):
                pe.wait_ge(w_ready, WG * (m + 1))
                for n in range(NCH):
                    if n >= 2 or not isinstance(m, int) or m > 0:
                        pe.wait_ge(raw_ready, NCH * m + n - 1)
                    b, h = divmod(n, NCH // B)
                    for i in range(MQ):
                        for a in range(TAPS):
                            for w, x in ((0, 0), (0, 1), (1, 0)):
                                last = pe.matmul(ps_c[n % 2][:], wT[u][:, w, i * TAPS + a, :],
                                                 conv_in[:, x, i, b, h * CH + a:h * CH + a + CH],
                                                 start=(i == 0 and a == 0 and w == 0 and x == 0),
                                                 stop=(i == MQ - 1 and a == TAPS - 1 and w == 1))
                    last.then_inc(conv_done, 1)
                    for what, j in after(m, n):
                        if what == "sums":
                            sums(j)
                        elif what == "spread":
                            spread(j)
                        else:
                            turn(m + 1, 1 - u, range(2 * j, 2 * j + 2))

            pe.wait_ge(tables, 16 * 6)
            sums(0)
            turn(0, 0, range(WG))
            tile(0, 0)
            with pe.Fori(0, MQ // 2 - 1) as i:
                tile(2 * i + 1, 1)
                tile(2 * i + 2, 0)
            tile(MQ - 1, 1)
            sums(MQ + 1)
            spread(MQ + 1)

        @block.scalar
        def _(act):
            def weights(k, u, groups):
                for g in groups:
                    act.wait_ge(w_turned, WG * k + g + 1)
                    act.activation(wT[u][:, 0, 4 * g:4 * g + 4, :].rearrange("p j n -> p (j n)"), ps_t[g % 2][:], ACT.Copy)\
                       .then_inc(w_high, 1)

            def scale_rows(k, u):
                act.wait_ge(w_step, 5 * (k + 1))
                act.activation(rows[u][:].rearrange("p i a -> p (i a)"), rows[u][:].rearrange("p i a -> p (i a)"), ACT.Identity,
                               scale=w_scale[u][:, 0:1]).then_inc(w_scaled, 1)
                if not isinstance(k, int) or k > 1:
                    wait_apart(act, raw_ready, NCH * (k - 1), ticks)
                act.activation(offset[u][:], k_mean[:], ACT.Identity, bias=bias[:, ds(k, 1)]).then_inc(offset_ready, 1)

            def squares(j, src):
                if isinstance(j, int) and j < MK:
                    act.wait_ge(k_loaded, 32)
                else:
                    act.wait_ge(raw_ready, NCH * (j - MK + 1))
                if not isinstance(j, int) or j > 0:
                    act.wait_ge(spread_done, NCH * j)
                act.activation(square[:], src, ACT.Square).then_inc(square_ready, 1)

            def highs(j):
                act.wait_ge(unit_ready, NCH * (j + 1))
                if not isinstance(j, int) or j > 0:
                    act.wait_ge(stored, stored_by(j))
                act.activation(high[:], turned[:].rearrange("p b s -> p (b s)"), ACT.Copy).then_inc(high_ready, 1)

            def tile(m, u, last=False):
                if not last:
                    scale_rows(m + 1, 1 - u)
                squares(m + 1, raw[1 - u][:])
                if not last:
                    weights(m + 1, 1 - u, range(WG))
                highs(m + 1)

            act.wait_ge(tables, 16 * 6)
            squares(0, k_in[:])
            scale_rows(0, 0)
            weights(0, 0, range(WG))
            scale_rows(1, 1)
            weights(1, 1, range(2))
            highs(0)
            squares(1, raw[1][:])
            weights(1, 1, range(2, WG))
            highs(1)
            with act.Fori(0, MQ // 2 - 1) as i:
                tile(2 * i + 1, 1)
                tile(2 * i + 2, 0)
            tile(MQ - 1, 1, True)
            squares(MQ + 1, raw[1][:])
            highs(MQ + 1)

        @block.gpsimd
        def _(pool):
            pool.wait_ge(tables, 16 * 6)

            def rotate(j, src):
                src = src.rearrange("p (b s) -> p b s", b=B)
                if not isinstance(j, int) or j > 0:
                    pool.wait_ge(spread_done, NCH * j)
                pool.wait_ge(norm_ready, j + 1)
                pool.tensor_tensor(rnorm[:], norm[:], half[:, 0:2 * T // P], ALU.pow).then_inc(powed, 1)
                wait_apart(pool, powed, j + 1, ticks)
                pool.tensor_scalar(square[:].rearrange("p (n c) -> p n c", c=HD0),
                                   rnorm[:].rearrange("p (n o) -> p n o", o=1).to_broadcast((P, 2 * T // P, HD0)),
                                   temp[:, 0:1] if isinstance(j, int) and j < MK else 1.0, None, ALU.mult)\
                    .then_inc(rnorm_ready, 1)
                if not isinstance(j, int) or j > 0:
                    pool.wait_ge(low_ready, j)
                pool.wait_ge(swap_ready, j + 1)
                for b in range(B):
                    pool.tensor_tensor(turned[:, b, :], src[:, b, :], cos[:], ALU.mult)
                    pool.tensor_tensor(swapped[:, b, :], swapped[:, b, :], sin[:], ALU.mult).then_inc(rot_step, 1)
                for b in range(B):
                    pool.wait_ge(rot_step, 2 * B * j + B)
                    pool.tensor_tensor(turned[:, b, :], turned[:, b, :], swapped[:, b, :], ALU.add).then_inc(rot_step, 1)

            rotate(0, k_in[:])
            rotate(1, raw[1][:])
            with pool.Fori(0, MQ // 2 - 1) as i:
                rotate(2 * i + 2, raw[0][:])
                rotate(2 * i + 3, raw[1][:])
            rotate(MQ, raw[0][:])
            rotate(MQ + 1, raw[1][:])

        @block.vector
        def _(dve):
            dve.wait_ge(tables, 16 * 6)

            def take(m, u, n):
                dve.wait_ge(offset_ready, m + 1)
                dve.wait_ge(conv_done, NCH * m + n + 1)
                dve.scalar_tensor_tensor(raw[u][:, n * CH:(n + 1) * CH], ps_c[n % 2][:], w_unscale[u][:, 0:1],
                                         offset[u][:, n * CH:(n + 1) * CH], ALU.mult, ALU.add).then_inc(raw_ready, 1)

            def scales(k, u, loaded):
                flat = rows[u][:].rearrange("p i a -> p (i a)")
                dve.wait_ge(rows_loaded[u], 16 * loaded)
                dve.tensor_reduce(ends[:, 0:1], flat, AX.X, ALU.max)
                dve.tensor_reduce(ends[:, 1:2], flat, AX.X, ALU.min).then_inc(w_step, 1)
                dve.wait_ge(w_step, 5 * k + 1)
                dve.tensor_scalar(ends[:, 2:3], ends[:, 1:2], -1 / FULL, 1e-30, ALU.mult, ALU.max)
                dve.tensor_scalar(ends[:, 3:4], ends[:, 0:1], 1 / FULL, None, ALU.mult).then_inc(w_step, 1)
                dve.wait_ge(w_step, 5 * k + 2)
                dve.tensor_tensor(ends[:, 2:3], ends[:, 2:3], ends[:, 3:4], ALU.max).then_inc(w_step, 1)
                dve.wait_ge(w_step, 5 * k + 3)
                dve.reciprocal(w_scale[u][:], ends[:, 2:3]).then_inc(w_step, 1)
                dve.wait_ge(w_step, 5 * k + 4)
                if not isinstance(k, int) or k > 1:
                    dve.wait_ge(raw_ready, NCH * (k - 1))
                dve.tensor_tensor(w_unscale[u][:], ends[:, 2:3], unscale[:], ALU.mult).then_inc(w_step, 1)

            def lows(k, u, groups):
                for g in groups:
                    dve.wait_ge(w_high, WG * k + g + 1)
                    dve.tensor_tensor(wT[u][:, 1, 4 * g:4 * g + 4, :].rearrange("p j n -> p (j n)"), ps_t[g % 2][:],
                                      wT[u][:, 0, 4 * g:4 * g + 4, :].rearrange("p j n -> p (j n)"), ALU.subtract).then_inc(w_ready, 1)

            def norms(j, src):
                dve.wait_ge(sums_done, j + 1)
                dve.tensor_scalar(norm[:], ps_s[:, 0:2 * T // P], 1e-24, None, ALU.max).then_inc(norm_ready, 1)
                if isinstance(j, int) and j < MK:
                    dve.wait_ge(k_loaded, 32)
                else:
                    wait_apart(dve, raw_ready, NCH * (j - MK + 1), ticks)
                dve.stream_shuffle(swapped[:].rearrange("p b s -> p (b s)"), src, PAIRS).then_inc(swap_ready, 1)

            def split(j):
                dve.wait_ge(rot_step, 2 * B * (j + 1))
                flat = turned[:].rearrange("p b s -> p (b s)")
                for n in range(NCH):
                    dve.wait_ge(spread_done, NCH * j + n + 1)
                    dve.tensor_tensor(flat[:, n * CH:(n + 1) * CH], flat[:, n * CH:(n + 1) * CH], ps_b[n % 2][:], ALU.mult)\
                       .then_inc(unit_ready, 1)
                dve.wait_ge(high_ready, j + 1)
                dve.tensor_tensor(low[:], flat, high[:], ALU.subtract).then_inc(low_ready, 1)

            def tile(m, u, loaded):
                take(m, u, 0)
                norms(m + 1, raw[1 - u][:])
                if not isinstance(m, int) or m < LAST:
                    lows(m + 1, 1 - u, range(0, 2))
                take(m, u, 1)
                if not isinstance(m, int) or m < LAST:
                    lows(m + 1, 1 - u, range(2, 4))
                take(m, u, 2)
                split(m + 1)
                if not isinstance(m, int) or m < LAST:
                    lows(m + 1, 1 - u, range(4, WG))
                take(m, u, 3)
                if loaded is not None:
                    scales(m + 2, u, loaded)

            LAST = MQ - 1
            scales(0, 0, 1)
            norms(0, k_in[:])
            lows(0, 0, range(WG))
            scales(1, 1, 1)
            take(0, 0, 0)
            split(0)
            lows(1, 1, range(0, 2))
            take(0, 0, 1)
            lows(1, 1, range(2, 4))
            norms(1, raw[1][:])
            take(0, 0, 2)
            lows(1, 1, range(4, WG))
            take(0, 0, 3)
            split(1)
            scales(2, 0, 2)
            with dve.Fori(0, MQ // 2 - 2) as i:
                tile(2 * i + 1, 1, i + 2)
                tile(2 * i + 2, 0, i + 3)
            tile(MQ - 3, 1, MQ // 2)
            tile(MQ - 2, 0, None)
            tile(LAST, 1, None)
            norms(MQ + 1, raw[1][:])
            split(MQ + 1)


def attend_phase(nc, sem, dram, ident_bf, mask_kq, weights):
    with ExitStack() as ctx:
        def sb(name, shape, dt=F32):
            return ctx.enter_context(nc.sbuf_tensor(f"d_{name}", shape, dt))

        G0 = H0 // KV0
        RING = 4
        q = [sb(f"q{b}", [P, G0, S], FP16) for b in range(B)]
        k_high = [sb(f"k_high{b}", [P, S], FP16) for b in range(B)]
        k_low = [sb(f"k_low{b}", [P, S], FP16) for b in range(B)]
        v = [sb(f"v{b}", [P, QT, 3 * HD0]) for b in range(B)]
        probs = [sb(f"probs{i}", [P, S]) for i in range(RING)]
        inverse = [sb(f"inverse{i}", [P, S]) for i in range(2)]
        stage = [sb(f"stage{i}", [P, S]) for i in range(2)]
        temp = sb("temp", [P, 1])
        minus = sb("minus", [P, 1])
        bound = sb("bound", [P, 1])
        shift = sb("shift", [P, 1])
        ps_s = [ctx.enter_context(nc.psum_tensor(f"d_ps_s{i}", [P, S], F32)) for i in range(2)]
        ps_o = [ctx.enter_context(nc.psum_tensor(f"d_ps_o{i}", [P, S], F32)) for i in range(2)]

        tables = sem("d_tables")
        ones_set = sem("d_ones_set")
        bound_step = sem("d_bound_step")
        loaded = [sem(f"d_loaded{b}") for b in range(B)]
        s_done = sem("d_s_done")
        p_ready = sem("d_p_ready")
        pv_done = sem("d_pv_done")
        inverse_ready = sem("d_inverse_ready")
        o_used = sem("d_o_used")
        stored = [sem(f"d_stored{i}") for i in range(2)]

        STEPS = QT
        BODY = B * G0 * STEPS
        HEADS = B * G0
        PAIRS = HEADS // 2
        block = ctx.enter_context(nc.Block())

        @block.sync
        def _(sp):
            sp.dma_start(ident_bf[:], dram["ident_bf"]).then_inc(tables, 16)
            sp.dma_start(mask_kq[:], dram["mask_kq"]).then_inc(tables, 16)
            sp.dma_start(temp[:], dram["key_temp"].rearrange("(a n) -> a n", a=1).to_broadcast((P, 1))).then_inc(tables, 16)

            def load(g, b):
                sp.dma_start(q[b][:], dram["q_parts"].rearrange("(g h) p t -> g p h t", h=G0)[ds(g, 1), :, :, b * S:(b + 1) * S]
                             .rearrange("a p h t -> p (a h) t")).then_inc(loaded[b], 16)
                for to, name in ((k_high, "k_high"), (k_low, "k_low")):
                    sp.dma_start(to[b][:], dram[name][ds(g, 1), :, b * S:(b + 1) * S].rearrange("a p t -> p (a t)")).then_inc(loaded[b], 16)
                sp.dma_start(v[b][:, :, HD0:2 * HD0],
                             dram["v"][b * S:(b + 1) * S, ds(g * HD0, HD0)].rearrange("(n p) c -> p n c", p=P)).then_inc(loaded[b], 16)

            def store(g, b):
                for n in range(b * (G0 // 2), (b + 1) * (G0 // 2)):
                    sp.wait_ge(o_used, g * HEADS + 2 * n + 4)
                    sp.dma_start(dram["o0T"][ds(g * (G0 // 2) + n % (G0 // 2), 1), :, b * S:(b + 1) * S].rearrange("a p t -> p (a t)"),
                                 stage[n % 2][:]).then_inc(stored[n % 2], 16)

            for b in range(B):
                load(0, b)
            weights.load(sp)
            with sp.Fori(0, KV0 - 1) as g:
                for b in range(B):
                    store(g, b)
                    sp.wait_ge(pv_done, g * BODY + (b + 1) * G0 * STEPS + RING)
                    load(g + 1, b)
            for b in range(B):
                store(KV0 - 1, b)
            for i in range(2):
                sp.wait_ge(stored[i], 16 * (KV0 * PAIRS // 2 + 1))

        def halves(kt):
            return [(max(lo, kt * P), lo + CH) for lo in range(0, S, CH) if lo + CH > kt * P]

        @block.tensor
        def _(pe):
            def scores(g, n):
                hb, kt = divmod(n, STEPS)
                b, h = divmod(hb, G0)
                if n % (G0 * STEPS) == 0:
                    pe.wait_ge(loaded[b], 64 * (g + 1))
                pe.wait_ge(p_ready, g * BODY + n + 1)
                out = ps_s[n % 2]
                for lo, hi in halves(kt):
                    pe.matmul(out[:, lo:hi], k_high[b][:, kt * P:(kt + 1) * P], q[b][:, h, lo:hi], start=True, stop=False)
                pe.matmul(out[:, kt * P:(kt + 1) * P], ident_bf[:], mask_kq[:], start=False, stop=False)
                for lo, hi in halves(kt):
                    last = pe.matmul(out[:, lo:hi], k_low[b][:, kt * P:(kt + 1) * P], q[b][:, h, lo:hi], start=False, stop=True)
                last.then_inc(s_done, 1)

            def values(g, n):
                hb, kt = divmod(n, STEPS)
                b, h = divmod(hb, G0)
                if kt == 0:
                    pe.wait_ge(o_used, g * HEADS + hb + 1)
                pe.wait_ge(p_ready, g * BODY + n + 3)
                at = HD0 if h % 2 == 0 else 0
                for lo, hi in halves(kt):
                    last = pe.matmul(ps_o[hb % 2][:, lo:hi], v[b][:, kt, at:at + P], probs[n % RING][:, lo:hi],
                                     start=(kt == 0), stop=((kt + 1) * P == hi))
                last.then_inc(pv_done, 1)

            pe.wait_ge(tables, 48)
            pe.wait_ge(ones_set, 2 * B)
            with pe.Fori(0, KV0) as g:
                scores(g, 0)
                for n in range(BODY):
                    if n + 1 < BODY:
                        scores(g, n + 1)
                    values(g, n)

        @block.scalar
        def _(act):
            primed(act, p_ready, 2)
            act.wait_ge(bound_step, 4)
            with act.Fori(0, KV0) as g:
                for n in range(BODY):
                    kt = n % STEPS
                    act.wait_ge(pv_done, g * BODY + n + 1)
                    act.wait_ge(s_done, g * BODY + n + 1)
                    act.activation(probs[n % RING][:, kt * P:], ps_s[n % 2][:, kt * P:], ACT.Exp, bias=shift[:, 0:1],
                                   scale=HD0 ** -0.5).then_inc(p_ready, 1)

        @block.gpsimd
        def _(pool):
            primed(pool, pv_done, RING)
            for b in range(B):
                pool.memset(v[b][:, :, 0:HD0], 1.0).then_inc(ones_set, 1)
                pool.memset(v[b][:, :, 2 * HD0:], 1.0).then_inc(ones_set, 1)

        @block.vector
        def _(dve):
            primed(dve, o_used, 2)
            for i in range(2):
                primed(dve, stored[i], 16)
            dve.wait_ge(tables, 48)
            dve.tensor_scalar(minus[:], temp[:], -1.0, None, ALU.mult).then_inc(bound_step, 1)
            dve.wait_ge(bound_step, 1)
            dve.tensor_tensor(bound[:], temp[:], minus[:], ALU.max).then_inc(bound_step, 1)
            dve.wait_ge(bound_step, 2)
            dve.tensor_scalar(minus[:], bound[:], -HD0 ** -0.5, 60.0, ALU.mult, ALU.add).then_inc(bound_step, 1)
            dve.wait_ge(bound_step, 3)
            dve.tensor_scalar(shift[:], minus[:], 0.0, None, ALU.min).then_inc(bound_step, 1)
            with dve.Fori(0, KV0) as g:
                for hb in range(HEADS):
                    rows, sums = (slice(0, HD0), slice(HD0, P)) if hb % 2 == 0 else (slice(HD0, P), slice(0, HD0))
                    n = hb // 2
                    dve.wait_ge(pv_done, g * BODY + (hb + 1) * STEPS + RING)
                    dve.reciprocal(inverse[hb % 2][rows, :], ps_o[hb % 2][sums, :]).then_inc(inverse_ready, 1)
                    if hb % 2 == 0:
                        dve.wait_ge(stored[n % 2], 16 * (g * PAIRS // 2 + n // 2 + 1))
                    dve.wait_ge(inverse_ready, g * HEADS + hb + 1)
                    dve.tensor_tensor(stage[n % 2][rows, :], ps_o[hb % 2][rows, :], inverse[hb % 2][rows, :], ALU.mult)\
                       .then_inc(o_used, 1)


class MiddleWeights:

    def __init__(self, ctx, nc, dram, sem):
        def raw(name, shape):
            return ctx.enter_context(nc.sbuf_tensor(f"e_w_{name}", shape, F32))

        self.dram = dram
        self.o_rows = raw("o", [P, KD, LAT])
        self.q_rows = raw("q", [P, (D + KV1 * HD1) // P, D])
        self.v_rows = raw("v", [P, 2, D])
        self.r_rows = raw("r", [HL, D])
        self.b_rows = raw("b", [P, OL // P, HL, RL])
        self.loaded = sem("e_w_loaded")
        self.loads = 6 + OL // P

    def load(self, sp):
        dram = self.dram
        sp.dma_start(self.o_rows[:], dram["w_o"].rearrange("(o p) c -> p o c", p=P)).then_inc(self.loaded, 16)
        sp.dma_start(self.q_rows[:, 0:D // P, :], dram["wq"].rearrange("(o p) c -> p o c", p=P)).then_inc(self.loaded, 16)
        sp.dma_start(self.q_rows[:, D // P:, :], dram["wk"].rearrange("(o p) c -> p o c", p=P)).then_inc(self.loaded, 16)
        sp.dma_start(self.v_rows[:, 0, :], dram["wv"]).then_inc(self.loaded, 16)
        sp.dma_start(self.v_rows[:, 1, :], dram["lora_a"].rearrange("h r d -> (h r) d")).then_inc(self.loaded, 16)
        sp.dma_start(self.r_rows[:], dram["lora_r"]).then_inc(self.loaded, 16)
        for o in range(OL // P):
            sp.dma_start(self.b_rows[:, o, :, :], dram["lora_b"][:, o * P:(o + 1) * P, :].rearrange("h p r -> p h r")).then_inc(self.loaded, 16)


def middle_phase(nc, sem, dram, ident, half, weights):
    with ExitStack() as ctx:
        def sb(name, shape, dt=F32):
            return ctx.enter_context(nc.sbuf_tensor(f"e_{name}", shape, dt))

        KV1D = KV1 * HD1
        TOK = KV1D + HL * RL + HL
        LOW, LOG = KV1D, KV1D + HL * RL
        NQK = D // P + KV1D // P
        oT = sb("oT", [P, MQ, D])
        qkT = sb("qkT", [P, NQK, KD, P])
        tokT = sb("tokT", [P, KD, TOK])
        bT = sb("bT", [P, OL])
        br = sb("br", [P, HL])
        cos = sb("cos", [P, B, S])
        sin = sb("sin", [P, B, S])

        x_in = sb("x_in", [P, TT, D])
        g_in = sb("g_in", [P, TT, D])
        o_in = sb("o_in", [P, MQ, CH])
        loaded = sem("e_loaded")

        def tokens(name):
            return dram[name].rearrange("(c t p) d -> c p t d", t=TT, p=P)

        def load(sp, c):
            sp.dma_start(o_in[:], dram["o0T"][:, :, ds(c * CH, CH)].rearrange("m p t -> p m t")).then_inc(loaded, 16)
            sp.dma_start(g_in[:], tokens("g")[ds(c, 1)].rearrange("a p t d -> p (a t) d")).then_inc(loaded, 16)
            sp.dma_start(x_in[:], tokens("x")[ds(c, 1)].rearrange("a p t d -> p (a t) d")).then_inc(loaded, 16)

        turned = sem("e_turned")
        out_act = sem("e_out_act")
        out_dve = sem("e_out_dve")
        tables = sem("e_tables")

        with ExitStack() as prep:
            o_rows, q_rows, v_rows, r_rows, b_rows = weights.o_rows, weights.q_rows, weights.v_rows, weights.r_rows, weights.b_rows
            ps = [prep.enter_context(nc.psum_tensor(f"e_psw{i}", [P, CH], F32)) for i in range(4)]
            groups = []
            for m in range(MQ):
                groups.append(([o_rows[:, o, m * P:(m + 1) * P] for o in range(KD)], P, oT[:, m, :].rearrange("p (o n) -> p o n", n=P)))
            for i in range(NQK):
                groups.append(([q_rows[:, i, k * P:(k + 1) * P] for k in range(KD)], P, qkT[:, i, :, :]))
            for i in range(2):
                groups.append(([v_rows[:, i, k * P:(k + 1) * P] for k in range(KD)], P, tokT[:, :, i * P:(i + 1) * P]))
            groups.append(([r_rows[:, k * P:(k + 1) * P] for k in range(KD)], HL, tokT[:, :, LOG:]))
            groups.append(([b_rows[:, o, :, :].rearrange("p h r -> p (h r)") for o in range(OL // P)], P,
                           bT[:].rearrange("p (o n) -> p o n", n=P)))
            with nc.Block() as block:
                @block.sync
                def _(sp):
                    load(sp, 0)
                    for b in range(B):
                        sp.dma_start(cos[:, b, :], dram["cos1"]).then_inc(tables, 16)
                        sp.dma_start(sin[:, b, :], dram["sin1"]).then_inc(tables, 16)
                    sp.dma_start(br[:], dram["lora_br"].rearrange("(a n) -> a n", a=1).to_broadcast((P, HL))).then_inc(tables, 16)

                @block.tensor
                def _(pe):
                    pe.wait_ge(weights.loaded, 16 * weights.loads)
                    for n, (blocks, cols, _) in enumerate(groups):
                        if n >= 4:
                            pe.wait_ge(out_dve if n % 2 else out_act, (n - 4) // 2 + 1)
                        for j, src in enumerate(blocks):
                            last = pe.transpose(ps[n % 4][:, j * cols:(j + 1) * cols], src, ident[0:cols, 0:cols])
                        last.then_inc(turned, 1)

                @block.scalar
                def _(act):
                    for n, (blocks, cols, to) in enumerate(groups):
                        if n % 2 == 0:
                            act.wait_ge(turned, n + 1)
                            act.activation(to, ps[n % 4][:, 0:len(blocks) * cols].rearrange("p (j n) -> p j n", n=cols),
                                           ACT.Copy).then_inc(out_act, 1)

                @block.vector
                def _(dve):
                    for n, (blocks, cols, to) in enumerate(groups):
                        if n % 2 == 1:
                            dve.wait_ge(turned, n + 1)
                            dve.tensor_copy(to, ps[n % 4][:, 0:len(blocks) * cols].rearrange("p (j n) -> p j n", n=cols))\
                               .then_inc(out_dve, 1)

        x1 = sb("x1", [P, TT, D])
        stats = sb("stats", [P, TT, 6])
        mv = sb("mv", [P, TT, 2])
        var = sb("var", [P, TT])
        rstd = sb("rstd", [P, TT])
        xn = sb("xn", [P, TT, D])
        xnT = sb("xnT", [P, KD, CH])
        raw = sb("raw", [P, NQK, CH])
        swapped = sb("swapped", [P, NQK, CH])
        turn = sb("turn", [P, NQK, CH])
        high = sb("high", [P, NQK, CH], F32R)
        low = sb("low", [P, NQK, CH], F32R)
        tok = sb("tok", [P, TT, TOK])
        logits = sb("logits", [P, TT, HL])
        top = sb("top", [P, TT])
        expo = sb("expo", [P, TT, HL])
        total = sb("total", [P, TT])
        inverse = sb("inverse", [P, TT])
        share = sb("share", [P, TT, HL])
        weighted = sb("weighted", [P, TT, HL * RL])
        weightedT = sb("weightedT", [P, CH])
        gate = sb("gate", [P, TT, OL])

        def bank(name):
            return ctx.enter_context(nc.psum_tensor(f"e_{name}", [P, CH], F32))
        ps_s = [bank(f"ps_s{i}") for i in range(2)]
        ps_t = [bank(f"ps_t{i}") for i in range(2)]
        ps_q = [bank(f"ps_q{i}") for i in range(2)]
        ps_y = [bank(f"ps_y{i}") for i in range(2)]

        s_done = sem("e_s_done")
        s_used = sem("e_s_used")
        x1_ready = sem("e_x1_ready")
        x1_stored = sem("e_x1_stored")
        stats_done = sem("e_stats_done")
        var_ready = sem("e_var_ready")
        rstd_ready = sem("e_rstd_ready")
        xn_ready = sem("e_xn_ready")
        t_done = sem("e_t_done")
        xnT_ready = sem("e_xnT_ready")
        tok_done = sem("e_tok_done")
        tok_ready = sem("e_tok_ready")
        tok_stored = sem("e_tok_stored")
        qk_done = sem("e_qk_done")
        raw_ready = sem("e_raw_ready")
        swap_ready = sem("e_swap_ready")
        rot_step = sem("e_rot_step")
        turn_ready = sem("e_turn_ready")
        high_ready = sem("e_high_ready")
        low_ready = sem("e_low_ready")
        parts_stored = sem("e_parts_stored")
        soft_step = sem("e_soft_step")
        expo_ready = sem("e_expo_ready")
        wT_done = sem("e_wT_done")
        wT_ready = sem("e_wT_ready")
        y_done = sem("e_y_done")
        gate_ready = sem("e_gate_ready")
        gate_stored = sem("e_gate_stored")
        ticks = sem("ticks")
        SOFT = 7

        block = ctx.enter_context(nc.Block())

        @block.sync
        def _(sp):
            def store_x1(c):
                sp.wait_ge(x1_ready, TT * (c + 1))
                sp.dma_start(tokens("x1")[ds(c, 1)].rearrange("a p t d -> p (a t) d"), x1[:]).then_inc(x1_stored, 16)

            def store_rest(c):
                sp.wait_ge(tok_ready, TT * (c + 1))
                sp.dma_start(tokens("v1")[ds(c, 1)].rearrange("a p t d -> p (a t) d"), tok[:, :, 0:KV1D]).then_inc(tok_stored, 16)
                sp.wait_ge(low_ready, NQK * (c + 2))
                for n, part in enumerate((high, low)):
                    sp.dma_start(dram["qk1"][n, :, :, ds(c * CH, CH)].rearrange("n p t -> p n t"), part[:].bitcast(F32)).then_inc(parts_stored, 16)
                sp.wait_ge(gate_ready, TT * (c + 2))
                sp.dma_start(tokens("g1")[ds(c, 1)].rearrange("a p t d -> p (a t) d"), gate[:]).then_inc(gate_stored, 16)

            store_x1(0)
            load(sp, 1)
            with sp.Fori(0, NCH - 2) as c:
                store_x1(c + 1)
                load(sp, c + 2)
                store_rest(c)
            store_x1(NCH - 1)
            store_rest(NCH - 2)
            store_rest(NCH - 1)
            sp.wait_ge(x1_stored, 16 * (NCH + 1))
            sp.wait_ge(tok_stored, 16 * (NCH + 1))
            sp.wait_ge(parts_stored, 32 * (NCH + 1))
            sp.wait_ge(gate_stored, 16 * (NCH + 1))

        @block.tensor
        def _(pe):
            def project(c):
                pe.wait_ge(loaded, 48 * (c + 1))
                for t in range(TT):
                    pe.wait_ge(s_used, TT * c + t + 1)
                    for m in range(MQ):
                        last = pe.matmul(ps_s[t % 2][:], o_in[:, m, t * P:(t + 1) * P], oT[:, m, :], start=(m == 0), stop=(m == MQ - 1))
                    last.then_inc(s_done, 1)

            def rest(c):
                pe.wait_ge(xn_ready, c + 1)
                for k in range(KD):
                    if k == 0:
                        pe.wait_ge(wT_ready, c + 1)
                    pe.wait_ge(xnT_ready, KD * c + max(k - 1, 0) + 2)
                    for t in range(TT):
                        last = pe.transpose(ps_t[k % 2][:, t * P:(t + 1) * P], xn[:, t, k * P:(k + 1) * P], ident[:])
                    last.then_inc(t_done, 1)
                pe.wait_ge(xnT_ready, KD * (c + 1) + 2)
                pe.wait_ge(gate_ready, TT * (c + 1))
                for t in range(TT):
                    if t >= 2:
                        pe.wait_ge(tok_ready, TT * c + t - 1)
                    for k in range(KD):
                        last = pe.matmul(ps_y[t % 2][:, 0:TOK], xnT[:, k, t * P:(t + 1) * P], tokT[:, k, :],
                                         start=(k == 0), stop=(k == KD - 1))
                    last.then_inc(tok_done, 1)
                for i in range(NQK):
                    pe.wait_ge(raw_ready, NQK * c + max(i - 1, 0) + 2)
                    for k in range(KD):
                        last = pe.matmul(ps_q[i % 2][:], qkT[:, i, k, :], xnT[:, k, :], start=(k == 0), stop=(k == KD - 1))
                    last.then_inc(qk_done, 1)
                pe.wait_ge(soft_step, SOFT * (c + 1))
                for t in range(TT):
                    last = pe.transpose(ps_t[0][:, t * P:(t + 1) * P], weighted[:, t, :], ident[:])
                last.then_inc(wT_done, 1)
                pe.wait_ge(wT_ready, c + 2)
                pe.wait_ge(tok_ready, TT * (c + 1))
                for t in range(TT):
                    if t >= 2:
                        pe.wait_ge(gate_ready, TT * (c + 1) + t - 1)
                    pe.matmul(ps_y[t % 2][:], weightedT[:, t * P:(t + 1) * P], bT[:], start=True, stop=True).then_inc(y_done, 1)

            project(0)
            with pe.Fori(0, NCH - 1) as c:
                project(c + 1)
                rest(c)
            rest(NCH - 1)

        @block.scalar
        def _(act):
            primed(act, xnT_ready, 2)
            primed(act, wT_ready, 1)
            primed(act, raw_ready, 2)
            primed(act, gate_ready, TT)

            def rest(c):
                for k in range(KD):
                    act.wait_ge(t_done, KD * c + k + 1)
                    act.activation(xnT[:, k, :], ps_t[k % 2][:], ACT.Copy).then_inc(xnT_ready, 1)
                act.wait_ge(tok_stored, 16 * (c + 1))
                for t in range(TT):
                    act.wait_ge(tok_done, TT * c + t + 1)
                    act.activation(tok[:, t, :], ps_y[t % 2][:, 0:TOK], ACT.Copy).then_inc(tok_ready, 1)

                def highs(i):
                    act.wait_ge(turn_ready, NQK * c + i + 1)
                    act.activation(high[:, i, :], turn[:, i, :], ACT.Copy).then_inc(high_ready, 1)

                for i in range(NQK):
                    act.wait_ge(qk_done, NQK * c + i + 1)
                    act.activation(raw[:, i, :], ps_q[i % 2][:], ACT.Copy).then_inc(raw_ready, 1)
                    if i == 0:
                        act.wait_ge(soft_step, SOFT * c + 3)
                        act.activation(expo[:], logits[:], ACT.Exp).then_inc(expo_ready, 1)
                    if i == 2:
                        act.wait_ge(parts_stored, 32 * (c + 1))
                    if i >= 2:
                        highs(i - 2)
                highs(NQK - 2)
                act.wait_ge(wT_done, c + 1)
                act.activation(weightedT[:], ps_t[0][:], ACT.Copy).then_inc(wT_ready, 1)
                highs(NQK - 1)
                act.wait_ge(gate_stored, 16 * (c + 1))
                for t in range(TT):
                    act.wait_ge(y_done, TT * c + t + 1)
                    act.activation(gate[:, t, :], ps_y[t % 2][:], ACT.Silu).then_inc(gate_ready, 1)

            with act.Fori(0, NCH) as c:
                rest(c)

        @block.gpsimd
        def _(pool):
            primed(pool, x1_stored, 16)
            primed(pool, tok_stored, 16)
            primed(pool, parts_stored, 32)
            primed(pool, gate_stored, 16)
            pool.wait_ge(tables, 16 * (2 * B + 1))

            def power(c):
                pool.wait_ge(var_ready, c + 1)
                pool.tensor_tensor(rstd[:], var[:], half[:, 0:TT], ALU.pow).then_inc(rstd_ready, 1)

            def rotate(c):
                flat = [t[:].rearrange("p b s -> p (b s)") for t in (cos, sin)]
                for i in range(NQK):
                    wait_apart(pool, raw_ready, NQK * c + i + 3, ticks)
                    wait_apart(pool, high_ready, NQK * c + i + 1, ticks)
                    wait_apart(pool, low_ready, NQK * c + i + 1, ticks)
                    pool.tensor_tensor(turn[:, i, :], raw[:, i, :], flat[0][:, ds(c * CH, CH)], ALU.mult)
                    wait_apart(pool, swap_ready, NQK * c + i + 1, ticks)
                    pool.tensor_tensor(swapped[:, i, :], swapped[:, i, :], flat[1][:, ds(c * CH, CH)], ALU.mult)\
                        .then_inc(rot_step, 1)

            power(0)
            with pool.Fori(0, NCH - 1) as c:
                rotate(c)
                power(c + 1)
            rotate(NCH - 1)

        @block.vector
        def _(dve):
            primed(dve, s_used, 2)
            primed(dve, high_ready, NQK)
            primed(dve, low_ready, NQK)
            SWAP = [p ^ (HD1 // 2) for p in range(32)]
            dve.wait_ge(tables, 16 * (2 * B + 1))

            def add(c):
                dve.wait_ge(x1_stored, 16 * (c + 1))
                if not isinstance(c, int):
                    dve.wait_ge(xn_ready, c)
                for t in range(TT):
                    dve.wait_ge(s_done, TT * c + t + 1)
                    dve.tensor_tensor(x1[:, t, :], ps_s[t % 2][:], g_in[:, t, :], ALU.mult).then_inc(s_used, 1)
                    dve.wait_ge(s_used, TT * c + t + 3)
                    dve.tensor_tensor(x1[:, t, :], x1[:, t, :], x_in[:, t, :], ALU.add).then_inc(x1_ready, 1)

            def norm(c):
                for t in range(TT):
                    dve.wait_ge(x1_ready, TT * c + t + 1)
                    dve.bn_stats(stats[:, t, :], x1[:, t, :]).then_inc(stats_done, 1)
                for t in range(TT):
                    wait_apart(dve, stats_done, 2 * c * TT + t + 1, ticks)
                    dve.bn_aggr(mv[:, t, :], stats[:, t, :]).then_inc(stats_done, 1)
                dve.wait_ge(stats_done, 2 * (c + 1) * TT)
                dve.tensor_scalar(var[:], mv[:, :, 1], EPS, None, ALU.add).then_inc(var_ready, 1)
                dve.wait_ge(rstd_ready, c + 1)
                for t in range(TT):
                    last = dve.tensor_scalar(xn[:, t, :], x1[:, t, :], mv[:, t, 0:1], rstd[:, t:t + 1],
                                             ALU.subtract, ALU.mult)
                last.then_inc(xn_ready, 1)

            def route(c):
                dve.wait_ge(tok_ready, TT * (c + 1))
                for t in range(TT):
                    last = dve.tensor_tensor(logits[:, t, :], tok[:, t, LOG:], br[:], ALU.add)
                last.then_inc(soft_step, 1)
                dve.wait_ge(soft_step, SOFT * c + 1)
                dve.tensor_reduce(top[:], logits[:], AX.X, ALU.max).then_inc(soft_step, 1)
                dve.wait_ge(soft_step, SOFT * c + 2)
                dve.tensor_tensor(logits[:], logits[:], top[:].rearrange("p (t o) -> p t o", o=1).to_broadcast((P, TT, HL)),
                                  ALU.subtract).then_inc(soft_step, 1)
                dve.wait_ge(expo_ready, c + 1)
                dve.tensor_reduce(total[:], expo[:], AX.X, ALU.add).then_inc(soft_step, 1)
                dve.wait_ge(soft_step, SOFT * c + 4)
                dve.reciprocal(inverse[:], total[:]).then_inc(soft_step, 1)
                dve.wait_ge(soft_step, SOFT * c + 5)
                dve.tensor_tensor(share[:], expo[:], inverse[:].rearrange("p (t o) -> p t o", o=1).to_broadcast((P, TT, HL)),
                                  ALU.mult).then_inc(soft_step, 1)
                dve.wait_ge(soft_step, SOFT * c + 6)
                for t in range(TT):
                    last = dve.scalar_tensor_tensor(weighted[:, t, :].rearrange("p (h r) -> p h r", r=RL),
                                                    tok[:, t, LOW:LOG].rearrange("p (h r) -> p h r", r=RL), GAIN,
                                                    share[:, t, :].rearrange("p (h o) -> p h o", o=1).to_broadcast((P, HL, RL)),
                                                    ALU.mult, ALU.mult)
                last.then_inc(soft_step, 1)

            def rotate(c):
                def swap(i):
                    wait_apart(dve, raw_ready, NQK * c + i + 3, ticks)
                    dve.stream_shuffle(swapped[:, i, :], raw[:, i, :], SWAP).then_inc(swap_ready, 1)

                def combine(i):
                    dve.wait_ge(rot_step, NQK * c + i + 1)
                    dve.tensor_tensor(turn[:, i, :], turn[:, i, :], swapped[:, i, :], ALU.add).then_inc(turn_ready, 1)

                def split(i):
                    dve.wait_ge(high_ready, NQK * (c + 1) + i + 1)
                    dve.tensor_tensor(low[:, i, :], turn[:, i, :], high[:, i, :].bitcast(F32), ALU.subtract).then_inc(low_ready, 1)

                for i in range(NQK + 2):
                    if i < NQK:
                        swap(i)
                    if 1 <= i <= NQK:
                        combine(i - 1)
                    if i >= 2:
                        split(i - 2)

            add(0)
            norm(0)
            with dve.Fori(0, NCH - 1) as c:
                add(c + 1)
                route(c)
                rotate(c)
                norm(c + 1)
            route(NCH - 1)
            rotate(NCH - 1)


def select_phase(nc, sem, dram, ident, ident_bf, mask_kq, inputs):
    with ExitStack() as ctx:
        def sb(name, shape, dt=F32):
            return ctx.enter_context(nc.sbuf_tensor(f"f_{name}", shape, dt))

        PAIRS = GRP // 2
        LATE = QT - 2
        GROUPS = B * KV1
        PARTS = 3 * HD1
        EXTRA = P // 2
        SENT = 3e38
        qa = [sb(f"qa{u}", [P, GRP, S], F32R) for u in range(B)]
        ka = [sb(f"ka{u}", [P, S], F32R) for u in range(B)]
        qs = [sb(f"qs{u}", [P, GRP, S], F32R) for u in range(B)]
        ks = [sb(f"ks{u}", [P, S], F32R) for u in range(B)]
        v_all = sb("v_all", [P, QT, B, KV1 * HD1])
        v = [sb(f"v{u}", [P, QT, 2 * HD1]) for u in range(B)]
        chunk_max = sb("chunk_max", [P, LATE, 2, NC])
        rest = [sb(f"rest{p}", [P, LATE, 2, NC]) for p in range(PAIRS)]
        top = [sb(f"top{p}", [P, QT, 2, 8]) for p in range(PAIRS)]
        penalty = [sb(f"penalty{p}", [P, QT, 2, EXTRA]) for p in range(PAIRS)]
        part = [sb(f"part{p}", [P, 2, LATE, CPT]) for p in range(PAIRS)]
        missed = [sb(f"missed{p}", [P, 2 * LATE]) for p in range(PAIRS)]
        diag = [[sb(f"diag{u}{p}", [P, 2 * LATE, P], BF16) for p in range(PAIRS)] for u in range(B)]
        probs = [sb(f"probs{i}", [P, GRP, CH]) for i in range(2)]
        o_rows = sb("o_rows", [P, CH])
        inverse = sb("inverse", [P, TT * GRP])
        o_out = [sb(f"o_out{i}", [P, TT, GRP * HD1]) for i in range(2)]
        may_miss = sb("may_miss", [P, 2 * LATE, MISS])
        part_chunk = sb("part_chunk", [P, CPT])
        mask_qk = sb("mask_qk", [P, P], BF16)
        mask_part = sb("mask_part", [P, P], BF16)
        ps_a = [ctx.enter_context(nc.psum_tensor(f"f_ps_a{i}", [P, S], F32)) for i in range(2)]
        ps_s = [ctx.enter_context(nc.psum_tensor(f"f_ps_s{i}", [P, CH], F32)) for i in range(2)]
        ps_o = ctx.enter_context(nc.psum_tensor("f_ps_o", [P, CH], F32))
        ps_t = ctx.enter_context(nc.psum_tensor("f_ps_t", [P, CH], F32))

        tables = sem("f_tables")
        zeroed = sem("f_zeroed")
        cleared = sem("f_cleared")
        a_loaded = [sem(f"f_a_loaded{u}") for u in range(B)]
        s_loaded = [sem(f"f_s_loaded{u}") for u in range(B)]
        a_done = sem("f_a_done")
        a_used = sem("f_a_used")
        top_done = sem("f_top_done")
        rest_done = sem("f_rest_done")
        pen_step = sem("f_pen_step")
        missed_ready = sem("f_missed_ready")
        diag_ready = sem("f_diag_ready")
        v_ready = sem("f_v_ready")
        tp_done = sem("f_tp_done")
        qs_ready = sem("f_qs_ready")
        s_done = sem("f_s_done")
        exp_ready = sem("f_exp_ready")
        pv_done = sem("f_pv_done")
        o_copied = sem("f_o_copied")
        to_done = sem("f_to_done")
        inverse_ready = sem("f_inverse_ready")
        o_ready = sem("f_o_ready")
        o_stored = [sem(f"f_o_stored{i}") for i in range(2)]
        ticks = sem("ticks")

        UNITS = GRP * QT
        PUNITS = 2 * QT
        KTILES = [(0, kt) for kt in range(QT // 2)] + [(1, kt) for kt in range(QT)]
        M = len(KTILES)
        N_S = M * GRP

        def unit(n):
            p, r = divmod(n, PUNITS)
            return p, QT - 1 - r // 2, r % 2

        def columns(m):
            half, kt = KTILES[m]
            return max(half * CH, kt * P), (half + 1) * CH

        steps = []
        for m in range(M):
            steps += [("s", m, 0), ("s", m, 1)]
            if m > 0:
                steps.append(("pv", m - 1))
            steps += [("s", m, 2), ("s", m, 3)]
            if m == QT // 2:
                steps.append(("copy", 0))
            if m == QT // 2 + 1:
                steps.append(("turn", 0))
        steps += [("pv", M - 1), ("copy", 1)]
        LAG, TURN1, PEN0, PEN1 = 6, 8, (27, 28), (2, 3)

        def width(step):
            lo, hi = columns(step[1]) if step[0] in ("s", "pv") else (0, CH)
            return (hi - lo + P) * (2 if step[0] == "pv" else 1)

        order = [(LAG + n) % UNITS for n in range(UNITS)]
        room = [unit(n)[1] + 3 + 2 * (n % 4 < 2) + 5 * (n % PUNITS in (12, 13)) for n in order]
        after = {n: [] for n in range(UNITS)}
        done, total, n = 0, sum(width(x) for x in steps), 0
        for x in steps:
            while done * sum(room) >= total * sum(room[:n + 1]):
                n += 1
            after[order[n]].append(x)
            done += width(x)
        TURN0 = next(n for n in order if ("turn", 0) in after[n])

        def second(n):
            return after[n]

        block = ctx.enter_context(nc.Block())

        @block.sync
        def _(sp):
            sp.dma_start(mask_qk[:], dram["mask_qk"]).then_inc(tables, 16)
            sp.dma_start(mask_part[:], dram["mask_part"]).then_inc(tables, 16)
            sp.dma_start(part_chunk[:], dram["part_chunk"]).then_inc(tables, 16)
            sp.dma_start(may_miss[:], dram["may_miss"].rearrange("p q h k -> p (q h) k")).then_inc(tables, 16)
            for u in range(B):
                sp.dma_start(v_all[:, :, u, :], dram["v1"][u * S:(u + 1) * S, :].rearrange("(n p) c -> p n c", p=P)).then_inc(tables, 16)

            def store(i, j, u, half):
                sp.wait_ge(o_ready, 2 * i + half + 3)
                sp.dma_start(dram["o1"][u * S + half * CH:u * S + (half + 1) * CH, ds(j * GRP * HD1, GRP * HD1)].rearrange("(t p) c -> p t c", p=P),
                             o_out[half][:]).then_inc(o_stored[half], 16)

            sp.wait_ge(a_done, UNITS)
            inputs.load_weights(sp)
            for u in range(2):
                inputs.load(sp, u, u)
            with sp.Fori(0, KV1) as j:
                for u in range(B):
                    for half in range(2):
                        store(2 * j + u, j, u, half)
            for half in range(2):
                sp.wait_ge(o_stored[half], 16 * (GROUPS + 1))

        @block.tensor
        def _(pe):
            primed(pe, s_done, 1)
            primed(pe, to_done, 1)

            def choose(g, j, u, n):
                p, qt, h = unit(n)
                if n == 0:
                    pe.wait_ge(a_loaded[u], 96 * (j + 1))
                pe.wait_ge(a_used, UNITS * g + n + 1)
                out, end = ps_a[n % 2], (qt + 1) * P
                for lo in range(0, end, CH):
                    hi = min(end, lo + CH)
                    pe.matmul(out[:, lo:hi], qa[u][:, 2 * p + h, qt * P:end], ka[u][:, lo:hi], start=True, stop=(hi < end))
                pe.matmul(out[:, qt * P:end], ident_bf[:], mask_qk[:], start=False, stop=True).then_inc(a_done, 1)

            def penalties(g, p, half):
                pe.wait_ge(pen_step, 4 * (2 * g + p + 1))
                pe.wait_ge(qs_ready, 4 * g + 2 * p + half + 1)
                pe.wait_ge(o_ready, 2 * g + 1)
                for t in range(TT):
                    last = pe.transpose(ps_t[:, t * P:(t + 1) * P], penalty[p][:, half * TT + t, :, :].rearrange("p h k -> p (h k)"), ident[:])
                last.then_inc(tp_done, 1)

            def scores(i, j, u, m, h):
                n, (half, kt) = m * GRP + h, KTILES[m]
                lo, hi = columns(m)
                if n == 0:
                    pe.wait_ge(s_loaded[u], 96 * (j + 1) + 16)
                    pe.wait_ge(qs_ready, 4 * i + 5)
                if n == GRP:
                    pe.wait_ge(diag_ready, 2 * (i + 1))
                pe.wait_ge(exp_ready, N_S * i + n + 1)
                out, q0 = ps_s[n % 2], half * CH
                masked, parted = kt * P >= q0, kt >= 1 and q0 <= (kt + 1) * P < hi
                last = pe.matmul(out[:, lo - q0:], ks[u][:, kt * P:(kt + 1) * P], qs[u][:, h, lo:hi],
                                 start=True, stop=not (masked or parted))
                if masked:
                    last = pe.matmul(out[:, lo - q0:lo - q0 + P], ident_bf[:], mask_kq[:], start=False, stop=not parted)
                if parted:
                    at = (kt + 1) * P - q0
                    last = pe.matmul(out[:, at:at + P], mask_part[:], diag[u][h // 2][:, (h % 2) * LATE + kt - 1, :], start=False, stop=True)
                last.then_inc(s_done, 1)

            def values(i, u, m):
                half, kt = KTILES[m]
                lo, hi = columns(m)
                if m == 0:
                    pe.wait_ge(v_ready, i + 1)
                if kt == 0:
                    pe.wait_ge(o_copied, 2 * i + half + 1)
                pe.wait_ge(exp_ready, N_S * i + (m + 1) * GRP + 2)
                for h in range(GRP):
                    last = pe.matmul(ps_o[2 * HD1 * h:2 * HD1 * (h + 1), lo - half * CH:], v[u][:, kt, :],
                                     probs[m % 2][:, h, lo - half * CH:], start=(kt == 0), stop=((kt + 1) * P == hi))
                last.then_inc(pv_done, 1)

            def outputs(i, half, last_group):
                pe.wait_ge(o_copied, 2 * i + half + 2)
                pe.wait_ge(qs_ready, 4 * i + 5 if half == 0 or last_group else 4 * i + 9)
                pe.wait_ge(o_ready, 2 * i + half + 2)
                for t in range(TT):
                    last = pe.transpose(ps_t[:, t * P:(t + 1) * P], o_rows[:, t * P:(t + 1) * P], ident[:])
                last.then_inc(to_done, 1)

            def attend(i, j, u, todo):
                for what, *at in todo:
                    if what == "s":
                        scores(i, j, u, *at)
                    elif what == "pv":
                        values(i, u, *at)
                    elif what == "turn":
                        outputs(i, *at, False)

            def iteration(i, j, u, ja, first=False):
                for n in range(UNITS):
                    choose(i + 1, ja, 1 - u, n)
                    if n in PEN1:
                        penalties(i, 1, PEN1.index(n))
                    if n in PEN0:
                        penalties(i + 1, 0, PEN0.index(n))
                    if n >= LAG:
                        attend(i, j, u, second(n))
                    elif not first:
                        attend(i - 1, None, 1 - u, second(n))
                    if n == TURN1 and not first:
                        outputs(i - 1, 1, False)

            pe.wait_ge(tables, 16 * (4 + B))
            for n in range(UNITS):
                choose(0, 0, 0, n)
                if n in PEN0:
                    penalties(0, 0, PEN0.index(n))
            iteration(0, 0, 0, 0, True)
            with pe.Fori(0, KV1 - 1) as j:
                iteration(2 * j + 1, j, 1, j + 1)
                iteration(2 * j + 2, j + 1, 0, j + 1)
            for half in range(2):
                penalties(GROUPS - 1, 1, half)
            for n in range(LAG):
                attend(GROUPS - 2, None, 0, second(n))
            outputs(GROUPS - 2, 1, False)
            attend(GROUPS - 1, KV1 - 1, 1, steps)
            outputs(GROUPS - 1, 1, True)

        @block.scalar
        def _(act):
            primed(act, qs_ready, 1)
            primed(act, exp_ready, 2)
            primed(act, o_copied, 1)

            def penalties(g, u, p, half):
                act.wait_ge(tp_done, 4 * g + 2 * p + half + 1)
                for h in range(2):
                    last = act.activation(qs[u][EXTRA:, 2 * p + h, half * CH:(half + 1) * CH], ps_t[h * EXTRA:(h + 1) * EXTRA, :], ACT.Copy)
                last.then_inc(qs_ready, 1)

            def exponentials(i, m, h):
                n, (half, kt) = m * GRP + h, KTILES[m]
                at = columns(m)[0] - half * CH
                if h == 0:
                    act.wait_ge(pv_done, M * i + m + 1)
                act.wait_ge(s_done, N_S * i + n + 2)
                act.activation(probs[m % 2][:, h, at:], ps_s[n % 2][:, at:], ACT.Exp, scale=HD1 ** -0.5).then_inc(exp_ready, 1)

            def outputs(i, half):
                act.wait_ge(to_done, 2 * i + half + 1)
                act.wait_ge(pv_done, M * i + (QT // 2 if half == 0 else M) + 2)
                act.activation(o_rows[:], ps_o[:], ACT.Copy).then_inc(o_copied, 1)

            def attend(i, todo):
                for what, *at in todo:
                    if what == "s":
                        exponentials(i, *at)
                    elif what == "copy":
                        outputs(i, *at)

            def iteration(i, u, first=False):
                for n in range(UNITS):
                    if n in PEN1:
                        penalties(i, u, 1, PEN1.index(n))
                    if n in PEN0:
                        penalties(i + 1, 1 - u, 0, PEN0.index(n))
                    if n >= LAG:
                        attend(i, second(n))
                    elif not first:
                        attend(i - 1, second(n))

            for half in range(2):
                penalties(0, 0, 0, half)
            iteration(0, 0, True)
            with act.Fori(0, KV1 - 1) as j:
                iteration(2 * j + 1, 1)
                iteration(2 * j + 2, 0)
            for half in range(2):
                penalties(GROUPS - 1, 1, 1, half)
            for n in range(LAG):
                attend(GROUPS - 2, second(n))
            attend(GROUPS - 1, steps)

        @block.gpsimd
        def _(pool):
            primed(pool, pv_done, 2)
            rows = dram["qk1"].rearrange("a n p t -> a (n p) t")
            k0 = H1 * HD1

            def load(j, u, q, k, loaded):
                for n, (qp, kp) in enumerate(((0, 0), (0, 1), (1, 0))):
                    to = slice(n * HD1, (n + 1) * HD1)
                    pool.dma_start(q[u][to, :, :],
                                   rows[qp, ds(j * GRP * HD1, GRP * HD1), u * S:(u + 1) * S].rearrange("(h c) t -> c h t", c=HD1)).then_inc(loaded[u], 16)
                    pool.dma_start(k[u][to, :], rows[kp, ds(k0 + j * HD1, HD1), u * S:(u + 1) * S]).then_inc(loaded[u], 16)

            def reload_choose(j, u):
                wait_apart(pool, a_done, UNITS * (2 * j + u + 1), ticks)
                load(j + 1, u, qa, ka, a_loaded)

            def reload_attend(j, u):
                wait_apart(pool, s_done, N_S * (2 * j + u + 1) + 1, ticks)
                load(j + 1, u, qs, ks, s_loaded)

            for u in range(B):
                pool.memset(qa[u][:].bitcast(F32), 0.0)
                pool.memset(ka[u][:].bitcast(F32), 0.0).then_inc(cleared, 1)
                pool.wait_ge(cleared, u + 1)
                load(0, u, qa, ka, a_loaded)
                pool.memset(v[u][:, :, HD1:], 1.0)
            pool.wait_ge(zeroed, 2)
            for u in range(B):
                load(0, u, qs, ks, s_loaded)
                pool.dma_start(ks[u][EXTRA:, :], dram["chunk_of"]).then_inc(s_loaded[u], 16)
            pool.wait_ge(tables, 16 * (4 + B))

            def prepare(g, j, u, first):
                if not first:
                    wait_apart(pool, pv_done, M * (g - 1) + 2, ticks)
                pool.tensor_copy(v[u][:, :, 0:HD1], v_all[:, :, u, ds(j * HD1, HD1)]).then_inc(v_ready, 1)
                if not first:
                    wait_apart(pool, s_done, N_S * (g - 1) + 1, ticks)
                for p in range(PAIRS):
                    pool.wait_ge(missed_ready, 2 * g + p + 1)
                    pool.tensor_tensor(diag[u][p][:], ident[:].rearrange("p (o n) -> p o n", o=1).to_broadcast((P, 2 * LATE, P)),
                                       missed[p][:].rearrange("p (n o) -> p n o", o=1).to_broadcast((P, 2 * LATE, P)), ALU.mult)\
                        .then_inc(diag_ready, 1)

            prepare(0, 0, 0, True)
            with pool.Fori(0, KV1 - 1) as j:
                reload_choose(j, 0)
                prepare(2 * j + 1, j, 1, False)
                reload_attend(j, 0)
                reload_choose(j, 1)
                prepare(2 * j + 2, j + 1, 0, False)
                reload_attend(j, 1)
            prepare(GROUPS - 1, KV1 - 1, 1, False)

        @block.vector
        def _(dve):
            primed(dve, a_used, 2)
            primed(dve, o_ready, 2)
            for half in range(2):
                primed(dve, o_stored[half], 16)
            for p in range(PAIRS):
                dve.memset(rest[p][:], 0.0)
                dve.memset(penalty[p][:], 0.0)
            dve.memset(o_rows[:], 0.0)
            dve.memset(qs[0][32:64, :, :].bitcast(F32), 0.0)
            dve.memset(ks[0][32:64, :].bitcast(F32), 0.0).then_inc(zeroed, 1)
            dve.memset(qs[1][32:64, :, :].bitcast(F32), 0.0)
            dve.memset(ks[1][32:64, :].bitcast(F32), 0.0).then_inc(zeroed, 1)
            dve.wait_ge(tables, 16 * (4 + B))
            dve.wait_ge(zeroed, 2)

            def reduce(g, n):
                p, qt, h = unit(n)
                dve.wait_ge(a_done, UNITS * g + n + 1)
                src = ps_a[n % 2][:, 0:(qt + 1) * P]
                if qt < 2:
                    dve.tensor_reduce(top[p][:, qt, h, 0:1], src, AX.X, ALU.max).then_inc(a_used, 1)
                else:
                    dve.tensor_reduce(chunk_max[:, qt - 2, h, 0:(qt + 1) * CPT], src.rearrange("p (c k) -> p c k", k=CHUNK),
                                      AX.X, ALU.max).then_inc(a_used, 1)

            def choose(g, q):
                tiles = [unit(n) for n in range(4 * q, 4 * q + 4)]
                for n in range(4 * q, 4 * q + 4):
                    reduce(g, n)
                if tiles[0][1] < 2:
                    return
                late = 12 * (q // 4) + 4 * (q % 4)
                wait_apart(dve, a_used, UNITS * g + 4 * q + 6, ticks)
                for p, qt, h in tiles:
                    dve.max(top[p][:, qt, h, :], chunk_max[:, qt - 2, h, 0:(qt + 1) * CPT]).then_inc(top_done, 1)
                wait_apart(dve, top_done, 2 * 2 * LATE * g + late + 4, ticks)
                for p, qt, h in tiles:
                    n = (qt + 1) * CPT
                    dve.match_replace(rest[p][:, qt - 2, h, 0:n], top[p][:, qt, h, :], chunk_max[:, qt - 2, h, 0:n], SENT).then_inc(rest_done, 1)

            def penalise(g, p, first):
                if not first:
                    dve.wait_ge(tp_done, 4 * (g - 1) + 2 * p + 2)
                dve.wait_ge(rest_done, 2 * 2 * LATE * g + 2 * LATE * (p + 1))
                dve.scalar_tensor_tensor(penalty[p][:, 2:, :, 0:MISS].rearrange("p q h k -> p (q h) k"),
                                         rest[p][:, :, :, CPT:CPT + MISS].rearrange("p q h k -> p (q h) k"), SENT, may_miss[:],
                                         ALU.not_equal, ALU.mult).then_inc(pen_step, 1)
                for h in range(2):
                    flat = rest[p][:].rearrange("p q h k -> p (q h k)")
                    dve.scalar_tensor_tensor(part[p][:, h, :, :], diagonal(flat, h), SENT,
                                             part_chunk[:].rearrange("p (o k) -> p o k", o=1).to_broadcast((P, LATE, CPT)),
                                             ALU.not_equal, ALU.mult).then_inc(pen_step, 1)
                if not first:
                    dve.wait_ge(diag_ready, 2 * (g - 1) + p + 1)
                dve.wait_ge(pen_step, 4 * (2 * g + p) + 3)
                dve.tensor_reduce(missed[p][:], part[p][:].rearrange("p h q k -> p (h q) k"), AX.X, ALU.add).then_inc(missed_ready, 1)

            def shift(g, p):
                dve.wait_ge(a_used, UNITS * g + PUNITS * (p + 1) + 2)
                dve.tensor_scalar(penalty[p][:, :, :, MISS:MISS + 1].rearrange("p q h o -> p (q h) o"),
                                  top[p][:, :, :, 0:1].rearrange("p q h o -> p (q h) o"), -1.0, None, ALU.mult).then_inc(pen_step, 1)

            def diagonal(flat, h):
                start, pitch = h * NC + CPT, 2 * NC + CPT
                return bass.AP(tensor=flat.tensor, offset=flat.offset + start, ap=[list(flat.ap[0]), [pitch, LATE], [1, CPT]])

            def outputs(i, half):
                src = ps_t[:].rearrange("p (n c) -> p n c", c=2 * HD1)
                dve.wait_ge(to_done, 2 * i + half + 2)
                dve.reciprocal(inverse[:].rearrange("p (n o) -> p n o", o=1), src[:, :, HD1:HD1 + 1]).then_inc(inverse_ready, 1)
                dve.wait_ge(o_stored[half], 16 * (i + 1))
                dve.wait_ge(inverse_ready, 2 * i + half + 1)
                dve.tensor_tensor(o_out[half][:].rearrange("p t (h c) -> p (t h) c", c=HD1), src[:, :, 0:HD1],
                                  inverse[:].rearrange("p (n o) -> p n o", o=1).to_broadcast((P, TT * GRP, HD1)), ALU.mult).then_inc(o_ready, 1)

            def stage(g, first, second):
                for q in range(UNITS // 4):
                    choose(g, q)
                    if q % 4 == 2:
                        penalise(g, q // 4, first)
                    if q % 4 == 3:
                        shift(g, q // 4)
                    if q == TURN1 // 4 and not (first or second):
                        outputs(g - 2, 1)
                    if q == TURN0 // 4 and not first:
                        outputs(g - 1, 0)

            stage(0, True, False)
            stage(1, False, True)
            with dve.Fori(0, KV1 - 1) as j:
                for u in range(2):
                    stage(2 * j + 2 + u, False, False)
            outputs(GROUPS - 2, 1)
            for half in range(2):
                outputs(GROUPS - 1, half)


class FinishInputs:

    def __init__(self, ctx, nc, dram, sem):
        def sb(name, shape):
            return ctx.enter_context(nc.sbuf_tensor(f"h_{name}", shape, F32))

        self.dram = dram
        self.w_rows = sb("w_rows", [P, D // P, H1 * HD1])
        self.g_in = [sb(f"g_in{i}", [P, TT, D]) for i in range(2)]
        self.x_in = [sb(f"x_in{i}", [P, TT, D]) for i in range(2)]
        self.w_loaded = sem("h_w_loaded")
        self.loaded = [sem(f"h_loaded{i}") for i in range(2)]

    def load_weights(self, sp):
        sp.dma_start(self.w_rows[:], self.dram["wo"].rearrange("(o p) c -> p o c", p=P)).then_inc(self.w_loaded, 16)

    def load(self, sp, c, u):
        for to, name in ((self.g_in, "g1"), (self.x_in, "x1")):
            sp.dma_start(to[u][:], self.dram[name].rearrange("(c t p) d -> c p t d", t=TT, p=P)[ds(c, 1)]
                         .rearrange("a p t d -> p (a t) d")).then_inc(self.loaded[u], 16)


def finish_phase(nc, sem, dram, ident, out, inputs):
    with ExitStack() as ctx:
        def sb(name, shape, dt=F32):
            return ctx.enter_context(nc.sbuf_tensor(f"h_{name}", shape, dt))

        KO = H1 * HD1 // P
        w_rows, g_in, x_in, loaded = inputs.w_rows, inputs.g_in, inputs.x_in, inputs.loaded
        wT = sb("wT", [P, KO, D])
        o_in = [sb(f"o_in{i}", [P, TT, KO * P]) for i in range(2)]
        oT = [sb(f"oT{i}", [P, KO, CH]) for i in range(2)]
        y = [sb(f"y{i}", [P, TT, D]) for i in range(2)]
        ps_t = [ctx.enter_context(nc.psum_tensor(f"h_ps_t{i}", [P, CH], F32)) for i in range(4)]
        ps_y = [ctx.enter_context(nc.psum_tensor(f"h_ps_y{i}", [P, CH], F32)) for i in range(2)]

        w_turned = sem("h_w_turned")
        w_ready = sem("h_w_ready")
        t_done = sem("h_t_done")
        t_ready = sem("h_t_ready")
        y_done = sem("h_y_done")
        gated = sem("h_gated")
        y_ready = sem("h_y_ready")
        stored = [sem(f"h_stored{i}") for i in range(2)]
        block = ctx.enter_context(nc.Block())

        def tokens(ap):
            return ap.rearrange("(c t p) d -> c p t d", t=TT, p=P)

        @block.sync
        def _(sp):
            def load(c, u):
                sp.dma_start(o_in[u][:], tokens(dram["o1"])[ds(c, 1)].rearrange("a p t d -> p (a t) d")).then_inc(loaded[u], 16)

            def store(c, u):
                sp.wait_ge(y_ready, TT * (c + 1))
                sp.dma_start(tokens(out)[ds(c, 1)].rearrange("a p t d -> p (a t) d"), y[u][:]).then_inc(stored[u], 16)

            for u in range(2):
                load(u, u)
            with sp.Fori(0, NCH // 2 - 1) as i:
                for u in range(2):
                    store(2 * i + u, u)
                    inputs.load(sp, 2 * i + 2 + u, u)
                    load(2 * i + 2 + u, u)
            for u in range(2):
                store(NCH - 2 + u, u)
            for u in range(2):
                sp.wait_ge(stored[u], 16 * (NCH // 2 + 1))

        @block.tensor
        def _(pe):
            primed(pe, y_done, 2 * TT)
            pe.wait_ge(inputs.w_loaded, 16)
            for k in range(KO):
                for o in range(D // P):
                    last = pe.transpose(ps_t[k % 4][:, o * P:(o + 1) * P], w_rows[:, o, k * P:(k + 1) * P], ident[:])
                last.then_inc(w_turned, 1)

            def turn(i, u):
                pe.wait_ge(loaded[u], 48 * (i + 1))
                for k in range(KO):
                    if k == 0:
                        pe.wait_ge(w_ready, KO)
                    pe.wait_ge(t_ready, KO * (2 * i + u) + k + 1)
                    for t in range(TT):
                        last = pe.transpose(ps_t[k][:, t * P:(t + 1) * P], o_in[u][:, t, k * P:(k + 1) * P], ident[:])
                    last.then_inc(t_done, 1)

            def project(i, u):
                c = 2 * i + u
                pe.wait_ge(t_ready, KO * (c + 2))
                for t in range(TT):
                    pe.wait_ge(gated, TT * c + t + 1)
                    for k in range(KO):
                        last = pe.matmul(ps_y[t % 2][:], oT[u][:, k, t * P:(t + 1) * P], wT[:, k, :], start=(k == 0), stop=(k == KO - 1))
                    last.then_inc(y_done, 1)

            turn(0, 0)
            with pe.Fori(0, NCH // 2 - 1) as i:
                turn(i, 1)
                project(i, 0)
                turn(i + 1, 0)
                project(i, 1)
            turn(NCH // 2 - 1, 1)
            project(NCH // 2 - 1, 0)
            project(NCH // 2 - 1, 1)

        @block.scalar
        def _(act):
            primed(act, t_ready, KO)
            for k in range(KO):
                act.wait_ge(w_turned, k + 1)
                act.activation(wT[:, k, :], ps_t[k % 4][:], ACT.Copy).then_inc(w_ready, 1)
            with act.Fori(0, NCH // 2) as i:
                for u in range(2):
                    c = 2 * i + u
                    act.wait_ge(y_done, TT * (c + 1))
                    for k in range(KO):
                        act.wait_ge(t_done, KO * c + k + 1)
                        act.activation(oT[u][:, k, :], ps_t[k][:], ACT.Copy).then_inc(t_ready, 1)

        @block.gpsimd
        def _(pool):
            primed(pool, gated, 2)

        @block.vector
        def _(dve):
            for u in range(2):
                primed(dve, stored[u], 16)
            with dve.Fori(0, NCH // 2) as i:
                for u in range(2):
                    c = 2 * i + u
                    dve.wait_ge(loaded[u], 48 * (i + 1))
                    dve.wait_ge(stored[u], 16 * (i + 1))
                    for t in range(TT):
                        dve.wait_ge(y_done, TT * (c + 2) + t + 1)
                        dve.tensor_tensor(y[u][:, t, :], ps_y[t % 2][:], g_in[u][:, t, :], ALU.mult).then_inc(gated, 1)
                        dve.wait_ge(gated, TT * c + t + 3)
                        dve.tensor_tensor(y[u][:, t, :], y[u][:, t, :], x_in[u][:, t, :], ALU.add).then_inc(y_ready, 1)


def program(nc, dram, out):
    def scratch(name, shape, dt=F32):
        dram[name] = nc.dram_tensor(name, shape, dt, kind="Internal").ap()

    scratch("xnT", (KD, P, T))
    scratch("g", (T, D))
    scratch("v", (T, KVD))
    scratch("k_mean", (P, T))
    scratch("k_raw", (MK, P, T))
    scratch("k_high", (KV0, P, T), FP16)
    scratch("k_low", (KV0, P, T), FP16)
    scratch("q_parts", (H0, P, T), FP16)
    scratch("o0T", (MQ, P, T))
    scratch("x1", (T, D))
    scratch("v1", (T, KV1 * HD1))
    scratch("qk1", (2, (H1 + KV1) * HD1 // P, P, T))
    scratch("g1", (T, OL))
    scratch("o1", (T, H1 * HD1))
    with ExitStack() as ctx:
        shared = {"ticks": ctx.enter_context(nc.semaphore("ticks"))}

        def sem(name):
            return shared[name] if name in shared else ctx.enter_context(nc.semaphore(name))

        def kept(name, shape, dt=F32):
            return ctx.enter_context(nc.sbuf_tensor(name, shape, dt))

        ident = kept("ident", [P, P])
        half = kept("half", [P, 2 * T // P])
        ident_bf = kept("ident_bf", [P, P], BF16)
        mask_kq = kept("mask_kq", [P, P], BF16)
        with ExitStack() as inner:
            conv_in = inner.enter_context(nc.sbuf_tensor("conv_in", [P, 2, MQ, B, PAD + S], FP16))
            unscale = inner.enter_context(nc.sbuf_tensor("unscale", [P, 1], F32))
            rows0 = inner.enter_context(nc.sbuf_tensor("rows0", [P, LAT, TAPS], F32))
            rows0_loaded = sem("c_rows0_loaded")
            weights = ProjectionWeights(dram, sem, conv_in)
            gate_phase(nc, sem, dram, ident, half, weights)
            project_phase(nc, sem, dram, ident, conv_in, weights, unscale, rows0, rows0_loaded)
            query_phase(nc, sem, dram, ident, half, conv_in, unscale, rows0, rows0_loaded)
        with ExitStack() as inner:
            middle_weights = MiddleWeights(inner, nc, dram, sem)
            attend_phase(nc, sem, dram, ident_bf, mask_kq, middle_weights)
            middle_phase(nc, sem, dram, ident, half, middle_weights)
        finish_inputs = FinishInputs(ctx, nc, dram, sem)
        select_phase(nc, sem, dram, ident, ident_bf, mask_kq, finish_inputs)
        finish_phase(nc, sem, dram, ident, out, finish_inputs)


NAMES = {"x": "L0_attn_x", "w_qkv": "L0_attn_w_qkv", "w_o": "L0_attn_w_o", "qc1_w": "L0_attn_qc1_w",
         "qc1_b": "L0_attn_qc1_b", "qc2_w": "L0_attn_qc2_w", "qc2_b": "L0_attn_qc2_b", "kc1_w": "L0_attn_kc1_w",
         "kc1_b": "L0_attn_kc1_b", "kc2_w": "L0_attn_kc2_w", "kc2_b": "L0_attn_kc2_b", "key_temp": "L0_attn_key_temp",
         "gate_w": "L0_ffn_gate_w", "up_w": "L0_ffn_up_w", "down_w": "L0_ffn_down_w", "fc1_w": "L0_ffn_fc1_w",
         "fc2_w": "L0_ffn_fc2_w", "expert_w": "L0_ffn_expert_w", "ln_gamma": "L0_ffn_ln_gamma",
         "ln_beta": "L0_ffn_ln_beta", "wq": "L1_attn_wq", "wk": "L1_attn_wk", "wv": "L1_attn_wv", "wo": "L1_attn_wo",
         "lora_a": "L1_ffn_A", "lora_b": "L1_ffn_B", "lora_r": "L1_ffn_Wr", "lora_br": "L1_ffn_br"}


def constants():
    import numpy as np

    bf = mybir.dt.np(BF16)
    part, row = np.arange(P)[:, None], np.arange(P)[None, :]
    c = {"ident": np.eye(P, dtype=np.float32)}

    def angles(dim):
        inv = (1.0 / np.float32(10000.0) ** (np.arange(0, dim, 2, dtype=np.float32) / np.float32(dim))).astype(np.float32)
        return (np.arange(S, dtype=np.float32)[:, None] * inv[None, :]).astype(np.float32)

    a = angles(HD0)[:, (np.arange(P) % HD0) // 2].T
    c["cos0"] = np.cos(a).astype(np.float32)
    c["sin0"] = (np.sin(a) * np.where(np.arange(P) % 2 == 0, -1, 1)[:, None]).astype(np.float32)
    a = angles(HD1)[:, np.arange(P) % (HD1 // 2)].T
    c["cos1"] = np.cos(a).astype(np.float32)
    c["sin1"] = (np.sin(a) * np.where(np.arange(P) % HD1 < HD1 // 2, -1, 1)[:, None]).astype(np.float32)
    c["head2"] = (part // HD0 == np.arange(2)[None, :]).astype(np.float32)
    c["ident_bf"] = np.eye(P).astype(bf)
    c["mask_kq"] = np.where(part <= row, 0, -BIG).astype(bf)
    c["mask_qk"] = np.where(row <= part, 0, -BIG).astype(bf)
    c["mask_part"] = np.where((part // CHUNK == row // CHUNK) & (row <= part), -BIG, 0).astype(bf)
    chunk = np.arange(CPT, CPT + MISS)[:, None] == np.arange(S)[None, :] // CHUNK
    c["chunk_of"] = np.concatenate([chunk, np.ones((1, S)), np.zeros((P // 2 - MISS - 1, S))]).astype(np.float32)
    q = np.arange(P)[:, None, None, None] + P * np.arange(2, QT)[None, :, None, None]
    k = np.arange(CPT, CPT + MISS)[None, None, None, :]
    c["may_miss"] = np.where((k < (q - P) // CHUNK) & np.ones((1, 1, 2, 1), bool), -BIG, 0).astype(np.float32)
    c["part_chunk"] = (part // CHUNK == np.arange(CPT)[None, :]).astype(np.float32)
    return c


def kernel(**inputs):
    import concourse.bacc as bacc
    import numpy as np
    from concourse.bass_utils import run_bass_kernel_spmd as run

    nc = bacc.Bacc("TRN2", target_bir_lowering=False, num_devices=1)
    arrays = {short: np.ascontiguousarray(inputs[name]) for short, name in NAMES.items()}
    arrays["x"] = arrays["x"].reshape(T, D)
    arrays.update(constants())
    dram = {n: nc.dram_tensor(f"in_{n}", a.shape, mybir.dt.from_np(a.dtype), kind="ExternalInput").ap()
            for n, a in arrays.items()}
    out = nc.dram_tensor("out", (T, D), F32, kind="ExternalOutput").ap()
    program(nc, dram, out)
    results = run(nc, [{f"in_{n}": a for n, a in arrays.items()}], core_ids=[0]).results[0]
    return results["out"].reshape(inputs["L0_attn_x"].shape)
```
